# Optimizing a Trainium2 kernel written in Bass

```python
import numpy as np
import jax
import jax.numpy as jnp

def _softmax(x, axis=-1):
    return jax.nn.softmax(x, axis=axis)

def _gelu(x):
    return jax.nn.gelu(x, approximate=True)

def _silu(x):
    return jax.nn.silu(x)

def _sigmoid(x):
    return jax.nn.sigmoid(x)

def _layernorm(x, axis=-1, eps=1e-05):
    m = jnp.mean(x, axis=axis, keepdims=True)
    v = jnp.var(x, axis=axis, keepdims=True)
    return (x - m) / jnp.sqrt(v + eps)

def _scatter_add(tgt, idx, src, axis=0):
    return tgt.at[idx].add(src)

def _segment_sum(src, seg, n):
    return jax.ops.segment_sum(src, seg, n)
kernel_name = 'mk_seq_postln_d1_jaxref_r4_f3a9bd'

def setup_inputs(seed: int=0):
    np.random.seed(seed)
    _w = jnp.asarray

    def _L0_attn_setup():
        import jax, jax.numpy as jnp
        import numpy as np
        B, L, D = (2, 512, 256)
        H = 16
        DH = D // H

        def rope_tables(seq_len, dim):
            inv_freq = 1.0 / 10000.0 ** (jnp.arange(0, dim, 2, dtype=jnp.float32) / dim)
            t = jnp.arange(seq_len, dtype=jnp.float32)
            freqs = jnp.outer(t, inv_freq)
            emb = jnp.concatenate([freqs, freqs], -1)
            return (jnp.cos(emb), jnp.sin(emb))

        def rotate_half(x):
            x1, x2 = (x[..., :x.shape[-1] // 2], x[..., x.shape[-1] // 2:])
            return jnp.concatenate([-x2, x1], axis=-1)
        key = jax.random.key(seed)
        k1, k2, k3 = jax.random.split(key, 3)
        x = jax.random.normal(k1, (B, L, D), dtype=jnp.float32)
        Wqkv = jax.random.normal(k2, (D, 3 * D), dtype=jnp.float32) / np.sqrt(D)
        Wo = jax.random.normal(k3, (D, D), dtype=jnp.float32) / np.sqrt(D)
        return {'x': x, 'Wqkv': Wqkv, 'Wo': Wo}
    _L0_attn_in = _L0_attn_setup()

    def _L0_ffn_setup():
        import jax, jax.numpy as jnp
        import numpy as np
        D, H, O, E, TOPK = (256, 1024, 256, 8, 2)
        B, S = (4, 256)
        key = jax.random.key(seed)
        ks = jax.random.split(key, 12)
        std = 0.02
        return {'hidden_states': jax.random.normal(ks[0], (B, S, D), dtype=jnp.float32), 'norm_weight': jnp.ones((D,), dtype=jnp.float32), 'router_w': jax.random.normal(ks[1], (E, D), dtype=jnp.float32) * std, 'sw1': jax.random.normal(ks[2], (D, H), dtype=jnp.float32) * (1.0 / np.sqrt(D)), 'sb1': jnp.zeros((H,), dtype=jnp.float32), 'sw2': jax.random.normal(ks[3], (H, O), dtype=jnp.float32) * (1.0 / np.sqrt(H)), 'sb2': jnp.zeros((O,), dtype=jnp.float32), 'ew1': jax.random.normal(ks[4], (E, D, H), dtype=jnp.float32) * (1.0 / np.sqrt(D)), 'eb1': jnp.zeros((E, H), dtype=jnp.float32), 'ew2': jax.random.normal(ks[5], (E, H, O), dtype=jnp.float32) * (1.0 / np.sqrt(H)), 'eb2': jnp.zeros((E, O), dtype=jnp.float32)}
    _L0_ffn_in = _L0_ffn_setup()
    _d = {'L0_attn_x': _L0_attn_in['x'], 'L0_attn_Wqkv': _L0_attn_in['Wqkv'], 'L0_attn_Wo': _L0_attn_in['Wo'], 'L0_ffn_norm_weight': _L0_ffn_in['norm_weight'], 'L0_ffn_router_w': _L0_ffn_in['router_w'], 'L0_ffn_sw1': _L0_ffn_in['sw1'], 'L0_ffn_sb1': _L0_ffn_in['sb1'], 'L0_ffn_sw2': _L0_ffn_in['sw2'], 'L0_ffn_sb2': _L0_ffn_in['sb2'], 'L0_ffn_ew1': _L0_ffn_in['ew1'], 'L0_ffn_eb1': _L0_ffn_in['eb1'], 'L0_ffn_ew2': _L0_ffn_in['ew2'], 'L0_ffn_eb2': _L0_ffn_in['eb2']}
    _x0 = _d['L0_attn_x']
    _d['L0_attn_x'] = jax.random.normal(jax.random.fold_in(jax.random.key(seed), 1), (8, 512, 256), dtype=_x0.dtype)
    del _x0
    return _d

def reference(L0_attn_x, L0_attn_Wqkv, L0_attn_Wo, L0_ffn_norm_weight, L0_ffn_router_w, L0_ffn_sw1, L0_ffn_sb1, L0_ffn_sw2, L0_ffn_sb2, L0_ffn_ew1, L0_ffn_eb1, L0_ffn_ew2, L0_ffn_eb2):

    def _L0_attn_ref(x, Wqkv, Wo):
        import jax, jax.numpy as jnp
        import numpy as np
        B, L, D = (2, 512, 256)
        H = 16
        DH = D // H

        def rope_tables(seq_len, dim):
            inv_freq = 1.0 / 10000.0 ** (jnp.arange(0, dim, 2, dtype=jnp.float32) / dim)
            t = jnp.arange(seq_len, dtype=jnp.float32)
            freqs = jnp.outer(t, inv_freq)
            emb = jnp.concatenate([freqs, freqs], -1)
            return (jnp.cos(emb), jnp.sin(emb))

        def rotate_half(x):
            x1, x2 = (x[..., :x.shape[-1] // 2], x[..., x.shape[-1] // 2:])
            return jnp.concatenate([-x2, x1], axis=-1)
        b, l, d = x.shape
        qkv = (x @ Wqkv).reshape(b, l, 3, H, DH)
        q, k, v = (qkv[:, :, 0], qkv[:, :, 1], qkv[:, :, 2])
        cos, sin = rope_tables(l, DH)
        cos = cos[:, None, :]
        sin = sin[:, None, :]
        q = q * cos + rotate_half(q) * sin
        k = k * cos + rotate_half(k) * sin
        scale = DH ** (-0.5)
        scores = jnp.einsum('bqhd,bkhd->bhqk', q, k) * scale
        attn = jax.nn.softmax(scores, axis=-1)
        out = jnp.einsum('bhqk,bkhd->bqhd', attn, v)
        out = out.reshape(b, l, d)
        return out @ Wo

    def _L0_ffn_ref(hidden_states, norm_weight, router_w, sw1, sb1, sw2, sb2, ew1, eb1, ew2, eb2):
        import jax, jax.numpy as jnp
        import numpy as np
        D, H, O, E, TOPK = (256, 1024, 256, 8, 2)
        B, S = (4, 256)
        b, s, d = hidden_states.shape
        var = jnp.mean(jnp.square(hidden_states), axis=-1, keepdims=True)
        normed = hidden_states * jax.lax.rsqrt(var + 1e-08) * norm_weight
        shared = jnp.maximum(normed @ sw1 + sb1, 0.0) @ sw2 + sb2
        flat = normed.reshape(-1, d)
        T = flat.shape[0]
        probs = jax.nn.sigmoid(flat @ router_w.T)
        scores, idx = jax.lax.top_k(probs, TOPK)
        w = scores / (jnp.sum(scores, axis=-1, keepdims=True) + 1e-06)
        comb = jnp.zeros((T, E), dtype=flat.dtype)
        comb = comb.at[jnp.arange(T)[:, None], idx].add(w)
        h = jnp.maximum(jnp.einsum('td,edh->teh', flat, ew1) + eb1[None, :, :], 0.0)
        eo = jnp.einsum('teh,eho->teo', h, ew2) + eb2[None, :, :]
        routed = jnp.einsum('teo,te->to', eo, comb)
        return shared + routed.reshape(b, s, -1)
    x = L0_attn_x
    x = _layernorm(x + _L0_attn_ref(x, L0_attn_Wqkv, L0_attn_Wo), axis=-1)
    x = _layernorm(x + _L0_ffn_ref(x, L0_ffn_norm_weight, L0_ffn_router_w, L0_ffn_sw1, L0_ffn_sb1, L0_ffn_sw2, L0_ffn_sb2, L0_ffn_ew1, L0_ffn_eb1, L0_ffn_ew2, L0_ffn_eb2), axis=-1)
    return x

_drawn_inputs = setup_inputs


def setup_inputs(seed=0):
    import zlib

    import numpy as np

    out = dict(_drawn_inputs(seed))
    spreads = {'L0_ffn_norm_weight': (1.0, 0.2),
     'L0_ffn_sb1': (0.0, 0.1),
     'L0_ffn_sb2': (0.0, 0.1),
     'L0_ffn_eb1': (0.0, 0.1),
     'L0_ffn_eb2': (0.0, 0.1)}
    factors = {}
    for name, (base, spread) in spreads.items():
        noise = np.random.default_rng([zlib.crc32(name.encode()), seed]).standard_normal(out[name].shape)
        drawn = base * np.exp(spread * noise) if base else spread * noise
        out[name] = jnp.asarray(drawn.astype(out[name].dtype))
    for name, factor in factors.items():
        out[name] = (out[name] * factor).astype(out[name].dtype)
    return out
```

```python
from contextlib import ExitStack

import concourse.bass as bass
from concourse import mybir
import numpy as np

F32 = mybir.dt.float32
BF16 = mybir.dt.bfloat16
U32 = mybir.dt.uint32
I32 = mybir.dt.int32
ALU = mybir.AluOpType
ACT = mybir.ActivationFunctionType
AX_X = mybir.AxisListType.X
P = 128


class Steps:

    def __init__(self, nc, ctx, tag):
        self.nc, self.ctx, self.tag = nc, ctx, tag

    def sb(self, name, shape, dt):
        return self.ctx.enter_context(self.nc.sbuf_tensor(f"{self.tag}_{name}", shape, dt))

    def ps(self, name, shape, dt):
        return self.ctx.enter_context(self.nc.psum_tensor(f"{self.tag}_{name}", shape, dt))

    def sem(self, name):
        return self.ctx.enter_context(self.nc.semaphore(f"{self.tag}_{name}"))


def attention(nc, xT, Wqkv, rope_cos, rope_sin, attn_out, slots_x):
    D, T = xT.shape
    DH, L = rope_cos.shape[2], P * rope_cos.shape[1]
    H = D // DH
    B = T // L
    NT = L // P
    DC = D // P
    G = 4
    HG = H // G
    U = G * NT
    NG = B * HG
    TERMS = 6
    KR = TERMS * DH
    SCALE = float(DH) ** -0.5
    A_LEAD = U + 4
    BODY = 2 * HG
    FIRST = 1
    PASSES = (NG - FIRST - 1) // BODY
    HEAD, TAIL = FIRST, FIRST + PASSES * BODY
    QK_LEAD, V_LEAD = 6, 4
    T_LEAD = A_LEAD + 6
    RING = 4
    PR = 8
    assert NT == HG and NG % BODY == 0 and U == 16

    Q_PIECES, K_PIECES = (1, 1, 1, 2, 2, 3), (1, 2, 3, 1, 2, 1)
    assert len(Q_PIECES) == len(K_PIECES) == TERMS

    with ExitStack() as ctx:
        a = Steps(nc, ctx, "att")
        w = a.sb("w", [P, DC, 3 * D], F32)
        cos = a.sb("cos", [P, NT, DH], F32)
        sin = a.sb("sin", [P, NT, DH], F32)
        xt = a.sb("xt", [P, 2, DC, L], F32)
        zero = a.sb("zero", [P, 2048], F32)
        ident = a.sb("ident", [P, P], BF16)
        identf = a.sb("identf", [P, P], F32)
        stack = a.sb("stack", [P, 2, NT, 2, H, KR], BF16)
        qk = a.sb("qk", [P, RING, G, 2, L], BF16)
        V = a.sb("V", [P, 2, NT, H, 32], F32)
        prob = a.sb("prob", [P, PR, L], F32)
        mx = a.sb("mx", [P, 2, U], F32)
        mrest = a.sb("mrest", [P, U], F32)
        mstk = a.sb("mstk", [P, U, 32], BF16)
        rc = a.sb("rc", [P, 2 * D], F32)
        rs = a.sb("rs", [P, 2 * D], F32)
        rr = a.sb("rr", [P, 2 * D], F32)
        r1 = a.sb("r1", [P, 2 * D], F32)
        oT = a.sb("oT", [P, L], F32)
        rden = a.sb("rden", [P, U], F32)
        ob = a.sb("ob", [P, 2, NT, D], F32)

        psA = [a.ps(f"psA{i}", [P, L], F32) for i in range(2)]
        psB = [a.ps(f"psB{i}", [P, L], F32) for i in range(2)]
        psV = a.ps("psV", [P, L], F32)
        psT = a.ps("psT", [P, 2, L], BF16)
        psX = a.ps("psX", [P, 512], F32)
        psM = a.ps("psM", [P, 512], F32)
        psMt = psM[:, :].bitcast(BF16)

        s_w = a.sem("w_loaded")
        s_x = [a.sem(f"x_loaded{i}") for i in range(2)]
        s_const = a.sem("constants")
        s_init = a.sem("init")
        s_zero = a.sem("slots_zeroed")
        s_amm = a.sem("score_rows")
        s_max = a.sem("row_max")
        s_bmm = a.sem("score_cols")
        s_exp = a.sem("probs")
        s_pv = a.sem("pv")
        s_oev = a.sem("o_copied")
        s_otr = a.sem("o_turned")
        s_onrm = a.sem("o_normed")
        s_ost = [a.sem(f"o_stored{i}") for i in range(2)]
        s_tmm = a.sem("head_turned")
        s_tev = a.sem("head_ready")
        s_msp = a.sem("max_split")
        s_mtr = a.sem("max_turned")
        s_mev = a.sem("max_ready")
        s_qmm = a.sem("qk_projected")
        s_qrd = a.sem("qk_read")
        s_qsp = a.sem("qk_split")
        s_stk = a.sem("stacked")
        s_vmm = a.sem("v_projected")
        s_vev = a.sem("v_ready")
        s_dve = a.sem("vector_chain")

        def at(it, v, per_group):
            return v if it is None else v + it * (per_group * BODY)

        def wait(eng, it, s, v, per_group):
            if it is None and v <= 0:
                return
            assert v >= 0
            eng.wait_ge(s, at(it, v, per_group))

        def groups(eng, period, after_loop=None):
            for p in range(-QK_LEAD, HEAD):
                period(p, None)
            with eng.Fori(0, PASSES) as it:
                for p in range(HEAD, HEAD + BODY):
                    period(p, it)
            if after_loop is not None:
                after_loop()
            for p in range(TAIL, NG + 1):
                period(p, None)

        def valid(i, n):
            return 0 <= i < n

        block = ctx.enter_context(nc.Block())

        @block.sync
        def _(sp):
            x_seq = xT.rearrange("(c p) (b l) -> b p c l", p=P, l=L)
            out_seq = attn_out.rearrange("(b t p) d -> b p t d", t=NT, p=P)
            sp.dma_start(w[:, :, :], Wqkv.rearrange("(c p) n -> p c n", p=P)).then_inc(s_w, 16)
            sp.dma_start(xt[:, 0, :, :], x_seq[0]).then_inc(s_x[0], 16)
            sp.dma_start(cos[:, :, :], rope_cos).then_inc(s_w, 16)
            sp.dma_start(sin[:, :, :], rope_sin).then_inc(s_w, 16)
            sp.dma_start(xt[:, 1, :, :], x_seq[1]).then_inc(s_x[1], 16)
            with sp.Fori(0, B // 2 - 1) as i:
                for k in range(2):
                    sp.wait_ge(s_vmm, NT * (k + 1) + i * (2 * NT))
                    sp.dma_start(xt[:, k, :, :], x_seq[bass.ds(2 + k + i * 2, 1)].rearrange("o p c l -> p (o c) l")).then_inc(s_x[k], 16)
                    sp.wait_ge(s_onrm, HG * (k + 1) + i * (2 * HG))
                    sp.dma_start(out_seq[bass.ds(k + i * 2, 1)].rearrange("o p t d -> p (o t) d"), ob[:, k, :, :]).then_inc(s_ost[k], 16)
            for k in range(2):
                sp.wait_ge(s_onrm, HG * (B - 1 + k))
                sp.dma_start(out_seq[B - 2 + k], ob[:, k, :, :]).then_inc(s_ost[k], 16)
            for k in range(2):
                sp.wait_ge(s_ost[k], 16 * (B // 2))

        @block.gpsimd
        def _(pool):
            for k, step in enumerate((
                lambda: pool.memset(ident[:, :], 0.0),
                lambda: pool.affine_select(out=ident[:, :], in_=ident[:, :], compare_op=ALU.not_equal, fill=1.0,
                                           base=0, pattern=[[-1, P]], channel_multiplier=1),
                lambda: pool.memset(identf[:, :], 0.0),
                lambda: pool.affine_select(out=identf[:, :], in_=identf[:, :], compare_op=ALU.not_equal, fill=1.0,
                                           base=0, pattern=[[-1, P]], channel_multiplier=1),
                lambda: pool.memset(zero[:, :], 0.0),
            )):
                step().then_inc(s_init, 1)
                pool.wait_ge(s_init, k + 1)
            rows = slots_x.shape[0] // P
            slots = slots_x.rearrange("(p r) d -> p (r d)", p=P)
            n = 0
            for c in range(0, rows * D, 2048):
                pool.dma_start(slots[:, c:c + 2048], zero[:, :]).then_inc(s_zero, 16)
                n += 16
            pool.wait_ge(s_zero, n)

        @block.tensor
        def _(pe):
            pe.wait_ge(s_init, 4)
            pe.wait_ge(s_const, 1)
            pe.wait_ge(s_w, 48)

            def score_rows(n, it):
                g, h, qt = n // U, n // NT, n % NT
                if qt == 0:
                    wait(pe, it, s_tev, h + 1, G)
                wait(pe, it, s_max, n - 1, U)
                r = qk[0:KR, g % RING, h % G]
                pe.matmul(psA[n % 2][:, :], r[:, 0, qt * P:(qt + 1) * P], r[:, 1, :], start=True, stop=True).then_inc(s_amm, 1)

            def score_cols(n, it):
                g, u = n // U, n % U
                kt, j = u // G, u % G
                if u % 2 == 0 and u < G:
                    wait(pe, it, s_mev, 2 * g + 1 + u // 2, 2)
                wait(pe, it, s_exp, n - 1, U)
                r = qk[:, g % RING, j]
                pe.matmul(psB[n % 2][:, :], r[:, 1, kt * P:(kt + 1) * P], r[:, 0, :], start=True, stop=True).then_inc(s_bmm, 1)

            def turn_head(h, half, it):
                g, b = h // G, h // H
                if half == 0:
                    wait(pe, it, s_tev, h, G)
                    if h % H == 0:
                        wait(pe, it, s_stk, NT * (b + 1), 1)
                for t in range(NT):
                    m = pe.transpose(psT[0:KR, half, t * P:(t + 1) * P], stack[:, b % 2, t, half, h % H, :], ident[:, :])
                if half == 1:
                    m.then_inc(s_tmm, 1)

            def turn_max(g, half, it):
                if half == 0:
                    wait(pe, it, s_msp, g + 1, 1)
                    wait(pe, it, s_onrm, g - 1, 1)
                else:
                    wait(pe, it, s_mev, 2 * g + 1, 2)
                for k in range(U // 2):
                    m = pe.transpose(psMt[96:128, k * P:(k + 1) * P], mstk[:, half * (U // 2) + k, :], ident[:, :])
                m.then_inc(s_mtr, 1)

            def add_pv(g, kt, it):
                b, hg = g // HG, g % HG
                if kt == 0:
                    wait(pe, it, s_oev, g, 1)
                    if hg == 0:
                        wait(pe, it, s_vev, NT * (b + 1), 1)
                n = g * U + kt * G
                wait(pe, it, s_exp, n + G, U)
                for j in range(G):
                    m = pe.matmul(psV[32 * j:32 * j + 32, :], V[:, b % 2, kt, hg * G + j, :], prob[:, (n + j) % PR, :],
                                  start=(kt == 0), stop=(kt == NT - 1))
                m.then_inc(s_pv, 1)

            def turn_out(g, it):
                wait(pe, it, s_oev, g + 1, 1)
                if g + 1 < NG:
                    wait(pe, it, s_mev, 2 * (g + 2), 2)
                else:
                    wait(pe, it, s_onrm, g, 1)
                for qt in range(NT):
                    m = pe.transpose(psM[:, qt * P:(qt + 1) * P], oT[:, qt * P:(qt + 1) * P], identf[:, :])
                m.then_inc(s_otr, 1)

            def project(tile, c, it, value):
                b, t = tile // NT, tile % NT
                if c == 0:
                    wait(pe, it, s_qrd, tile if not value else min(NT * B, tile + QK_LEAD - V_LEAD + 1), 1)
                    wait(pe, it, s_vev, tile if value else tile - (QK_LEAD - V_LEAD), 1)
                    if t == 0 and not value:
                        pe.wait_ge(s_x[b % 2], 16 * (b // 2 + 1) if it is None else 16 * (b // 2 + 1) + it * 16)
                o, cols = (psX[:, 0:D], w[:, c, 2 * D:3 * D]) if value else (psX[:, :], w[:, c, 0:2 * D])
                m = pe.matmul(o, xt[:, b % 2, c, t * P:(t + 1) * P], cols, start=(c == 0), stop=(c == DC - 1))
                if c == DC - 1:
                    m.then_inc(s_vmm if value else s_qmm, 1)

            def period(p, it):
                for u in range(U):
                    n = p * U + u
                    if valid(n + A_LEAD, NG * U):
                        score_rows(n + A_LEAD, it)
                    if valid(n, NG * U):
                        score_cols(n, it)
                    k = n + T_LEAD
                    if valid(k // 4, NG * G) and k % 4 < 2:
                        turn_head(k // 4, k % 4, it)
                    if u % 4 == 2 and valid(n - 6, NG * U):
                        add_pv((n - 6) // U, ((n - 6) % U) // G, it)
                    if u >= U - 2 and valid(p + 1, NG):
                        turn_max(p + 1, u - (U - 2), it)
                    if u == 5 and valid(p - 1, NG):
                        turn_out(p - 1, it)
                    if u in (1, 3) and valid(p + QK_LEAD, NT * B):
                        project(p + QK_LEAD, u // 2, it, False)
                    if u in (9, 10) and valid(p + V_LEAD, NT * B):
                        project(p + V_LEAD, u - 9, it, True)

            groups(pe, period)

        @block.scalar
        def _(act):
            def exps(n, it):
                wait(act, it, s_bmm, n + 1, U)
                if n % G == 0:
                    wait(act, it, s_pv, n // G + 1 - PR // G, NT)
                act.activation(prob[:, n % PR, :], psB[n % 2][:, :], ACT.Exp, scale=SCALE).then_inc(s_exp, 1)

            def copy_head(h, it):
                g = h // G
                wait(act, it, s_tmm, h + 1, G)
                act.activation(qk[0:KR, g % RING, h % G, :, :], psT[0:KR, :, :], ACT.Copy).then_inc(s_tev, 1)

            def copy_out(g, it):
                wait(act, it, s_pv, NT * (g + 1), NT)
                wait(act, it, s_otr, g, 1)
                act.activation(oT[:, :], psV[:, :], ACT.Copy).then_inc(s_oev, 1)

            def copy_v(tile, it):
                b, t = tile // NT, tile % NT
                wait(act, it, s_vmm, tile + 1, 1)
                if t == 0:
                    wait(act, it, s_pv, NT * HG * (b - 1), NT)
                act.activation(V[:, b % 2, t, :, 0:DH], psX[:, 0:D].rearrange("p (h d) -> p h d", d=DH), ACT.Copy).then_inc(s_vev, 1)

            def spread(tile, it):
                b, t = tile // NT, tile % NT
                q, k = (stack[:, b % 2, t, i].rearrange("p h (m d) -> p h m d", d=DH) for i in range(2))
                wait(act, it, s_qsp, tile + 1, 1)
                act.activation(q[:, :, 1:3, :], q[:, :, 0:1, :].to_broadcast([P, H, 2, DH]), ACT.Copy)
                act.activation(k[:, :, 3:6:2, :], k[:, :, 0:1, :].to_broadcast([P, H, 2, DH]), ACT.Copy)
                act.activation(q[:, :, 3, :], q[:, :, 4, :], ACT.Copy)
                act.activation(k[:, :, 1, :], k[:, :, 4, :], ACT.Copy).then_inc(s_stk, 1)

            def period(p, it):
                for u in range(U):
                    n = p * U + u
                    if valid(n, NG * U):
                        exps(n, it)
                    k = n + T_LEAD
                    if valid(k // 4, NG * G) and k % 4 == 2:
                        copy_head(k // 4, it)
                    if u == 4 and valid(p - 1, NG):
                        copy_out(p - 1, it)
                    if u == 12 and valid(p + V_LEAD, NT * B):
                        copy_v(p + V_LEAD, it)
                    if u == 13 and valid(p + QK_LEAD, NT * B):
                        spread(p + QK_LEAD, it)

            groups(act, period)

        @block.vector
        def _(dve):
            LINKS = 8
            done = [0]

            def link(ins):
                ins.then_inc(s_dve, 1)
                done[0] += 1

            def linked(it, back=0):
                wait(dve, it, s_dve, done[0] - back, LINKS)

            def row_max(n, it):
                wait(dve, it, s_amm, n + 1, U)
                g, h, qt = n // U, n // NT, n % NT
                dve.reduce_max(mx[:, g % 2, n % U:n % U + 1], psA[n % 2][:, :], AX_X).then_inc(s_max, 1)

            def split_max(g, k, it):
                m = mx[:, g % 2, :]
                if k == 0:
                    wait(dve, it, s_max, U * (g + 1), U)
                    wait(dve, it, s_mtr, 2 * g, 2)
                    link(dve.tensor_scalar(mstk[:, :, 0], m, -1.0, None, ALU.mult))
                elif k == 1:
                    linked(it)
                    link(dve.scalar_tensor_tensor(mrest[:, :], m, -1.0, mstk[:, :, 0], ALU.mult, ALU.subtract))
                elif k == 2:
                    linked(it)
                    link(dve.tensor_copy(mstk[:, :, 1], mrest[:, :]))
                else:
                    linked(it)
                    dve.tensor_tensor(mstk[:, :, 2], mrest[:, :], mstk[:, :, 1], ALU.subtract).then_inc(s_msp, 1)

            def copy_max(g, half, it):
                wait(dve, it, s_mtr, 2 * g + half + 1, 2)
                dve.tensor_copy(qk[96:128, g % RING, 2 * half:2 * half + 2, 0, :],
                                psMt[96:128, :].rearrange("p (j l) -> p j l", l=L)).then_inc(s_mev, 1)

            def norm_out(g, k, it):
                b, hg = g // HG, g % HG
                o = psM[:, :].rearrange("p (n c) -> p n c", c=32)
                if k == 0:
                    wait(dve, it, s_otr, g + 1, 1)
                    link(dve.reciprocal(rden[:, :], o[:, :, DH]))
                else:
                    linked(it)
                    if hg == 0:
                        v = 16 * (b // 2)
                        if it is not None:
                            dve.wait_ge(s_ost[b % 2], v + it * 16)
                        elif v > 0:
                            dve.wait_ge(s_ost[b % 2], v)
                    dve.tensor_tensor(ob[:, b % 2, :, hg * G * DH:(hg + 1) * G * DH].rearrange("p t (j d) -> p t j d", d=DH),
                                      o[:, :, 0:DH].rearrange("p (t j) d -> p t j d", j=G),
                                      rden[:, :].rearrange("p (t j) -> p t j", j=G).unsqueeze(3).to_broadcast([P, NT, G, DH]),
                                      ALU.mult).then_inc(s_onrm, 1)

            def heads_of(t):
                return t[:, :].rearrange("p (h d) -> p h d", d=DH)

            def rope(tile, k, it):
                b, t = tile // NT, tile % NT
                x, half = heads_of(psX), DH // 2
                st = stack[:, b % 2, t].rearrange("p i h (m d) -> p (i h) m d", d=DH)

                def table(tb, c0, c1):
                    return tb[:, t, c0:c1].unsqueeze(1).to_broadcast([P, 2 * H, c1 - c0])

                if k == 0:
                    wait(dve, it, s_qmm, tile + 1, 1)
                    dve.tensor_tensor(heads_of(rc), x, table(cos, 0, DH), ALU.mult)
                elif k == 1:
                    dve.tensor_tensor(heads_of(rs)[:, :, 0:half], x[:, :, half:], table(sin, 0, half), ALU.mult)
                elif k == 2:
                    ins = dve.tensor_tensor(heads_of(rs)[:, :, half:], x[:, :, 0:half], table(sin, half, DH), ALU.mult)
                    ins.then_inc(s_qrd, 1)
                elif k == 3:
                    wait(dve, it, s_qrd, tile + 1, 1)
                    link(dve.tensor_tensor(rr[:, :], rc[:, :], rs[:, :], ALU.add))
                elif k == 4:
                    linked(it)
                    if t == 0:
                        wait(dve, it, s_tmm, H * (b - 1), G)
                    link(dve.tensor_copy(st[:, :, 0, :], heads_of(rr)))
                elif k == 5:
                    linked(it)
                    link(dve.tensor_tensor(heads_of(r1), heads_of(rr), st[:, :, 0, :], ALU.subtract))
                elif k == 6:
                    linked(it)
                    link(dve.tensor_copy(st[:, :, 4, :], heads_of(r1)))
                elif k == 7:
                    linked(it)
                    dve.tensor_tensor(st[:, 0:H, 5, :], heads_of(r1)[:, 0:H], st[:, 0:H, 4, :], ALU.subtract)
                else:
                    dve.tensor_tensor(st[:, H:, 2, :], heads_of(r1)[:, H:], st[:, H:, 4, :], ALU.subtract).then_inc(s_qsp, 1)

            link(dve.memset(qk[96:128, :, :, 1, :], 0.0))
            dve.memset(V[:, :, :, :, DH + 1:], 0.0)
            dve.memset(V[:, :, :, :, DH:DH + 1], 1.0)
            link(dve.memset(mstk[:, :, :], 0.0))
            linked(None)
            dve.memset(qk[96:99, :, :, 1, :], 1.0).then_inc(s_const, 1)
            dve.wait_ge(s_w, 48)

            def period(p, it):
                for u in range(U):
                    n = p * U + u
                    if u == U - 1 and valid(p + 1, NG):
                        copy_max(p + 1, 0, it)
                    if valid(n + A_LEAD, NG * U):
                        row_max(n + A_LEAD, it)
                    if 3 <= u < 12 and valid(p + QK_LEAD, NT * B):
                        rope(p + QK_LEAD, u - 3, it)
                    if u in (6, 7) and valid(p - 1, NG):
                        norm_out(p - 1, u - 6, it)
                    if u in (12, 13) and valid(p + 1, NG):
                        split_max(p + 1, 2 * (u - 12), it)
                        split_max(p + 1, 2 * (u - 12) + 1, it)
                    if u == U - 1 and valid(p + 1, NG):
                        copy_max(p + 1, 1, it)

            def after_loop():
                done[0] += LINKS * BODY * (PASSES - 1)

            groups(dve, period, after_loop)


def norm_and_route(nc, x, attn, Wo, norm_w, router_wT, m):
    T, D = x.shape
    DC, NT = D // P, 4
    E = router_wT.shape[1]
    NB = T // (NT * P)
    TILES = NB * NT

    with ExitStack() as ctx:
        a = Steps(nc, ctx, "nrm")
        wo = a.sb("wo", [P, DC, D], F32)
        rw = a.sb("rw", [P, DC, E], F32)
        nw = a.sb("nw", [P, D], F32)
        ident = a.sb("ident", [P, P], F32)
        eps = a.sb("eps", [P, 2], F32)
        at = a.sb("at", [P, 2, NT, D], F32)
        xr = a.sb("xr", [P, 2, NT, D], F32)
        aT = a.sb("aT", [P, 2, D], F32)
        y = a.sb("y", [P, 4, D], F32)
        sq = a.sb("sq", [P, D], F32)
        st = a.sb("st", [P, 4, 6], F32)
        mv = a.sb("mv", [P, 4, 2], F32)
        sd = a.sb("sd", [P, 4, 4], F32)
        ms = a.sb("ms", [P, 4, 1], F32)

        psT = [a.ps(f"psT{i}", [P, 512], F32) for i in range(2)]
        psP = [a.ps(f"psP{i}", [P, 512], F32) for i in range(2)]
        psN = [a.ps(f"psN{i}", [P, 512], F32) for i in range(2)]
        psL = [a.ps(f"psL{i}", [P, 512], F32) for i in range(2)]

        s_w = a.sem("weights")
        s_in = [a.sem(f"rows_loaded{i}") for i in range(2)]
        s_id = a.sem("identity")
        s_ttr = a.sem("attn_turned")
        s_tcp = a.sem("attn_copied")
        s_prj = a.sem("projected")
        s_y = a.sem("residual_added")
        s_var = a.sem("variance")
        s_sd = a.sem("deviation")
        s_x1 = a.sem("x1")
        s_ms = a.sem("mean_square")
        s_rms = a.sem("root_mean_square")
        s_row = a.sem("normed")
        s_ntr = a.sem("normed_turned")
        s_ncp = a.sem("normed_copied")
        s_log = a.sem("logits")
        s_lcp = a.sem("logits_copied")
        s_dve = a.sem("vector_chain")

        block = ctx.enter_context(nc.Block())

        @block.sync
        def _(sp):
            sp.dma_start(wo[:, :, :], Wo.rearrange("(c p) n -> p c n", p=P)).then_inc(s_w, 16)
            sp.dma_start(rw[:, :, :], router_wT.rearrange("(c p) e -> p c e", p=P)).then_inc(s_w, 16)
            sp.dma_start(nw[:, :], norm_w.partition_broadcast(P)).then_inc(s_w, 16)
            a_blk = attn.rearrange("(b t p) d -> b p t d", t=NT, p=P)
            x_blk = x.rearrange("(b t p) d -> b p t d", t=NT, p=P)
            for b in range(NB):
                if b >= 2:
                    sp.wait_ge(s_y, NT * (b - 1))
                sp.dma_start(at[:, b % 2], a_blk[b]).then_inc(s_in[b % 2], 16)
                sp.dma_start(xr[:, b % 2], x_blk[b]).then_inc(s_in[b % 2], 16)

        @block.gpsimd
        def _(pool):
            for k, step in enumerate((
                lambda: pool.memset(ident[:, :], 0.0),
                lambda: pool.affine_select(out=ident[:, :], in_=ident[:, :], compare_op=ALU.not_equal, fill=1.0,
                                           base=0, pattern=[[-1, P]], channel_multiplier=1),
                lambda: pool.memset(eps[:, 0:1], 1e-5),
                lambda: pool.memset(eps[:, 1:2], 1e-8),
            )):
                step().then_inc(s_id, 1)
                pool.wait_ge(s_id, k + 1)

        SLOTS = TILES + 7

        def stages(slot, lags):
            return [slot - lag if 0 <= slot - lag < TILES else None for lag in lags]

        @block.tensor
        def _(pe):
            pe.wait_ge(s_id, 2)
            pe.wait_ge(s_w, 48)
            for slot in range(SLOTS):
                turn, proj, norm, route = stages(slot, (0, 1, 5, 6))
                if turn is not None:
                    i = turn
                    b, t = i // NT, i % NT
                    if t == 0:
                        pe.wait_ge(s_in[b % 2], 32 * (b // 2 + 1))
                    if i >= 2:
                        pe.wait_ge(s_tcp, i - 1)
                    for c in range(DC):
                        ins = pe.transpose(psT[i % 2][:, c * P:(c + 1) * P], at[:, b % 2, t, c * P:(c + 1) * P], ident[:, :])
                    ins.then_inc(s_ttr, 1)
                if proj is not None:
                    i = proj
                    pe.wait_ge(s_tcp, i + 1)
                    if i >= 2:
                        pe.wait_ge(s_y, i - 1)
                    for c in range(DC):
                        ins = pe.matmul(psP[i % 2][:, 0:D], aT[:, i % 2, c * P:(c + 1) * P], wo[:, c, :],
                                        start=(c == 0), stop=(c == DC - 1))
                    ins.then_inc(s_prj, 1)
                if norm is not None:
                    i = norm
                    pe.wait_ge(s_row, i + 1)
                    if i >= 2:
                        pe.wait_ge(s_ncp, i - 1)
                    for c in range(DC):
                        ins = pe.transpose(psN[i % 2][:, c * P:(c + 1) * P], m.rows[:, i, c * P:(c + 1) * P], ident[:, :])
                    ins.then_inc(s_ntr, 1)
                if route is not None:
                    i = route
                    pe.wait_ge(s_ncp, i + 1)
                    if i >= 2:
                        pe.wait_ge(s_lcp, i - 1)
                    for c in range(DC):
                        ins = pe.matmul(psL[i % 2][:, 0:E], m.rowsT[:, c, i * P:(i + 1) * P], rw[:, c, :],
                                        start=(c == 0), stop=(c == DC - 1))
                    ins.then_inc(s_log, 1)

        @block.scalar
        def _(act):
            act.wait_ge(s_id, 4)
            for slot in range(SLOTS):
                turn, dev, rms, norm, route = stages(slot, (0, 2, 3, 5, 6))
                if turn is not None:
                    i = turn
                    act.wait_ge(s_ttr, i + 1)
                    if i >= 2:
                        act.wait_ge(s_prj, i - 1)
                    act.activation(aT[:, i % 2, :], psT[i % 2][:, 0:D], ACT.Copy).then_inc(s_tcp, 1)
                if dev is not None:
                    i = dev
                    act.wait_ge(s_var, i + 1)
                    act.activation(sd[:, i % 4, 0:1], mv[:, i % 4, 1:2], ACT.Sqrt, bias=eps[:, 0:1]).then_inc(s_sd, 1)
                if rms is not None:
                    i = rms
                    act.wait_ge(s_x1, i + 1)
                    act.activation(sq[:, :], m.acc[:, i, :], ACT.Square, accum_out=ms[:, i % 4, :]).then_inc(s_ms, 1)
                    act.wait_ge(s_ms, i + 1)
                    act.activation(sd[:, i % 4, 2:3], ms[:, i % 4, :], ACT.Sqrt, bias=eps[:, 1:2], scale=1.0 / D).then_inc(s_rms, 1)
                if norm is not None:
                    i = norm
                    act.wait_ge(s_ntr, i + 1)
                    act.activation(m.rowsT[:, :, i * P:(i + 1) * P], psN[i % 2][:, 0:D].rearrange("p (c q) -> p c q", c=DC),
                                   ACT.Copy).then_inc(s_ncp, 1)
                if route is not None:
                    i = route
                    act.wait_ge(s_log, i + 1)
                    act.activation(m.logits[:, i, :], psL[i % 2][:, 0:E], ACT.Copy).then_inc(s_lcp, 1)

        @block.vector
        def _(dve):
            done = [0]

            def link(ins):
                ins.then_inc(s_dve, 1)
                done[0] += 1
                dve.wait_ge(s_dve, done[0])

            dve.wait_ge(s_w, 48)
            for slot in range(SLOTS):
                proj, dev, rms = stages(slot, (1, 3, 4))
                if dev is not None:
                    i = dev
                    dve.wait_ge(s_sd, i + 1)
                    link(dve.reciprocal(sd[:, i % 4, 1:2], sd[:, i % 4, 0:1]))
                    dve.tensor_scalar(m.acc[:, i, :], y[:, i % 4, :], mv[:, i % 4, 0:1], sd[:, i % 4, 1:2],
                                      ALU.subtract, ALU.mult).then_inc(s_x1, 1)
                if rms is not None:
                    i = rms
                    dve.wait_ge(s_rms, i + 1)
                    link(dve.reciprocal(sd[:, i % 4, 3:4], sd[:, i % 4, 2:3]))
                    dve.scalar_tensor_tensor(m.rows[:, i, :], m.acc[:, i, :], sd[:, i % 4, 3:4], nw[:, :],
                                             ALU.mult, ALU.mult).then_inc(s_row, 1)
                if proj is not None:
                    i = proj
                    b, t = i // NT, i % NT
                    if t == 0:
                        dve.wait_ge(s_in[b % 2], 32 * (b // 2 + 1))
                    dve.wait_ge(s_prj, i + 1)
                    dve.tensor_tensor(y[:, i % 4, :], psP[i % 2][:, 0:D], xr[:, b % 2, t, :], ALU.add).then_inc(s_y, 1)
                    dve.wait_ge(s_y, i + 1)
                    link(dve.bn_stats(st[:, i % 4, :], y[:, i % 4, :]))
                    dve.bn_aggr(mv[:, i % 4, :], st[:, i % 4, :]).then_inc(s_var, 1)


def shared_and_dispatch(nc, sw1, sb1c, sw2, sb2, tri, marks, slots_x, m):
    D, HID = sw1.shape
    DC, HC = D // P, HID // P
    TILES, E = m.logits.shape[1], m.logits.shape[2]
    BL = 512
    NB = TILES * P // BL
    NT = BL // P
    LT = m.list_tile
    NL = m.tile_expert.shape[1]
    MOST = TILES * P // LT

    with ExitStack() as ctx:
        a = Steps(nc, ctx, "shr")
        w1 = a.sb("w1", [P, DC, HID], F32)
        w2 = a.sb("w2", [P, HC, D], F32)
        b1 = a.sb("b1", [P, HC], F32)
        b2 = a.sb("b2", [P, D], F32)
        hT = a.sb("hT", [P, 2, HC, BL], F32)
        trs = a.sb("trs", [P, P], F32)
        ones = a.sb("ones", [P, P], F32)
        mk = a.sb("mk", [P, marks.shape[1]], F32)
        prb = a.sb("prb", [P, TILES, E], F32)
        key = a.sb("key", [P, TILES, E], F32)
        oh = a.sb("oh", [P, 2, TILES, E], F32)
        both = a.sb("both", [P, TILES, E], F32)
        top = a.sb("top", [P, 2, TILES], F32)
        kt = a.sb("kt", [P, TILES], F32)
        den = a.sb("den", [P, TILES], F32)
        tot = a.sb("tot", [P, E, TILES], F32)
        cum = a.sb("cum", [P, E, TILES], F32)
        over = a.sb("over", [P, E, MOST], F32)
        nb = a.sb("nb", [P, E], F32)
        cb = a.sb("cb", [P, E], F32)
        base = a.sb("base", [P, E], F32)
        pos = a.sb("pos", [P, TILES, E], F32)
        spot = a.sb("spot", [P, 2, TILES], F32)
        past = a.sb("past", [P, NL, E], F32)
        tef = a.sb("tef", [P, NL], F32)

        psU = [a.ps(f"psU{i}", [P, BL], F32) for i in range(4)]
        psD = [a.ps(f"psD{i}", [P, 512], F32) for i in range(2)]
        psR = a.ps("psR", [P, 512], F32)
        psC = a.ps("psC", [P, 512], F32)

        s_w = a.sem("weights")
        s_k = a.sem("constants")
        s_up = a.sem("up")
        s_rel = a.sem("relu")
        s_relv = a.sem("relu_vector")
        s_dn = a.sem("down")
        s_add = a.sem("added")
        s_sig = a.sem("probabilities")
        s_both = a.sem("experts_marked")
        s_rank = a.sem("ranks")
        s_tot = a.sem("totals_read")
        s_slot = a.sem("slots")
        s_sc = a.sem("rows_scattered")
        s_dve = a.sem("vector_chain")

        rev = mk[:, 0:E]
        thr = mk[:, E:E + MOST]
        idx = mk[:, E + MOST:E + MOST + NL]
        first = mk[:, E + MOST + NL:E + MOST + NL + TILES]
        assert marks.shape[1] == E + MOST + NL + TILES

        block = ctx.enter_context(nc.Block())

        @block.sync
        def _(sp):
            sp.dma_start(mk[:, :], marks).then_inc(s_k, 16)
            sp.dma_start(trs[:, :], tri).then_inc(s_k, 16)
            sp.dma_start(w1[:, :, :], sw1.rearrange("(c p) h -> p c h", p=P)).then_inc(s_w, 16)
            sp.dma_start(b1[:, :], sb1c).then_inc(s_w, 16)
            sp.dma_start(b2[:, :], sb2.partition_broadcast(P)).then_inc(s_w, 16)
            sp.dma_start(w2[:, :, :], sw2.rearrange("(c p) o -> p c o", p=P)).then_inc(s_w, 16)

        @block.tensor
        def _(pe):
            pe.wait_ge(s_w, 64)
            for b in range(NB):
                for h in range(HC):
                    n = b * HC + h
                    if n >= 4:
                        pe.wait_ge(s_rel if n % 2 == 0 else s_relv, (n - 4) // 2 + 1)
                    for c in range(DC):
                        ins = pe.matmul(psU[n % 4][:, :], w1[:, c, h * P:(h + 1) * P], m.rowsT[:, c, b * BL:(b + 1) * BL],
                                        start=(c == 0), stop=(c == DC - 1))
                    ins.then_inc(s_up, 1)
                if b == 0:
                    pe.wait_ge(s_both, 1)
                    pe.wait_ge(s_k, 32)
                    flat = both[:, :, :].rearrange("p t e -> p (t e)")
                    pe.matmul(psR[:, 0:TILES * E], trs[:, :], flat, start=True, stop=True)
                    pe.matmul(psC[:, 0:TILES * E], ones[:, :], flat, start=True, stop=True).then_inc(s_rank, 1)
                for t in range(NT):
                    i = b * NT + t
                    if i >= 2:
                        pe.wait_ge(s_add, i - 1)
                    for h in range(HC):
                        if t == 0:
                            n = b * HC + h
                            pe.wait_ge(s_rel if n % 2 == 0 else s_relv, n // 2 + 1)
                        ins = pe.matmul(psD[i % 2][:, 0:D], hT[:, b % 2, h, t * P:(t + 1) * P], w2[:, h, :],
                                        start=(h == 0), stop=(h == HC - 1))
                    ins.then_inc(s_dn, 1)

        @block.scalar
        def _(act):
            act.activation(prb[:, :, :], m.logits[:, :, :], ACT.Sigmoid).then_inc(s_sig, 1)
            act.wait_ge(s_w, 64)
            for b in range(NB):
                if b >= 2:
                    act.wait_ge(s_dn, NT * (b - 1))
                for h in range(0, HC, 2):
                    n = b * HC + h
                    act.wait_ge(s_up, n + 1)
                    act.activation(hT[:, b % 2, h, :], psU[n % 4][:, :], ACT.Relu, bias=b1[:, h:h + 1]).then_inc(s_rel, 1)

        @block.vector
        def _(dve):
            done = [0]

            def link(ins):
                ins.then_inc(s_dve, 1)
                done[0] += 1
                dve.wait_ge(s_dve, done[0])

            def over_experts(v):
                return v.unsqueeze(2).to_broadcast([P, TILES, E])

            def over_tiles(v):
                return v.unsqueeze(1).to_broadcast([P, TILES, E])

            def pick(k):
                link(dve.reduce_max(top[:, k, :], prb[:, :, :], AX_X))
                link(dve.tensor_tensor(key[:, :, :], prb[:, :, :], over_experts(top[:, k, :]), ALU.is_equal))
                link(dve.tensor_tensor(key[:, :, :], key[:, :, :], over_tiles(rev), ALU.mult))
                link(dve.reduce_max(kt[:, :], key[:, :, :], AX_X))
                link(dve.tensor_tensor(oh[:, k, :, :], key[:, :, :], over_experts(kt[:, :]), ALU.is_equal))

            def choose():
                dve.wait_ge(s_k, 32)
                dve.wait_ge(s_sig, 1)
                link(dve.memset(ones[:, :], 1.0))
                pick(0)
                link(dve.scalar_tensor_tensor(prb[:, :, :].rearrange("p t e -> p (t e)"), oh[:, 0, :, :].rearrange("p t e -> p (t e)"),
                                              -2.0, prb[:, :, :].rearrange("p t e -> p (t e)"), ALU.mult, ALU.add))
                pick(1)
                dve.tensor_tensor(both[:, :, :], oh[:, 0, :, :], oh[:, 1, :, :], ALU.add).then_inc(s_both, 1)
                link(dve.tensor_tensor(den[:, :], top[:, 0, :], top[:, 1, :], ALU.add))
                link(dve.tensor_scalar(den[:, :], den[:, :], 1e-6, None, ALU.add))
                link(dve.reciprocal(den[:, :], den[:, :]))
                link(dve.tensor_tensor(m.gate[:, :, :], top[:, :, :], den[:, :].unsqueeze(1).to_broadcast([P, 2, TILES]), ALU.mult))

            def place():
                dve.wait_ge(s_rank, 1)
                link(dve.tensor_copy(tot[:, :, :], psC[:, 0:TILES * E].rearrange("p (t e) -> p e t", e=E)))
                for e in range(E):
                    link(dve.tensor_tensor_scan(cum[:, e, :], first, tot[:, e, :], 0.0, ALU.mult, ALU.add))
                link(dve.tensor_tensor(over[:, :, :], cum[:, :, TILES - 1:TILES].to_broadcast([P, E, MOST]),
                                       thr.unsqueeze(1).to_broadcast([P, E, MOST]), ALU.is_gt))
                link(dve.reduce_sum(nb[:, :], over[:, :, :], AX_X))
                link(dve.tensor_tensor_scan(cb[:, :], first[:, 0:E], nb[:, :], 0.0, ALU.mult, ALU.add))
                link(dve.tensor_tensor(base[:, :], cb[:, :], nb[:, :], ALU.subtract))
                link(dve.tensor_scalar(base[:, :], base[:, :], float(LT), None, ALU.mult))
                link(dve.tensor_tensor(cum[:, :, :], cum[:, :, :], tot[:, :, :], ALU.subtract))
                link(dve.tensor_tensor(pos[:, :, :], psR[:, 0:TILES * E].rearrange("p (t e) -> p t e", e=E),
                                       cum[:, :, :].rearrange("p e t -> p t e"), ALU.add))
                link(dve.tensor_tensor(pos[:, :, :], pos[:, :, :], over_tiles(base[:, :]), ALU.add))
                for k in range(2):
                    link(dve.tensor_tensor(key[:, :, :], pos[:, :, :], oh[:, k, :, :], ALU.mult))
                    link(dve.reduce_sum(spot[:, k, :], key[:, :, :], AX_X))
                dve.tensor_copy(m.slot[:, :, :], spot[:, :, :]).then_inc(s_slot, 1)
                link(dve.tensor_tensor(past[:, :, :], idx.unsqueeze(2).to_broadcast([P, NL, E]),
                                       cb[:, :].unsqueeze(1).to_broadcast([P, NL, E]), ALU.is_ge))
                link(dve.reduce_sum(tef[:, :], past[:, :, :], AX_X))
                link(dve.tensor_scalar(tef[:, :], tef[:, :], float(E - 1), None, ALU.min))
                link(dve.tensor_copy(m.tile_expert[:, :], tef[:, :]))

            choose()
            dve.wait_ge(s_w, 64)
            for b in range(NB):
                for h in range(1, HC, 2):
                    n = b * HC + h
                    if b >= 2 and h == 1:
                        dve.wait_ge(s_dn, NT * (b - 1))
                    dve.wait_ge(s_up, n + 1)
                    dve.tensor_scalar(hT[:, b % 2, h, :], psU[n % 4][:, :], b1[:, h:h + 1], 0.0, ALU.add, ALU.max).then_inc(s_relv, 1)
                if b == 0:
                    place()
                for t in range(NT):
                    i = b * NT + t
                    link(dve.tensor_tensor(m.acc[:, i, :], m.acc[:, i, :], b2[:, :], ALU.add))
                    dve.wait_ge(s_dn, i + 1)
                    dve.tensor_tensor(m.acc[:, i, :], psD[i % 2][:, 0:D], m.acc[:, i, :], ALU.add).then_inc(s_add, 1)

        @block.gpsimd
        def _(pool):
            pool.wait_ge(s_slot, 1)
            for i in range(TILES):
                for k in range(2):
                    pool.indirect_dma_start(slots_x, bass.IndirectOffsetOnAxis(ap=m.slot[:, k, i:i + 1], axis=0),
                                            m.rows[:, i, :], None).then_inc(s_sc, 16)
            pool.wait_ge(s_sc, 16 * 2 * TILES)


def experts(nc, slots_x, ew1, eb1c, ew2, eb2, slots_y, m):
    E, D, HID = ew1.shape
    DC, HC = D // P, HID // P
    LT = m.list_tile
    NL = m.tile_expert.shape[1]
    RT = LT // P
    assert NL % 2 == 0 and RT * D == 512

    with ExitStack() as ctx:
        a = Steps(nc, ctx, "exp")
        ident = a.sb("ident", [P, P], F32)
        w1 = a.sb("w1", [P, 2, DC, HID], F32)
        w2 = a.sb("w2", [P, 2, HC, D], F32)
        b1 = a.sb("b1", [P, 2, HC], F32)
        b2 = a.sb("b2", [P, 2, D], F32)
        xs = a.sb("xs", [P, 2, RT, D], F32)
        xT = a.sb("xT", [P, 2, DC, LT], F32)
        hT = a.sb("hT", [P, 2, HC, LT], F32)
        ys = a.sb("ys", [P, 2, RT, D], F32)

        psT = a.ps("psT", [P, 512], F32)
        psU = [a.ps(f"psU{i}", [P, 512], F32) for i in range(4)]
        psD = [a.ps(f"psD{i}", [P, 512], F32) for i in range(2)]

        s_id = a.sem("identity")
        s_xs = [a.sem(f"rows_loaded{i}") for i in range(2)]
        s_w = [a.sem(f"weights_loaded{i}") for i in range(2)]
        s_tr = a.sem("rows_turned")
        s_tc = a.sem("rows_ready")
        s_up = a.sem("up")
        s_rel = a.sem("relu")
        s_relv = a.sem("relu_vector")
        s_dn = a.sem("down")
        s_y = a.sem("outputs")
        s_st = [a.sem(f"stored{i}") for i in range(2)]

        x_tile = slots_x.rearrange("(n r p) d -> n p r d", r=RT, p=P)
        y_tile = slots_y.rearrange("(n r p) d -> n p r d", r=RT, p=P)

        block = ctx.enter_context(nc.Block())

        def passes(eng, tile):
            for k in range(2):
                tile(k, k, lambda v, rise: v)
            with eng.Fori(1, NL // 2) as it:
                for k in range(2):
                    tile(k, k + it * 2, lambda v, rise: v + it * rise)

        @block.sync
        def _(sp):
            def tile(k, j, at, first=False):
                e = sp.value_load(m.tile_expert[0:1, bass.ds(j, 1)], min_val=0, max_val=E - 1)
                if not first:
                    sp.wait_ge(s_tr, at(k - 1, 2))
                sp.dma_start(xs[:, k], x_tile[bass.ds(j, 1)].rearrange("o p r d -> p (o r) d")).then_inc(s_xs[k], 16)
                if not first:
                    sp.wait_ge(s_y, at(RT * (k - 1), 2 * RT))
                sp.dma_start(w1[:, k], ew1[bass.ds(e, 1)].rearrange("o (c p) h -> p (o c) h", p=P)).then_inc(s_w[k], 16)
                sp.dma_start(b1[:, k, :], eb1c[bass.ds(e, 1)].rearrange("o p h -> p (o h)")).then_inc(s_w[k], 16)
                sp.dma_start(w2[:, k], ew2[bass.ds(e, 1)].rearrange("o (c p) d -> p (o c) d", p=P)).then_inc(s_w[k], 16)
                sp.dma_start(b2[:, k, :], eb2[bass.ds(e, 1), :].to_broadcast([P, D])).then_inc(s_w[k], 16)

            for k in range(2):
                tile(k, k, None, True)
            with sp.Fori(1, NL // 2) as it:
                for k in range(2):
                    tile(k, k + it * 2, lambda v, rise: v + it * rise)

        @block.gpsimd
        def _(pool):
            pool.memset(ident[:, :], 0.0).then_inc(s_id, 1)
            pool.wait_ge(s_id, 1)
            pool.affine_select(out=ident[:, :], in_=ident[:, :], compare_op=ALU.not_equal, fill=1.0,
                               base=0, pattern=[[-1, P]], channel_multiplier=1).then_inc(s_id, 1)

            def tile(k, j, at):
                pass

        @block.tensor
        def _(pe):
            pe.wait_ge(s_id, 2)

            def turn(k, at, first):
                pe.wait_ge(s_xs[k], at(16, 16))
                if not first:
                    pe.wait_ge(s_tc, at(k, 2))
                for r in range(RT):
                    for c in range(DC):
                        ins = pe.transpose(psT[:, c * LT + r * P:c * LT + (r + 1) * P], xs[:, k, r, c * P:(c + 1) * P], ident[:, :])
                ins.then_inc(s_tr, 1)

            def compute(k, at, first, turn_next):
                pe.wait_ge(s_tc, at(k + 1, 2))
                pe.wait_ge(s_w[k], at(64, 64))
                for h in range(HC):
                    if not (first and k == 0 and h < 4):
                        pe.wait_ge(s_rel if h % 2 == 0 else s_relv, at((k * HC + h - 4) // 2 + 1, HC))
                    for c in range(DC):
                        ins = pe.matmul(psU[h % 4][:, 0:LT], w1[:, k, c, h * P:(h + 1) * P], xT[:, k, c, :],
                                        start=(c == 0), stop=(c == DC - 1))
                    ins.then_inc(s_up, 1)
                turn_next()
                for r in range(RT):
                    if not (first and k == 0):
                        pe.wait_ge(s_y, at(RT * k + r - RT + 1, 2 * RT))
                    for h in range(HC):
                        if r == 0:
                            pe.wait_ge(s_rel if h % 2 == 0 else s_relv, at((k * HC + h) // 2 + 1, HC))
                        ins = pe.matmul(psD[r][:, 0:D], hT[:, k, h, r * P:(r + 1) * P], w2[:, k, h, :],
                                        start=(h == 0), stop=(h == HC - 1))
                    ins.then_inc(s_dn, 1)

            def here(v, rise):
                return v

            turn(0, here, True)
            compute(0, here, True, lambda: turn(1, here, False))
            compute(1, here, True, lambda: turn(0, lambda v, rise: v + rise, False))
            with pe.Fori(1, NL // 2 - 1) as it:
                def now(v, rise):
                    return v + it * rise

                compute(0, now, False, lambda: turn(1, now, False))
                compute(1, now, False, lambda: turn(0, lambda v, rise: v + rise + it * rise, False))

            def last(v, rise):
                return v + (NL // 2 - 1) * rise

            compute(0, last, False, lambda: turn(1, last, False))
            compute(1, last, False, lambda: None)

        @block.scalar
        def _(act):
            def tile(k, at, first):
                act.wait_ge(s_tr, at(k + 1, 2))
                if not first:
                    act.wait_ge(s_up, at(HC * (k - 1), 2 * HC))
                act.activation(xT[:, k], psT[:, :].rearrange("p (c r) -> p c r", c=DC), ACT.Copy).then_inc(s_tc, 1)

            def relus(k, at, first):
                act.wait_ge(s_w[k], at(64, 64))
                if not first:
                    act.wait_ge(s_dn, at(RT * (k - 1), 2 * RT))
                for h in range(0, HC, 2):
                    act.wait_ge(s_up, at(k * HC + h + 1, 2 * HC))
                    act.activation(hT[:, k, h, :], psU[h % 4][:, 0:LT], ACT.Relu, bias=b1[:, k, h:h + 1]).then_inc(s_rel, 1)

            def here(v, rise):
                return v

            tile(0, here, True)
            relus(0, here, True)
            tile(1, here, True)
            relus(1, here, True)
            with act.Fori(1, NL // 2) as it:
                def now(v, rise):
                    return v + it * rise

                for k in range(2):
                    tile(k, now, False)
                    relus(k, now, False)

        @block.vector
        def _(dve):
            def tile(k, at, first):
                dve.wait_ge(s_w[k], at(64, 64))
                if not first:
                    dve.wait_ge(s_dn, at(RT * (k - 1), 2 * RT))
                for h in range(1, HC, 2):
                    dve.wait_ge(s_up, at(k * HC + h + 1, 2 * HC))
                    dve.tensor_scalar(hT[:, k, h, :], psU[h % 4][:, 0:LT], b1[:, k, h:h + 1], 0.0, ALU.add, ALU.max).then_inc(s_relv, 1)
                if not first:
                    dve.wait_ge(s_st[k], at(0, 16))
                for r in range(RT):
                    dve.wait_ge(s_dn, at(RT * k + r + 1, 2 * RT))
                    dve.tensor_tensor(ys[:, k, r, :], psD[r][:, 0:D], b2[:, k, :], ALU.add).then_inc(s_y, 1)

            def here(v, rise):
                return v

            tile(0, here, True)
            tile(1, here, True)
            with dve.Fori(1, NL // 2) as it:
                def now(v, rise):
                    return v + it * rise

                for k in range(2):
                    tile(k, now, False)

        @block.gpsimd
        def _(pool):
            with pool.Fori(0, NL // 2) as it:
                for k in range(2):
                    pool.wait_ge(s_y, RT * (k + 1) + it * (2 * RT))
                    pool.dma_start(y_tile[bass.ds(k + it * 2, 1)].rearrange("o p r d -> p (o r) d"), ys[:, k]).then_inc(s_st[k], 16)
            for k in range(2):
                pool.wait_ge(s_st[k], 16 * (NL // 2))


def combine(nc, slots_y, out, m):
    T, D = out.shape
    TILES = T // P
    R = 4

    with ExitStack() as ctx:
        a = Steps(nc, ctx, "out")
        g = a.sb("g", [P, R, 2, D], F32)
        y = a.sb("y", [P, R, D], F32)
        o = a.sb("o", [P, R, D], F32)
        st = a.sb("st", [P, R, 6], F32)
        mv = a.sb("mv", [P, R, 2], F32)
        sd = a.sb("sd", [P, R, 2], F32)
        eps = a.sb("eps", [P, 1], F32)
        s_g = [a.sem(f"gathered{i}") for i in range(R)]
        s_eps = a.sem("eps_set")
        s_var = a.sem("variance")
        s_sd = a.sem("deviation")
        s_o = a.sem("normed")
        s_y = a.sem("summed")
        s_st = [a.sem(f"stored{i}") for i in range(R)]
        s_dve = a.sem("vector_chain")
        block = ctx.enter_context(nc.Block())

        @block.gpsimd
        def _(pool):
            for i in range(TILES):
                if i >= R:
                    pool.wait_ge(s_y, i - R + 1)
                for k in range(2):
                    pool.indirect_dma_start(g[:, i % R, k, :], None, slots_y,
                                            bass.IndirectOffsetOnAxis(ap=m.slot[:, k, i:i + 1], axis=0)).then_inc(s_g[i % R], 16)

        @block.vector
        def _(dve):
            done = [0]

            def link(ins):
                ins.then_inc(s_dve, 1)
                done[0] += 1
                dve.wait_ge(s_dve, done[0])

            dve.memset(eps[:, :], 1e-5).then_inc(s_eps, 1)
            for i in range(TILES + 1):
                if i < TILES:
                    r = i % R
                    dve.wait_ge(s_g[r], 32 * (i // R + 1))
                    link(dve.scalar_tensor_tensor(y[:, r, :], g[:, r, 0, :], m.gate[:, 0, i:i + 1], m.acc[:, i, :], ALU.mult, ALU.add))
                    dve.scalar_tensor_tensor(y[:, r, :], g[:, r, 1, :], m.gate[:, 1, i:i + 1], y[:, r, :], ALU.mult, ALU.add).then_inc(s_y, 1)
                    dve.wait_ge(s_y, i + 1)
                    link(dve.bn_stats(st[:, r, :], y[:, r, :]))
                    dve.bn_aggr(mv[:, r, :], st[:, r, :]).then_inc(s_var, 1)
                if i >= 1:
                    j = i - 1
                    r = j % R
                    dve.wait_ge(s_sd, j + 1)
                    link(dve.reciprocal(sd[:, r, 1:2], sd[:, r, 0:1]))
                    if j >= R:
                        dve.wait_ge(s_st[r], 16 * (j // R))
                    dve.tensor_scalar(o[:, r, :], y[:, r, :], mv[:, r, 0:1], sd[:, r, 1:2], ALU.subtract, ALU.mult).then_inc(s_o, 1)

        @block.scalar
        def _(act):
            act.wait_ge(s_eps, 1)
            for i in range(TILES):
                act.wait_ge(s_var, i + 1)
                act.activation(sd[:, i % R, 0:1], mv[:, i % R, 1:2], ACT.Sqrt, bias=eps[:, 0:1]).then_inc(s_sd, 1)

        @block.sync
        def _(sp):
            for i in range(TILES):
                sp.wait_ge(s_o, i + 1)
                sp.dma_start(out[i * P:(i + 1) * P, :], o[:, i % R, :]).then_inc(s_st[i % R], 16)
            for r in range(R):
                sp.wait_ge(s_st[r], 16 * (TILES // R))


class Carried:

    def __init__(self, nc, ctx, T, D, E, list_tile):
        a = Steps(nc, ctx, "all")
        n = T // P
        self.list_tile = list_tile
        lists = 2 * T // list_tile + E
        self.acc = a.sb("acc", [P, n, D], F32)
        self.rows = a.sb("rows", [P, n, D], F32)
        self.rowsT = a.sb("rowsT", [P, D // P, T], F32)
        self.logits = a.sb("logits", [P, n, E], F32)
        self.gate = a.sb("gate", [P, 2, n], F32)
        self.slot = a.sb("slot", [P, 2, n], U32)
        self.tile_expert = a.sb("tile_expert", [P, lists], I32)


def layer(nc, x, xT, Wqkv, rope_cos, rope_sin, Wo, norm_w, router_wT, sw1, sb1c, sw2, sb2,
          ew1, eb1c, ew2, eb2, tri, marks, out):
    T, D = x.shape
    E = ew1.shape[0]
    LT = 256
    slots = 2 * T + E * LT
    attn = nc.dram_tensor("attn_rows", (T, D), F32, kind="Internal").ap()
    slots_x = nc.dram_tensor("slots_x", (slots, D), F32, kind="Internal").ap()
    slots_y = nc.dram_tensor("slots_y", (slots, D), F32, kind="Internal").ap()
    attention(nc, xT, Wqkv, rope_cos, rope_sin, attn, slots_x)
    with ExitStack() as ctx:
        m = Carried(nc, ctx, T, D, E, LT)
        norm_and_route(nc, x, attn, Wo, norm_w, router_wT, m)
        shared_and_dispatch(nc, sw1, sb1c, sw2, sb2, tri, marks, slots_x, m)
        experts(nc, slots_x, ew1, eb1c, ew2, eb2, slots_y, m)
        combine(nc, slots_y, out, m)


def kernel(L0_attn_x, L0_attn_Wqkv, L0_attn_Wo, L0_ffn_norm_weight, L0_ffn_router_w, L0_ffn_sw1, L0_ffn_sb1,
           L0_ffn_sw2, L0_ffn_sb2, L0_ffn_ew1, L0_ffn_eb1, L0_ffn_ew2, L0_ffn_eb2):
    import concourse.bacc as bacc
    from concourse.bass_utils import run_bass_kernel_spmd

    x = np.asarray(L0_attn_x)
    B, L, D = x.shape
    T = B * L
    x2 = np.ascontiguousarray(x.reshape(T, D))
    E, _, HID = L0_ffn_ew1.shape
    DH, LT = 16, 256
    inv = (1.0 / np.float32(10000.0) ** (np.arange(0, DH, 2, dtype=np.float32) / np.float32(DH))).astype(np.float32)
    angles = np.outer(np.arange(L, dtype=np.float32), inv).astype(np.float32)
    angles = np.concatenate([angles, angles], -1)
    signs = np.where(np.arange(DH) < DH // 2, -1.0, 1.0).astype(np.float32)

    def by_tile(t):
        return np.ascontiguousarray(t.astype(np.float32).reshape(L // P, P, DH).transpose(1, 0, 2))

    tri = np.triu(np.ones((P, P), np.float32), 1)
    lists = 2 * T // LT + E
    marks = np.concatenate([
        np.arange(E, 0, -1), LT * np.arange(T // LT), np.arange(lists), np.arange(T // P) > 0,
    ]).astype(np.float32)
    marks = np.ascontiguousarray(np.broadcast_to(marks, (P, marks.size)))
    arrays = {
        "x": x2,
        "xT": np.ascontiguousarray(x2.T),
        "Wqkv": np.asarray(L0_attn_Wqkv),
        "rope_cos": by_tile(np.cos(angles)),
        "rope_sin": by_tile(np.sin(angles) * signs),
        "Wo": np.asarray(L0_attn_Wo),
        "norm_w": np.asarray(L0_ffn_norm_weight),
        "router_wT": np.ascontiguousarray(np.asarray(L0_ffn_router_w).T),
        "sw1": np.asarray(L0_ffn_sw1),
        "sb1c": np.ascontiguousarray(np.asarray(L0_ffn_sb1).reshape(HID // P, P).T),
        "sw2": np.asarray(L0_ffn_sw2),
        "sb2": np.asarray(L0_ffn_sb2),
        "ew1": np.asarray(L0_ffn_ew1),
        "eb1c": np.ascontiguousarray(np.asarray(L0_ffn_eb1).reshape(E, HID // P, P).transpose(0, 2, 1)),
        "ew2": np.asarray(L0_ffn_ew2),
        "eb2": np.asarray(L0_ffn_eb2),
        "tri": tri,
        "marks": marks,
    }
    nc = bacc.Bacc("TRN2", target_bir_lowering=False, num_devices=1)
    args = [nc.dram_tensor(n, v.shape, mybir.dt.from_np(v.dtype), kind="ExternalInput").ap() for n, v in arrays.items()]
    out = nc.dram_tensor("out", (T, D), F32, kind="ExternalOutput").ap()
    layer(nc, *args, out)
    r = run_bass_kernel_spmd(nc, [arrays], core_ids=[0])
    return r.results[0]["out"].reshape(B, L, D)
```

```python
from contextlib import ExitStack

import concourse.bass as bass
from concourse import mybir
import numpy as np

F32 = mybir.dt.float32
F32R = mybir.dt.float32r
BF16 = mybir.dt.bfloat16
U32 = mybir.dt.uint32
I32 = mybir.dt.int32
ALU = mybir.AluOpType
ACT = mybir.ActivationFunctionType
AX_X = mybir.AxisListType.X
P = 128


class Steps:

    def __init__(self, nc, ctx, tag):
        self.nc, self.ctx, self.tag = nc, ctx, tag

    def sb(self, name, shape, dt):
        return self.ctx.enter_context(self.nc.sbuf_tensor(f"{self.tag}_{name}", shape, dt))

    def ps(self, name, shape, dt):
        return self.ctx.enter_context(self.nc.psum_tensor(f"{self.tag}_{name}", shape, dt))

    def sem(self, name):
        return self.ctx.enter_context(self.nc.semaphore(f"{self.tag}_{name}"))


def attention(nc, xT, Wqkv, rope_cos, rope_sin, attn_out, slots_x):
    D, T = xT.shape
    DH, L = rope_cos.shape[2], P * rope_cos.shape[1]
    H = D // DH
    B = T // L
    NT = L // P
    DC = D // P
    G = 4
    HG = H // G
    U = G * NT
    NG = B * HG
    TERMS = 6
    KR = TERMS * DH
    SCALE = float(DH) ** -0.5
    A_LEAD = U + 4
    BODY = 2 * HG
    FIRST = 1
    PASSES = (NG - FIRST - 1) // BODY
    HEAD, TAIL = FIRST, FIRST + PASSES * BODY
    QK_LEAD, V_LEAD = 6, 4
    T_LEAD = A_LEAD + 8
    PROJECT_QK, ROPE, COPY_OUT, TURN_OUT, NORM_OUT = (1, 2), (2, 3, 4), 4, 7, (9, 10)
    PROJECT_V, COPY_V, SPLIT_MAX, TURN_MAX, COPY_MAX = 11, 12, 12, (13, 15), (14, U)
    PIECE_1, PIECE_2, SPREAD, SPLIT_X = 7, 11, 0, 12
    ADD_PV = 2
    RING = 4
    PR = 8
    assert NT == HG and NG % BODY == 0 and U == 16

    Q_PIECES, K_PIECES = (1, 1, 1, 2, 2, 3), (1, 2, 3, 1, 2, 1)
    assert len(Q_PIECES) == len(K_PIECES) == TERMS

    with ExitStack() as ctx:
        a = Steps(nc, ctx, "att")
        w = a.sb("w", [P, DC, 3 * D], F32)
        cos = a.sb("cos", [P, NT, DH], F32)
        sin = a.sb("sin", [P, NT, DH], F32)
        xt = a.sb("xt", [P, 2, DC, L], F32)
        wh = a.sb("wh", [P, DC, 3 * D], F32R)
        wl = a.sb("wl", [P, DC, 3 * D], F32R)
        xh = a.sb("xh", [P, 2, DC, L], F32R)
        xl = a.sb("xl", [P, 2, DC, L], F32R)
        zero = a.sb("zero", [P, 2048], F32)
        ident = a.sb("ident", [P, P], BF16)
        identf = a.sb("identf", [P, P], F32)
        stack = a.sb("stack", [P, 2, NT, 2, H, KR], BF16)
        qk = a.sb("qk", [P, RING, G, 2, L], BF16)
        V = a.sb("V", [P, 2, NT, H, 32], F32)
        prob = a.sb("prob", [P, PR, L], F32)
        mx = a.sb("mx", [P, 2, U], F32)
        mrest = a.sb("mrest", [P, U], F32)
        mstk = a.sb("mstk", [P, U, 32], BF16)
        rc = a.sb("rc", [P, 2 * D], F32)
        rs = a.sb("rs", [P, 2 * D], F32)
        rr = a.sb("rr", [P, 2 * D], F32)
        r1 = a.sb("r1", [P, 2 * D], F32)
        oT = a.sb("oT", [P, L], F32)
        rden = a.sb("rden", [P, U], F32)
        ob = a.sb("ob", [P, 2, NT, D], F32)

        psA = [a.ps(f"psA{i}", [P, L], F32) for i in range(3)]
        A_BANK = [0, 1, 2] * 5 + [1]
        psB = [a.ps(f"psB{i}", [P, L], F32) for i in range(2)]
        psV = a.ps("psV", [P, L], F32)
        psT = a.ps("psT", [P, 2, L], BF16)
        psX = a.ps("psX", [P, 512], F32)
        psXt = psX[:, :].bitcast(BF16)

        s_w = a.sem("w_loaded")
        s_x = [a.sem(f"x_loaded{i}") for i in range(2)]
        s_wh, s_wl = a.sem("w_hi"), a.sem("w_lo")
        s_xh, s_xl = a.sem("x_hi"), a.sem("x_lo")
        s_const = a.sem("constants")
        s_init = a.sem("init")
        s_zero = a.sem("slots_zeroed")
        s_amm = a.sem("score_rows")
        s_max = a.sem("row_max")
        s_bmm = a.sem("score_cols")
        s_exp = a.sem("probs")
        s_pv = a.sem("pv")
        s_oev = a.sem("o_copied")
        s_otr = a.sem("o_turned")
        s_onrm = a.sem("o_normed")
        s_ost = [a.sem(f"o_stored{i}") for i in range(2)]
        s_tmm = a.sem("head_turned")
        s_tev = a.sem("head_ready")
        s_msp = a.sem("max_split")
        s_mtr = a.sem("max_turned")
        s_mev = a.sem("max_ready")
        s_qmm = a.sem("qk_projected")
        s_qrd = a.sem("qk_read")
        s_rr = a.sem("qk_turned")
        s_p1 = a.sem("piece_1")
        s_r1 = a.sem("rest_1")
        s_p2 = a.sem("piece_2")
        s_p3 = a.sem("piece_3_q")
        s_qsp = a.sem("qk_split")
        s_stk = a.sem("stacked")
        s_vmm = a.sem("v_projected")
        s_vev = a.sem("v_ready")
        s_dve = a.sem("vector_chain")

        def at(it, v, per_group):
            return v if it is None else v + it * (per_group * BODY)

        def wait(eng, it, s, v, per_group):
            if it is None and v <= 0:
                return
            assert v > 0, (v, s)
            eng.wait_ge(s, at(it, v, per_group))

        def groups(eng, period, after_loop=None):
            for p in range(-QK_LEAD, HEAD):
                period(p, None)
            with eng.Fori(0, PASSES) as it:
                for p in range(HEAD, HEAD + BODY):
                    period(p, it)
            if after_loop is not None:
                after_loop()
            for p in range(TAIL, NG + 1):
                period(p, None)

        def valid(i, n):
            return 0 <= i < n

        def heads_of(t):
            return t[:, :].rearrange("p (h d) -> p h d", d=DH)

        def terms(stack, b, t):
            return stack[:, b % 2, t].rearrange("p i h (m d) -> p (i h) m d", d=DH)

        block = ctx.enter_context(nc.Block())

        @block.sync
        def _(sp):
            x_seq = xT.rearrange("(c p) (b l) -> b p c l", p=P, l=L)
            out_seq = attn_out.rearrange("(b t p) d -> b p t d", t=NT, p=P)
            sp.dma_start(w[:, :, :], Wqkv.rearrange("(c p) n -> p c n", p=P)).then_inc(s_w, 16)
            sp.wait_ge(s_w, 16)
            sp.dma_start(xt[:, 0, :, :], x_seq[0]).then_inc(s_x[0], 16)
            sp.dma_start(cos[:, :, :], rope_cos).then_inc(s_w, 16)
            sp.dma_start(sin[:, :, :], rope_sin).then_inc(s_w, 16)
            sp.dma_start(xt[:, 1, :, :], x_seq[1]).then_inc(s_x[1], 16)
            with sp.Fori(0, B // 2 - 1) as i:
                for k in range(2):
                    sp.wait_ge(s_xl, k + 1 + i * 2)
                    sp.dma_start(xt[:, k, :, :], x_seq[bass.ds(2 + k + i * 2, 1)].rearrange("o p c l -> p (o c) l")).then_inc(s_x[k], 16)
                    sp.wait_ge(s_onrm, HG * (k + 1) + i * (2 * HG))
                    sp.dma_start(out_seq[bass.ds(k + i * 2, 1)].rearrange("o p t d -> p (o t) d"), ob[:, k, :, :]).then_inc(s_ost[k], 16)
            for k in range(2):
                sp.wait_ge(s_onrm, HG * (B - 1 + k))
                sp.dma_start(out_seq[B - 2 + k], ob[:, k, :, :]).then_inc(s_ost[k], 16)
            for k in range(2):
                sp.wait_ge(s_ost[k], 16 * (B // 2))

        @block.gpsimd
        def _(pool):
            for k, step in enumerate((
                lambda: pool.memset(ident[:, :], 0.0),
                lambda: pool.affine_select(out=ident[:, :], in_=ident[:, :], compare_op=ALU.not_equal, fill=1.0,
                                           base=0, pattern=[[-1, P]], channel_multiplier=1),
                lambda: pool.memset(identf[:, :], 0.0),
                lambda: pool.affine_select(out=identf[:, :], in_=identf[:, :], compare_op=ALU.not_equal, fill=1.0,
                                           base=0, pattern=[[-1, P]], channel_multiplier=1),
                lambda: pool.memset(zero[:, :], 0.0),
            )):
                step().then_inc(s_init, 1)
                pool.wait_ge(s_init, k + 1)
            rows = slots_x.shape[0] // P
            slots = slots_x.rearrange("(p r) d -> p (r d)", p=P)
            n = 0
            for c in range(0, rows * D, 2048):
                pool.dma_start(slots[:, c:c + 2048], zero[:, :]).then_inc(s_zero, 16)
                n += 16

            def x_lo(b, it):
                v = b + 1
                pool.wait_ge(s_xh, v if it is None else v + it * 2)
                pool.tensor_tensor(xl[:, b % 2], xt[:, b % 2], xh[:, b % 2].bitcast(F32), ALU.subtract).then_inc(s_xl, 1)

            def period(p, it):
                tile = p + QK_LEAD
                if not valid(tile, NT * B):
                    return
                b, t = tile // NT, tile % NT
                st = terms(stack, b, t)
                wait(pool, it, s_qrd, tile + 1, 1)
                pool.tensor_tensor(rr[:, :], rc[:, :], rs[:, :], ALU.add).then_inc(s_rr, 1)
                wait(pool, it, s_p1, tile + 1, 1)
                pool.tensor_tensor(heads_of(r1), heads_of(rr), st[:, :, 0, :], ALU.subtract).then_inc(s_r1, 1)
                wait(pool, it, s_p2, tile + 1, 1)
                pool.tensor_tensor(st[:, 0:H, 5, :], heads_of(r1)[:, 0:H], st[:, 0:H, 4, :], ALU.subtract).then_inc(s_p3, 1)
                wait(pool, it, s_p3, tile + 1, 1)
                pool.tensor_tensor(st[:, H:, 2, :], heads_of(r1)[:, H:], st[:, H:, 4, :], ALU.subtract).then_inc(s_qsp, 1)
                if t == NT - 1 and valid(tile + 1, NT * B):
                    x_lo(b + 1, it)

            pool.wait_ge(s_wh, 1)
            pool.tensor_tensor(wl[:, :, :], w[:, :, :], wh[:, :, :].bitcast(F32), ALU.subtract).then_inc(s_wl, 1)
            x_lo(0, None)
            groups(pool, period)
            pool.wait_ge(s_zero, n)

        @block.tensor
        def _(pe):
            pe.wait_ge(s_init, 4)
            pe.wait_ge(s_const, 1)
            pe.wait_ge(s_wl, 1)

            def score_rows(n, it):
                g, h, qt = n // U, n // NT, n % NT
                if qt == 0:
                    wait(pe, it, s_tev, h + 1, G)
                back = next(d for d in range(1, U) if A_BANK[(n - d) % U] == A_BANK[n % U])
                wait(pe, it, s_max, n - back + 1, U)
                r = qk[0:KR, g % RING, h % G]
                pe.matmul(psA[A_BANK[n % U]][:, :], r[:, 0, qt * P:(qt + 1) * P], r[:, 1, :], start=True, stop=True).then_inc(s_amm, 1)

            def score_cols(n, it):
                g, u = n // U, n % U
                kt, j = u // G, u % G
                if u % 2 == 0 and u < G:
                    wait(pe, it, s_mev, 2 * g + 1 + u // 2, 2)
                wait(pe, it, s_exp, n - 1, U)
                r = qk[:, g % RING, j]
                pe.matmul(psB[n % 2][:, :], r[:, 1, kt * P:(kt + 1) * P], r[:, 0, :], start=True, stop=True).then_inc(s_bmm, 1)

            def turn_head(h, half, it):
                g, b = h // G, h // H
                if half == 0:
                    wait(pe, it, s_tev, h, G)
                    if h % H == 0:
                        wait(pe, it, s_stk, NT * (b + 1), 1)
                for t in range(NT):
                    m = pe.transpose(psT[0:KR, half, t * P:(t + 1) * P], stack[:, b % 2, t, half, h % H, :], ident[:, :])
                if half == 1:
                    m.then_inc(s_tmm, 1)

            QK, OUT, VALUE, MAX0, MAX1 = range(5)

            def take_psX(p, use, it):
                if it is not None:
                    last = {QK: (s_mev, 2 * p + 2, 2), OUT: (s_qrd, p + QK_LEAD + 1, 1), VALUE: (s_onrm, p, 1),
                            MAX0: (s_vev, p + V_LEAD + 1, 1), MAX1: (s_mev, 2 * p + 3, 2)}[use]
                    wait(pe, it, *last)
                    return
                for s, n, most in ((s_qrd, p + QK_LEAD + (use > QK), NG), (s_onrm, p - 1 + (use > OUT), NG),
                                   (s_vev, p + V_LEAD + (use > VALUE), NG), (s_mev, 2 * p + 2 + (use > MAX0), 2 * NG)):
                    wait(pe, it, s, min(n, most), 1)

            def turn_max(g, half, it):
                take_psX(g - 1, (MAX0, MAX1)[half], it)
                if half == 0:
                    wait(pe, it, s_msp, g + 1, 1)
                for k in range(U // 2):
                    m = pe.transpose(psXt[96:128, k * P:(k + 1) * P], mstk[:, half * (U // 2) + k, :], ident[:, :])
                m.then_inc(s_mtr, 1)

            def add_pv(g, kt, it):
                b, hg = g // HG, g % HG
                if kt == 0:
                    wait(pe, it, s_oev, g, 1)
                    if hg == 0:
                        wait(pe, it, s_vev, NT * (b + 1), 1)
                n = g * U + kt * G
                wait(pe, it, s_exp, n + G, U)
                for j in range(G):
                    m = pe.matmul(psV[32 * j:32 * j + 32, :], V[:, b % 2, kt, hg * G + j, :], prob[:, (n + j) % PR, :],
                                  start=(kt == 0), stop=(kt == NT - 1))
                m.then_inc(s_pv, 1)

            def turn_out(g, it):
                take_psX(g + 1, OUT, it)
                wait(pe, it, s_oev, g + 1, 1)
                for qt in range(NT):
                    m = pe.transpose(psX[:, qt * P:(qt + 1) * P], oT[:, qt * P:(qt + 1) * P], identf[:, :])
                m.then_inc(s_otr, 1)

            def project(tile, c, it, value):
                b, t = tile // NT, tile % NT
                if c == 0:
                    take_psX(tile - (V_LEAD if value else QK_LEAD), VALUE if value else QK, it)
                    if t == 0 and not value:
                        pe.wait_ge(s_xl, b + 1 if it is None else b + 1 + it * 2)
                o, cols = (psX[:, 0:D], slice(2 * D, 3 * D)) if value else (psX[:, :], slice(0, 2 * D))
                rows = slice(t * P, (t + 1) * P)
                pe.matmul(o, xh[:, b % 2, c, rows], wh[:, c, cols], start=(c == 0), stop=False)
                pe.matmul(o, xh[:, b % 2, c, rows], wl[:, c, cols], start=False, stop=False)
                m = pe.matmul(o, xl[:, b % 2, c, rows], wh[:, c, cols], start=False, stop=(c == DC - 1))
                if c == DC - 1:
                    m.then_inc(s_vmm if value else s_qmm, 1)

            def period(p, it):
                for u in range(U):
                    n = p * U + u
                    if valid(n, NG * U):
                        score_cols(n, it)
                    if valid(n + A_LEAD, NG * U):
                        score_rows(n + A_LEAD, it)
                    k = n + T_LEAD
                    if valid(k // 4, NG * G) and k % 4 < 2:
                        turn_head(k // 4, k % 4, it)
                    if u % G == ADD_PV and valid(n - ADD_PV - G, NG * U):
                        add_pv((n - ADD_PV - G) // U, ((n - ADD_PV - G) % U) // G, it)
                    if u in TURN_MAX and valid(p + 1, NG):
                        turn_max(p + 1, TURN_MAX.index(u), it)
                    if u == TURN_OUT and valid(p - 1, NG):
                        turn_out(p - 1, it)
                    if u in PROJECT_QK and valid(p + QK_LEAD, NT * B):
                        project(p + QK_LEAD, PROJECT_QK.index(u), it, False)
                    if u == PROJECT_V and valid(p + V_LEAD, NT * B):
                        for c in range(DC):
                            project(p + V_LEAD, c, it, True)

            groups(pe, period)

        @block.scalar
        def _(act):
            def exps(n, it):
                wait(act, it, s_bmm, n + 1, U)
                if n % G == 0:
                    wait(act, it, s_pv, n // G + 1 - PR // G, NT)
                act.activation(prob[:, n % PR, :], psB[n % 2][:, :], ACT.Exp, scale=SCALE).then_inc(s_exp, 1)

            def copy_head(h, it):
                g = h // G
                wait(act, it, s_tmm, h + 1, G)
                act.activation(qk[0:KR, g % RING, h % G, :, :], psT[0:KR, :, :], ACT.Copy).then_inc(s_tev, 1)

            def copy_out(g, it):
                wait(act, it, s_pv, NT * (g + 1), NT)
                act.activation(oT[:, :], psV[:, :], ACT.Copy).then_inc(s_oev, 1)

            def copy_v(tile, it):
                b, t = tile // NT, tile % NT
                wait(act, it, s_vmm, tile + 1, 1)
                if t == 0:
                    wait(act, it, s_pv, NT * HG * (b - 1), NT)
                act.activation(V[:, b % 2, t, :, 0:DH], psX[:, 0:D].rearrange("p (h d) -> p h d", d=DH), ACT.Copy).then_inc(s_vev, 1)

            def spread(tile, it):
                b, t = tile // NT, tile % NT
                q, k = (stack[:, b % 2, t, i].rearrange("p h (m d) -> p h m d", d=DH) for i in range(2))
                wait(act, it, s_qsp, tile + 1, 1)
                act.activation(q[:, :, 1:3, :], q[:, :, 0:1, :].to_broadcast([P, H, 2, DH]), ACT.Copy)
                act.activation(k[:, :, 3:6:2, :], k[:, :, 0:1, :].to_broadcast([P, H, 2, DH]), ACT.Copy)
                act.activation(q[:, :, 3, :], q[:, :, 4, :], ACT.Copy)
                act.activation(k[:, :, 1, :], k[:, :, 4, :], ACT.Copy).then_inc(s_stk, 1)

            def x_hi(b, it):
                v = 16 * (b // 2 + 1)
                act.wait_ge(s_x[b % 2], v if it is None else v + it * 16)
                wait(act, it, s_vmm, NT * (b - 1), 1)
                act.activation(xh[:, b % 2], xt[:, b % 2], ACT.Copy).then_inc(s_xh, 1)

            act.wait_ge(s_w, 16)
            act.activation(wh[:, :, :], w[:, :, :], ACT.Copy).then_inc(s_wh, 1)
            x_hi(0, None)

            def period(p, it):
                for u in range(U):
                    n = p * U + u
                    if u == SPLIT_X and (p + QK_LEAD + 1) % NT == 0 and valid(p + QK_LEAD + 1, NT * B):
                        x_hi((p + QK_LEAD + 1) // NT, it)
                    if valid(n, NG * U):
                        exps(n, it)
                    k = n + T_LEAD
                    if valid(k // 4, NG * G) and k % 4 == 2:
                        copy_head(k // 4, it)
                    if u == COPY_OUT and valid(p - 1, NG):
                        copy_out(p - 1, it)
                    if u == COPY_V and valid(p + V_LEAD, NT * B):
                        copy_v(p + V_LEAD, it)
                    if u == SPREAD and valid(p + QK_LEAD - 1, NT * B):
                        spread(p + QK_LEAD - 1, it)

            groups(act, period)

        @block.vector
        def _(dve):
            LINKS = 4
            done = [0]

            def link(ins):
                ins.then_inc(s_dve, 1)
                done[0] += 1

            def linked(it, back=0):
                wait(dve, it, s_dve, done[0] - back, LINKS)

            def row_max(n, it):
                wait(dve, it, s_amm, n + 1, U)
                g, h, qt = n // U, n // NT, n % NT
                dve.reduce_max(mx[:, g % 2, n % U:n % U + 1], psA[A_BANK[n % U]][:, :], AX_X).then_inc(s_max, 1)

            def split_max(g, k, it):
                m = mx[:, g % 2, :]
                if k == 0:
                    wait(dve, it, s_max, U * (g + 1), U)
                    wait(dve, it, s_mtr, 2 * g, 2)
                    link(dve.tensor_scalar(mstk[:, :, 0], m, -1.0, None, ALU.mult))
                elif k == 1:
                    linked(it)
                    link(dve.scalar_tensor_tensor(mrest[:, :], m, -1.0, mstk[:, :, 0], ALU.mult, ALU.subtract))
                elif k == 2:
                    linked(it)
                    link(dve.tensor_copy(mstk[:, :, 1], mrest[:, :]))
                else:
                    linked(it)
                    dve.tensor_tensor(mstk[:, :, 2], mrest[:, :], mstk[:, :, 1], ALU.subtract).then_inc(s_msp, 1)

            def copy_max(g, half, it):
                wait(dve, it, s_mtr, 2 * g + half + 1, 2)
                dve.tensor_copy(qk[96:128, g % RING, 2 * half:2 * half + 2, 0, :],
                                psXt[96:128, :].rearrange("p (j l) -> p j l", l=L)).then_inc(s_mev, 1)

            def norm_out(g, k, it):
                b, hg = g // HG, g % HG
                o = psX[:, :].rearrange("p (n c) -> p n c", c=32)
                if k == 0:
                    wait(dve, it, s_otr, g + 1, 1)
                    link(dve.reciprocal(rden[:, :], o[:, :, DH]))
                else:
                    linked(it)
                    if hg == 0:
                        v = 16 * (b // 2)
                        if it is not None:
                            dve.wait_ge(s_ost[b % 2], v + it * 16)
                        elif v > 0:
                            dve.wait_ge(s_ost[b % 2], v)
                    dve.tensor_tensor(ob[:, b % 2, :, hg * G * DH:(hg + 1) * G * DH].rearrange("p t (j d) -> p t j d", d=DH),
                                      o[:, :, 0:DH].rearrange("p (t j) d -> p t j d", j=G),
                                      rden[:, :].rearrange("p (t j) -> p t j", j=G).unsqueeze(3).to_broadcast([P, NT, G, DH]),
                                      ALU.mult).then_inc(s_onrm, 1)

            def rope(tile, k, it):
                b, t = tile // NT, tile % NT
                x, half = heads_of(psX), DH // 2

                def table(tb, c0, c1):
                    return tb[:, t, c0:c1].unsqueeze(1).to_broadcast([P, 2 * H, c1 - c0])

                if k == 0:
                    wait(dve, it, s_qmm, tile + 1, 1)
                    wait(dve, it, s_rr, tile, 1)
                    dve.tensor_tensor(heads_of(rc), x, table(cos, 0, DH), ALU.mult)
                elif k == 1:
                    dve.tensor_tensor(heads_of(rs)[:, :, 0:half], x[:, :, half:], table(sin, 0, half), ALU.mult)
                else:
                    dve.tensor_tensor(heads_of(rs)[:, :, half:], x[:, :, 0:half], table(sin, half, DH), ALU.mult).then_inc(s_qrd, 1)

            def piece_1(tile, it):
                b, t = tile // NT, tile % NT
                wait(dve, it, s_rr, tile + 1, 1)
                if t == 0:
                    wait(dve, it, s_tmm, H * (b - 1), G)
                dve.tensor_copy(terms(stack, b, t)[:, :, 0, :], heads_of(rr)).then_inc(s_p1, 1)

            def piece_2(tile, it):
                b, t = tile // NT, tile % NT
                wait(dve, it, s_r1, tile + 1, 1)
                dve.tensor_copy(terms(stack, b, t)[:, :, 4, :], heads_of(r1)).then_inc(s_p2, 1)

            link(dve.memset(qk[96:128, :, :, 1, :], 0.0))
            dve.memset(V[:, :, :, :, DH + 1:], 0.0)
            dve.memset(V[:, :, :, :, DH:DH + 1], 1.0)
            link(dve.memset(mstk[:, :, :], 0.0))
            linked(None)
            dve.memset(qk[96:99, :, :, 1, :], 1.0).then_inc(s_const, 1)
            dve.wait_ge(s_w, 48)

            def period(p, it):
                for u in range(U):
                    n = p * U + u
                    if u == COPY_MAX[1] % U and valid(p, NG):
                        copy_max(p, 1, it)
                    if u == COPY_MAX[0] and valid(p + 1, NG):
                        copy_max(p + 1, 0, it)
                    if valid(n + A_LEAD, NG * U):
                        row_max(n + A_LEAD, it)
                    if u in ROPE and valid(p + QK_LEAD, NT * B):
                        rope(p + QK_LEAD, ROPE.index(u), it)
                    if u == PIECE_1 and valid(p + QK_LEAD, NT * B):
                        piece_1(p + QK_LEAD, it)
                    if u == PIECE_2 and valid(p + QK_LEAD, NT * B):
                        piece_2(p + QK_LEAD, it)
                    if u in NORM_OUT and valid(p - 1, NG):
                        norm_out(p - 1, NORM_OUT.index(u), it)
                    if u == SPLIT_MAX and valid(p + 1, NG):
                        for k in range(4):
                            split_max(p + 1, k, it)

            def after_loop():
                done[0] += LINKS * BODY * (PASSES - 1)

            groups(dve, period, after_loop)


def norm_and_route(nc, x, attn, Wo, norm_w, router_wT, m):
    T, D = x.shape
    DC, NT = D // P, 4
    E = router_wT.shape[1]
    NB = T // (NT * P)
    TILES = NB * NT

    with ExitStack() as ctx:
        a = Steps(nc, ctx, "nrm")
        wo = a.sb("wo", [P, DC, D], F32)
        rw = a.sb("rw", [P, DC, E], F32)
        nw = a.sb("nw", [P, D], F32)
        ident = a.sb("ident", [P, P], F32)
        eps = a.sb("eps", [P, 2], F32)
        at = a.sb("at", [P, 2, NT, D], F32)
        xr = a.sb("xr", [P, 2, NT, D], F32)
        aT = a.sb("aT", [P, 2, D], F32)
        y = a.sb("y", [P, 4, D], F32)
        sq = a.sb("sq", [P, D], F32)
        st = a.sb("st", [P, 4, 6], F32)
        mv = a.sb("mv", [P, 4, 2], F32)
        sd = a.sb("sd", [P, 4, 4], F32)
        ms = a.sb("ms", [P, 4, 1], F32)

        psT = [a.ps(f"psT{i}", [P, 512], F32) for i in range(2)]
        psP = [a.ps(f"psP{i}", [P, 512], F32) for i in range(2)]
        psN = [a.ps(f"psN{i}", [P, 512], F32) for i in range(2)]
        psL = [a.ps(f"psL{i}", [P, 512], F32) for i in range(2)]

        s_w = a.sem("weights")
        s_in = [a.sem(f"rows_loaded{i}") for i in range(2)]
        s_id = a.sem("identity")
        s_ttr = a.sem("attn_turned")
        s_tcp = a.sem("attn_copied")
        s_prj = a.sem("projected")
        s_y = a.sem("residual_added")
        s_var = a.sem("variance")
        s_sd = a.sem("deviation")
        s_x1 = a.sem("x1")
        s_ms = a.sem("mean_square")
        s_rms = a.sem("root_mean_square")
        s_row = a.sem("normed")
        s_ntr = a.sem("normed_turned")
        s_ncp = a.sem("normed_copied")
        s_log = a.sem("logits")
        s_lcp = a.sem("logits_copied")
        s_dve = a.sem("vector_chain")

        block = ctx.enter_context(nc.Block())

        @block.sync
        def _(sp):
            sp.dma_start(wo[:, :, :], Wo.rearrange("(c p) n -> p c n", p=P)).then_inc(s_w, 16)
            sp.dma_start(rw[:, :, :], router_wT.rearrange("(c p) e -> p c e", p=P)).then_inc(s_w, 16)
            sp.dma_start(nw[:, :], norm_w.partition_broadcast(P)).then_inc(s_w, 16)
            a_blk = attn.rearrange("(b t p) d -> b p t d", t=NT, p=P)
            x_blk = x.rearrange("(b t p) d -> b p t d", t=NT, p=P)
            for b in range(NB):
                if b >= 2:
                    sp.wait_ge(s_y, NT * (b - 1))
                sp.dma_start(at[:, b % 2], a_blk[b]).then_inc(s_in[b % 2], 16)
                sp.dma_start(xr[:, b % 2], x_blk[b]).then_inc(s_in[b % 2], 16)

        @block.gpsimd
        def _(pool):
            for k, step in enumerate((
                lambda: pool.memset(ident[:, :], 0.0),
                lambda: pool.affine_select(out=ident[:, :], in_=ident[:, :], compare_op=ALU.not_equal, fill=1.0,
                                           base=0, pattern=[[-1, P]], channel_multiplier=1),
                lambda: pool.memset(eps[:, 0:1], 1e-5),
                lambda: pool.memset(eps[:, 1:2], 1e-8),
            )):
                step().then_inc(s_id, 1)
                pool.wait_ge(s_id, k + 1)

        SLOTS = TILES + 7

        def stages(slot, lags):
            return [slot - lag if 0 <= slot - lag < TILES else None for lag in lags]

        @block.tensor
        def _(pe):
            pe.wait_ge(s_id, 2)
            pe.wait_ge(s_w, 48)
            for slot in range(SLOTS):
                turn, proj, norm, route = stages(slot, (0, 1, 5, 6))
                if turn is not None:
                    i = turn
                    b, t = i // NT, i % NT
                    if t == 0:
                        pe.wait_ge(s_in[b % 2], 32 * (b // 2 + 1))
                    if i >= 2:
                        pe.wait_ge(s_tcp, i - 1)
                    for c in range(DC):
                        ins = pe.transpose(psT[i % 2][:, c * P:(c + 1) * P], at[:, b % 2, t, c * P:(c + 1) * P], ident[:, :])
                    ins.then_inc(s_ttr, 1)
                if proj is not None:
                    i = proj
                    pe.wait_ge(s_tcp, i + 1)
                    if i >= 2:
                        pe.wait_ge(s_y, i - 1)
                    for c in range(DC):
                        ins = pe.matmul(psP[i % 2][:, 0:D], aT[:, i % 2, c * P:(c + 1) * P], wo[:, c, :],
                                        start=(c == 0), stop=(c == DC - 1))
                    ins.then_inc(s_prj, 1)
                if norm is not None:
                    i = norm
                    pe.wait_ge(s_row, i + 1)
                    if i >= 2:
                        pe.wait_ge(s_ncp, i - 1)
                    for c in range(DC):
                        ins = pe.transpose(psN[i % 2][:, c * P:(c + 1) * P], m.rows[:, i, c * P:(c + 1) * P], ident[:, :])
                    ins.then_inc(s_ntr, 1)
                if route is not None:
                    i = route
                    pe.wait_ge(s_ncp, i + 1)
                    if i >= 2:
                        pe.wait_ge(s_lcp, i - 1)
                    for c in range(DC):
                        ins = pe.matmul(psL[i % 2][:, 0:E], m.rowsT[:, c, i * P:(i + 1) * P], rw[:, c, :],
                                        start=(c == 0), stop=(c == DC - 1))
                    ins.then_inc(s_log, 1)

        @block.scalar
        def _(act):
            act.wait_ge(s_id, 4)
            for slot in range(SLOTS):
                turn, dev, rms, norm, route = stages(slot, (0, 2, 3, 5, 6))
                if turn is not None:
                    i = turn
                    act.wait_ge(s_ttr, i + 1)
                    if i >= 2:
                        act.wait_ge(s_prj, i - 1)
                    act.activation(aT[:, i % 2, :], psT[i % 2][:, 0:D], ACT.Copy).then_inc(s_tcp, 1)
                if dev is not None:
                    i = dev
                    act.wait_ge(s_var, i + 1)
                    act.activation(sd[:, i % 4, 0:1], mv[:, i % 4, 1:2], ACT.Sqrt, bias=eps[:, 0:1]).then_inc(s_sd, 1)
                if rms is not None:
                    i = rms
                    act.wait_ge(s_x1, i + 1)
                    act.activation(sq[:, :], m.acc[:, i, :], ACT.Square, accum_out=ms[:, i % 4, :]).then_inc(s_ms, 1)
                    act.wait_ge(s_ms, i + 1)
                    act.activation(sd[:, i % 4, 2:3], ms[:, i % 4, :], ACT.Sqrt, bias=eps[:, 1:2], scale=1.0 / D).then_inc(s_rms, 1)
                if norm is not None:
                    i = norm
                    act.wait_ge(s_ntr, i + 1)
                    act.activation(m.rowsT[:, :, i * P:(i + 1) * P], psN[i % 2][:, 0:D].rearrange("p (c q) -> p c q", c=DC),
                                   ACT.Copy).then_inc(s_ncp, 1)
                if route is not None:
                    i = route
                    act.wait_ge(s_log, i + 1)
                    act.activation(m.logits[:, i, :], psL[i % 2][:, 0:E], ACT.Copy).then_inc(s_lcp, 1)

        @block.vector
        def _(dve):
            done = [0]

            def link(ins):
                ins.then_inc(s_dve, 1)
                done[0] += 1
                dve.wait_ge(s_dve, done[0])

            dve.wait_ge(s_w, 48)
            for slot in range(SLOTS):
                proj, dev, rms = stages(slot, (1, 3, 4))
                if dev is not None:
                    i = dev
                    dve.wait_ge(s_sd, i + 1)
                    link(dve.reciprocal(sd[:, i % 4, 1:2], sd[:, i % 4, 0:1]))
                    dve.tensor_scalar(m.acc[:, i, :], y[:, i % 4, :], mv[:, i % 4, 0:1], sd[:, i % 4, 1:2],
                                      ALU.subtract, ALU.mult).then_inc(s_x1, 1)
                if rms is not None:
                    i = rms
                    dve.wait_ge(s_rms, i + 1)
                    link(dve.reciprocal(sd[:, i % 4, 3:4], sd[:, i % 4, 2:3]))
                    dve.scalar_tensor_tensor(m.rows[:, i, :], m.acc[:, i, :], sd[:, i % 4, 3:4], nw[:, :],
                                             ALU.mult, ALU.mult).then_inc(s_row, 1)
                if proj is not None:
                    i = proj
                    b, t = i // NT, i % NT
                    if t == 0:
                        dve.wait_ge(s_in[b % 2], 32 * (b // 2 + 1))
                    dve.wait_ge(s_prj, i + 1)
                    dve.tensor_tensor(y[:, i % 4, :], psP[i % 2][:, 0:D], xr[:, b % 2, t, :], ALU.add).then_inc(s_y, 1)
                    dve.wait_ge(s_y, i + 1)
                    link(dve.bn_stats(st[:, i % 4, :], y[:, i % 4, :]))
                    dve.bn_aggr(mv[:, i % 4, :], st[:, i % 4, :]).then_inc(s_var, 1)


def shared_and_dispatch(nc, sw1, sb1c, sw2, sb2, tri, marks, slots_x, m):
    D, HID = sw1.shape
    DC, HC = D // P, HID // P
    TILES, E = m.logits.shape[1], m.logits.shape[2]
    BL = 512
    NB = TILES * P // BL
    NT = BL // P
    LT = m.list_tile
    NL = m.tile_expert.shape[1]
    MOST = TILES * P // LT

    with ExitStack() as ctx:
        a = Steps(nc, ctx, "shr")
        w1 = a.sb("w1", [P, DC, HID], F32)
        w2 = a.sb("w2", [P, HC, D], F32)
        b1 = a.sb("b1", [P, HC], F32)
        b2 = a.sb("b2", [P, D], F32)
        hT = a.sb("hT", [P, 2, HC, BL], F32)
        trs = a.sb("trs", [P, P], F32)
        ones = a.sb("ones", [P, P], F32)
        mk = a.sb("mk", [P, marks.shape[1]], F32)
        prb = a.sb("prb", [P, TILES, E], F32)
        key = a.sb("key", [P, TILES, E], F32)
        oh = a.sb("oh", [P, 2, TILES, E], F32)
        both = a.sb("both", [P, TILES, E], F32)
        top = a.sb("top", [P, 2, TILES], F32)
        kt = a.sb("kt", [P, TILES], F32)
        den = a.sb("den", [P, TILES], F32)
        tot = a.sb("tot", [P, E, TILES], F32)
        cum = a.sb("cum", [P, E, TILES], F32)
        over = a.sb("over", [P, E, MOST], F32)
        nb = a.sb("nb", [P, E], F32)
        cb = a.sb("cb", [P, E], F32)
        base = a.sb("base", [P, E], F32)
        pos = a.sb("pos", [P, TILES, E], F32)
        spot = a.sb("spot", [P, 2, TILES], F32)
        past = a.sb("past", [P, NL, E], F32)
        tef = a.sb("tef", [P, NL], F32)

        psU = [a.ps(f"psU{i}", [P, BL], F32) for i in range(4)]
        psD = [a.ps(f"psD{i}", [P, 512], F32) for i in range(2)]
        psR = a.ps("psR", [P, 512], F32)
        psC = a.ps("psC", [P, 512], F32)

        s_w = a.sem("weights")
        s_k = a.sem("constants")
        s_up = a.sem("up")
        s_rel = a.sem("relu")
        s_relv = a.sem("relu_vector")
        s_dn = a.sem("down")
        s_add = a.sem("added")
        s_sig = a.sem("probabilities")
        s_both = a.sem("experts_marked")
        s_rank = a.sem("ranks")
        s_tot = a.sem("totals_read")
        s_slot = a.sem("slots")
        s_sc = a.sem("rows_scattered")
        s_dve = a.sem("vector_chain")

        rev = mk[:, 0:E]
        thr = mk[:, E:E + MOST]
        idx = mk[:, E + MOST:E + MOST + NL]
        first = mk[:, E + MOST + NL:E + MOST + NL + TILES]
        assert marks.shape[1] == E + MOST + NL + TILES

        block = ctx.enter_context(nc.Block())

        @block.sync
        def _(sp):
            sp.dma_start(mk[:, :], marks).then_inc(s_k, 16)
            sp.dma_start(trs[:, :], tri).then_inc(s_k, 16)
            sp.dma_start(w1[:, :, :], sw1.rearrange("(c p) h -> p c h", p=P)).then_inc(s_w, 16)
            sp.dma_start(b1[:, :], sb1c).then_inc(s_w, 16)
            sp.dma_start(b2[:, :], sb2.partition_broadcast(P)).then_inc(s_w, 16)
            sp.dma_start(w2[:, :, :], sw2.rearrange("(c p) o -> p c o", p=P)).then_inc(s_w, 16)

        @block.tensor
        def _(pe):
            pe.wait_ge(s_w, 64)
            for b in range(NB):
                for h in range(HC):
                    n = b * HC + h
                    if n >= 4:
                        pe.wait_ge(s_rel if n % 2 == 0 else s_relv, (n - 4) // 2 + 1)
                    for c in range(DC):
                        ins = pe.matmul(psU[n % 4][:, :], w1[:, c, h * P:(h + 1) * P], m.rowsT[:, c, b * BL:(b + 1) * BL],
                                        start=(c == 0), stop=(c == DC - 1))
                    ins.then_inc(s_up, 1)
                if b == 0:
                    pe.wait_ge(s_both, 1)
                    pe.wait_ge(s_k, 32)
                    flat = both[:, :, :].rearrange("p t e -> p (t e)")
                    pe.matmul(psR[:, 0:TILES * E], trs[:, :], flat, start=True, stop=True)
                    pe.matmul(psC[:, 0:TILES * E], ones[:, :], flat, start=True, stop=True).then_inc(s_rank, 1)
                for t in range(NT):
                    i = b * NT + t
                    if i >= 2:
                        pe.wait_ge(s_add, i - 1)
                    for h in range(HC):
                        if t == 0:
                            n = b * HC + h
                            pe.wait_ge(s_rel if n % 2 == 0 else s_relv, n // 2 + 1)
                        ins = pe.matmul(psD[i % 2][:, 0:D], hT[:, b % 2, h, t * P:(t + 1) * P], w2[:, h, :],
                                        start=(h == 0), stop=(h == HC - 1))
                    ins.then_inc(s_dn, 1)

        @block.scalar
        def _(act):
            act.activation(prb[:, :, :], m.logits[:, :, :], ACT.Sigmoid).then_inc(s_sig, 1)
            act.wait_ge(s_w, 64)
            for b in range(NB):
                if b >= 2:
                    act.wait_ge(s_dn, NT * (b - 1))
                for h in range(0, HC, 2):
                    n = b * HC + h
                    act.wait_ge(s_up, n + 1)
                    act.activation(hT[:, b % 2, h, :], psU[n % 4][:, :], ACT.Relu, bias=b1[:, h:h + 1]).then_inc(s_rel, 1)

        @block.vector
        def _(dve):
            done = [0]

            def link(ins):
                ins.then_inc(s_dve, 1)
                done[0] += 1
                dve.wait_ge(s_dve, done[0])

            def over_experts(v):
                return v.unsqueeze(2).to_broadcast([P, TILES, E])

            def over_tiles(v):
                return v.unsqueeze(1).to_broadcast([P, TILES, E])

            def pick(k):
                link(dve.reduce_max(top[:, k, :], prb[:, :, :], AX_X))
                link(dve.tensor_tensor(key[:, :, :], prb[:, :, :], over_experts(top[:, k, :]), ALU.is_equal))
                link(dve.tensor_tensor(key[:, :, :], key[:, :, :], over_tiles(rev), ALU.mult))
                link(dve.reduce_max(kt[:, :], key[:, :, :], AX_X))
                link(dve.tensor_tensor(oh[:, k, :, :], key[:, :, :], over_experts(kt[:, :]), ALU.is_equal))

            def choose():
                dve.wait_ge(s_k, 32)
                dve.wait_ge(s_sig, 1)
                link(dve.memset(ones[:, :], 1.0))
                pick(0)
                link(dve.scalar_tensor_tensor(prb[:, :, :].rearrange("p t e -> p (t e)"), oh[:, 0, :, :].rearrange("p t e -> p (t e)"),
                                              -2.0, prb[:, :, :].rearrange("p t e -> p (t e)"), ALU.mult, ALU.add))
                pick(1)
                dve.tensor_tensor(both[:, :, :], oh[:, 0, :, :], oh[:, 1, :, :], ALU.add).then_inc(s_both, 1)
                link(dve.tensor_tensor(den[:, :], top[:, 0, :], top[:, 1, :], ALU.add))
                link(dve.tensor_scalar(den[:, :], den[:, :], 1e-6, None, ALU.add))
                link(dve.reciprocal(den[:, :], den[:, :]))
                link(dve.tensor_tensor(m.gate[:, :, :], top[:, :, :], den[:, :].unsqueeze(1).to_broadcast([P, 2, TILES]), ALU.mult))

            def place():
                dve.wait_ge(s_rank, 1)
                link(dve.tensor_copy(tot[:, :, :], psC[:, 0:TILES * E].rearrange("p (t e) -> p e t", e=E)))
                for e in range(E):
                    link(dve.tensor_tensor_scan(cum[:, e, :], first, tot[:, e, :], 0.0, ALU.mult, ALU.add))
                link(dve.tensor_tensor(over[:, :, :], cum[:, :, TILES - 1:TILES].to_broadcast([P, E, MOST]),
                                       thr.unsqueeze(1).to_broadcast([P, E, MOST]), ALU.is_gt))
                link(dve.reduce_sum(nb[:, :], over[:, :, :], AX_X))
                link(dve.tensor_tensor_scan(cb[:, :], first[:, 0:E], nb[:, :], 0.0, ALU.mult, ALU.add))
                link(dve.tensor_tensor(base[:, :], cb[:, :], nb[:, :], ALU.subtract))
                link(dve.tensor_scalar(base[:, :], base[:, :], float(LT), None, ALU.mult))
                link(dve.tensor_tensor(cum[:, :, :], cum[:, :, :], tot[:, :, :], ALU.subtract))
                link(dve.tensor_tensor(pos[:, :, :], psR[:, 0:TILES * E].rearrange("p (t e) -> p t e", e=E),
                                       cum[:, :, :].rearrange("p e t -> p t e"), ALU.add))
                link(dve.tensor_tensor(pos[:, :, :], pos[:, :, :], over_tiles(base[:, :]), ALU.add))
                for k in range(2):
                    link(dve.tensor_tensor(key[:, :, :], pos[:, :, :], oh[:, k, :, :], ALU.mult))
                    link(dve.reduce_sum(spot[:, k, :], key[:, :, :], AX_X))
                dve.tensor_copy(m.slot[:, :, :], spot[:, :, :]).then_inc(s_slot, 1)
                link(dve.tensor_tensor(past[:, :, :], idx.unsqueeze(2).to_broadcast([P, NL, E]),
                                       cb[:, :].unsqueeze(1).to_broadcast([P, NL, E]), ALU.is_ge))
                link(dve.reduce_sum(tef[:, :], past[:, :, :], AX_X))
                link(dve.tensor_scalar(tef[:, :], tef[:, :], float(E - 1), None, ALU.min))
                link(dve.tensor_copy(m.tile_expert[:, :], tef[:, :]))

            choose()
            dve.wait_ge(s_w, 64)
            for b in range(NB):
                for h in range(1, HC, 2):
                    n = b * HC + h
                    if b >= 2 and h == 1:
                        dve.wait_ge(s_dn, NT * (b - 1))
                    dve.wait_ge(s_up, n + 1)
                    dve.tensor_scalar(hT[:, b % 2, h, :], psU[n % 4][:, :], b1[:, h:h + 1], 0.0, ALU.add, ALU.max).then_inc(s_relv, 1)
                if b == 0:
                    place()
                for t in range(NT):
                    i = b * NT + t
                    link(dve.tensor_tensor(m.acc[:, i, :], m.acc[:, i, :], b2[:, :], ALU.add))
                    dve.wait_ge(s_dn, i + 1)
                    dve.tensor_tensor(m.acc[:, i, :], psD[i % 2][:, 0:D], m.acc[:, i, :], ALU.add).then_inc(s_add, 1)

        @block.gpsimd
        def _(pool):
            pool.wait_ge(s_slot, 1)
            for i in range(TILES):
                for k in range(2):
                    pool.indirect_dma_start(slots_x, bass.IndirectOffsetOnAxis(ap=m.slot[:, k, i:i + 1], axis=0),
                                            m.rows[:, i, :], None).then_inc(s_sc, 16)
            pool.wait_ge(s_sc, 16 * 2 * TILES)


def experts(nc, slots_x, ew1, eb1c, ew2, eb2, slots_y, m):
    E, D, HID = ew1.shape
    DC, HC = D // P, HID // P
    LT = m.list_tile
    NL = m.tile_expert.shape[1]
    RT = LT // P
    WP = 4
    HP = HC // WP
    assert NL % 2 == 0 and RT * D == 512 and RT == 2

    with ExitStack() as ctx:
        a = Steps(nc, ctx, "exp")
        ident = a.sb("ident", [P, P], F32)
        w1 = a.sb("w1", [P, 2, DC, HID], F32)
        w2 = a.sb("w2", [P, 2, HC, D], F32)
        b1 = a.sb("b1", [P, 2, HC], F32)
        b2 = a.sb("b2", [P, 2, D], F32)
        w1h = a.sb("w1h", [P, DC, HID], F32R)
        w1l = a.sb("w1l", [P, DC, HID], F32R)
        w2h = a.sb("w2h", [P, HC, D], F32R)
        w2l = a.sb("w2l", [P, HC, D], F32R)
        xs = a.sb("xs", [P, 2, RT, D], F32)
        xh = a.sb("xh", [P, 2, DC, LT], F32R)
        xl = a.sb("xl", [P, 2, DC, LT], F32R)
        h32 = a.sb("h32", [P, 4, LT], F32)
        hh = a.sb("hh", [P, HC, LT], F32R)
        hl = a.sb("hl", [P, HC, LT], F32R)
        ys = a.sb("ys", [P, 2, RT, D], F32)

        psT = a.ps("psT", [P, 512], F32)
        psU = [a.ps(f"psU{i}", [P, 512], F32) for i in range(4)]
        psD = [a.ps(f"psD{i}", [P, 512], F32) for i in range(RT)]

        s_id = a.sem("identity")
        s_x = [a.sem(f"rows_loaded{i}") for i in range(2)]
        s_w1 = [a.sem(f"w1_loaded{i}") for i in range(2)]
        s_w2 = [a.sem(f"w2_loaded{i}") for i in range(2)]
        s_tr = a.sem("rows_turned")
        s_xh, s_xl = a.sem("rows_hi"), a.sem("rows_lo")
        s_w1h, s_w1l = a.sem("w1_hi"), a.sem("w1_lo")
        s_w2h, s_w2l = a.sem("w2_hi"), a.sem("w2_lo")
        s_up = a.sem("up")
        s_rel = a.sem("relu")
        s_hh, s_hl = a.sem("hidden_hi"), a.sem("hidden_lo")
        s_dn = a.sem("down")
        s_y = a.sem("outputs")
        s_st = [a.sem(f"stored{i}") for i in range(2)]

        x_tile = slots_x.rearrange("(n r p) d -> n p r d", r=RT, p=P)
        y_tile = slots_y.rearrange("(n r p) d -> n p r d", r=RT, p=P)

        def w1_piece(t, q):
            return t[:, :, q * HP * P:(q + 1) * HP * P]

        def w2_piece(t, q):
            return t[:, q * HP:(q + 1) * HP, :]

        class Tile:

            def __init__(self, k, it, base=0):
                self.k, self.it, self.base = k, it, base
                self.j = k + 2 * base if it is None else k + 2 * base + it * 2
                self.first = it is None and base == 0

            def wait(self, eng, s, per_tile, off):
                v = per_tile * (self.k + 2 * self.base) + off
                if self.it is None:
                    if v > 0:
                        eng.wait_ge(s, v)
                else:
                    assert v + 2 * per_tile > 0
                    eng.wait_ge(s, v + self.it * (2 * per_tile))

            def wait_pair(self, eng, s, per_use, off):
                v = per_use * self.base + off
                if self.it is None:
                    if v > 0:
                        eng.wait_ge(s[self.k], v)
                else:
                    eng.wait_ge(s[self.k], v + self.it * per_use)

        def run(eng, tile, peel_last):
            for k in range(2):
                tile(Tile(k, None))
            with eng.Fori(1, NL // 2 - (1 if peel_last else 0)) as it:
                for k in range(2):
                    tile(Tile(k, it))
            if peel_last:
                for k in range(2):
                    tile(Tile(k, None, NL // 2 - 1))

        def is_last(t):
            return t.it is None and t.base > 0 and t.k == 1

        def after(t):
            if t.k == 0:
                return Tile(1, t.it, t.base)
            return Tile(0, t.it, t.base + 1)

        block = ctx.enter_context(nc.Block())

        @block.sync
        def _(sp):
            def tile(t):
                k, j = t.k, t.j
                e = sp.value_load(m.tile_expert[0:1, bass.ds(j, 1)], min_val=0, max_val=E - 1)
                t.wait(sp, s_tr, 1, -1)
                sp.dma_start(xs[:, k], x_tile[bass.ds(j, 1)].rearrange("o p r d -> p (o r) d")).then_inc(s_x[k], 16)
                t.wait(sp, s_w1l, WP, -WP)
                sp.dma_start(w1[:, k], ew1[bass.ds(e, 1)].rearrange("o (c p) h -> p (o c) h", p=P)).then_inc(s_w1[k], 16)
                t.wait(sp, s_rel, HC, -HC)
                sp.dma_start(b1[:, k, :], eb1c[bass.ds(e, 1)].rearrange("o p h -> p (o h)")).then_inc(s_w1[k], 16)
                t.wait(sp, s_w2l, WP, -WP)
                sp.dma_start(w2[:, k], ew2[bass.ds(e, 1)].rearrange("o (c p) d -> p (o c) d", p=P)).then_inc(s_w2[k], 16)
                t.wait(sp, s_y, RT, -RT)
                sp.dma_start(b2[:, k, :], eb2[bass.ds(e, 1), :].to_broadcast([P, D])).then_inc(s_w2[k], 16)

            run(sp, tile, False)

        @block.gpsimd
        def _(pool):
            pool.memset(ident[:, :], 0.0).then_inc(s_id, 1)
            pool.wait_ge(s_id, 1)
            pool.affine_select(out=ident[:, :], in_=ident[:, :], compare_op=ALU.not_equal, fill=1.0,
                               base=0, pattern=[[-1, P]], channel_multiplier=1).then_inc(s_id, 1)

            def store(k, j):
                pool.dma_start(y_tile[bass.ds(j, 1)].rearrange("o p r d -> p (o r) d"), ys[:, k]).then_inc(s_st[k], 16)

            def tile(t):
                for q in range(WP):
                    t.wait(pool, s_w2h, WP, q + 1)
                    pool.tensor_tensor(w2_piece(w2l, q), w2_piece(w2[:, t.k], q), w2_piece(w2h, q).bitcast(F32),
                                       ALU.subtract).then_inc(s_w2l, 1)
                t.wait(pool, s_y, RT, RT)
                store(t.k, t.j)

            run(pool, tile, False)
            for k in range(2):
                pool.wait_ge(s_st[k], 16 * (NL // 2))

        @block.tensor
        def _(pe):
            pe.wait_ge(s_id, 2)

            def turn(t):
                t.wait_pair(pe, s_x, 16, 16)
                t.wait(pe, s_xl, 1, 0)
                for r in range(RT):
                    for c in range(DC):
                        ins = pe.transpose(psT[:, c * LT + r * P:c * LT + (r + 1) * P], xs[:, t.k, r, c * P:(c + 1) * P], ident[:, :])
                ins.then_inc(s_tr, 1)

            def tile(t):
                k = t.k
                t.wait(pe, s_xl, 1, 1)
                for h in range(HC):
                    if h % HP == 0:
                        t.wait(pe, s_w1l, WP, h // HP + 1)
                    t.wait(pe, s_rel, HC, h - 3)
                    ps, cols = psU[h % 4][:, 0:LT], slice(h * P, (h + 1) * P)
                    for c in range(DC):
                        pe.matmul(ps, w1h[:, c, cols], xh[:, k, c, :], start=(c == 0), stop=False)
                        pe.matmul(ps, w1h[:, c, cols], xl[:, k, c, :], start=False, stop=False)
                        ins = pe.matmul(ps, w1l[:, c, cols], xh[:, k, c, :], start=False, stop=(c == DC - 1))
                    ins.then_inc(s_up, 1)
                if not is_last(t):
                    turn(after(t))
                for r in range(RT):
                    t.wait(pe, s_y, RT, r - 1)
                    for h in range(HC):
                        if r == 0:
                            t.wait(pe, s_hl, HC, h + 1)
                            if h % HP == 0:
                                t.wait(pe, s_w2l, WP, h // HP + 1)
                        ps, rows = psD[r][:, 0:D], slice(r * P, (r + 1) * P)
                        pe.matmul(ps, hh[:, h, rows], w2h[:, h, :], start=(h == 0), stop=False)
                        pe.matmul(ps, hh[:, h, rows], w2l[:, h, :], start=False, stop=False)
                        ins = pe.matmul(ps, hl[:, h, rows], w2h[:, h, :], start=False, stop=(h == HC - 1))
                    ins.then_inc(s_dn, 1)

            turn(Tile(0, None))
            run(pe, tile, True)

        @block.scalar
        def _(act):
            def rows_hi(t):
                t.wait(act, s_tr, 1, 1)
                t.wait(act, s_up, HC, -HC)
                act.activation(xh[:, t.k], psT[:, :].rearrange("p (c r) -> p c r", c=DC), ACT.Copy).then_inc(s_xh, 1)

            def w1_hi(t, q):
                if q == 0:
                    t.wait_pair(act, s_w1, 32, 32)
                t.wait(act, s_up, HC, (q + 1) * HP - HC)
                act.activation(w1_piece(w1h, q), w1_piece(w1[:, t.k], q), ACT.Copy).then_inc(s_w1h, 1)

            def w2_hi(t, q):
                if q == 0:
                    t.wait_pair(act, s_w2, 32, 32)
                    t.wait(act, s_dn, RT, 0)
                act.activation(w2_piece(w2h, q), w2_piece(w2[:, t.k], q), ACT.Copy).then_inc(s_w2h, 1)

            def relu(t, h):
                t.wait(act, s_up, HC, h + 1)
                t.wait(act, s_hl, HC, h - 3)
                act.activation(h32[:, h % 4, :], psU[h % 4][:, 0:LT], ACT.Relu, bias=b1[:, t.k, h:h + 1]).then_inc(s_rel, 1)

            def tile(t):
                for h in range(HC):
                    relu(t, h)
                    if h % 2 == 0:
                        w2_hi(t, h // 2)
                if not is_last(t):
                    rows_hi(after(t))
                    for q in range(WP):
                        w1_hi(after(t), q)

            rows_hi(Tile(0, None))
            for q in range(WP):
                w1_hi(Tile(0, None), q)
            run(act, tile, True)

        @block.vector
        def _(dve):
            def rows_lo(t):
                t.wait(dve, s_xh, 1, 1)
                dve.tensor_tensor(xl[:, t.k], psT[:, :].rearrange("p (c r) -> p c r", c=DC), xh[:, t.k].bitcast(F32),
                                  ALU.subtract).then_inc(s_xl, 1)

            def w1_lo(t, q):
                t.wait(dve, s_w1h, WP, q + 1)
                dve.tensor_tensor(w1_piece(w1l, q), w1_piece(w1[:, t.k], q), w1_piece(w1h, q).bitcast(F32),
                                  ALU.subtract).then_inc(s_w1l, 1)

            def split_hidden(t, h):
                t.wait(dve, s_rel, HC, h + 1)
                dve.tensor_copy(hh[:, h, :], h32[:, h % 4, :]).then_inc(s_hh, 1)

            def split_hidden_lo(t, h):
                t.wait(dve, s_hh, HC, h + 1)
                dve.tensor_tensor(hl[:, h, :], h32[:, h % 4, :], hh[:, h, :].bitcast(F32), ALU.subtract).then_inc(s_hl, 1)

            def output(t, r):
                if r == 0:
                    t.wait_pair(dve, s_w2, 32, 32)
                    t.wait_pair(dve, s_st, 16, 0)
                t.wait(dve, s_dn, RT, r + 1)
                dve.tensor_tensor(ys[:, t.k, r, :], psD[r][:, 0:D], b2[:, t.k, :], ALU.add).then_inc(s_y, 1)

            def tile(t):
                for h in range(HC):
                    split_hidden(t, h)
                    split_hidden_lo(t, h)
                if not is_last(t):
                    rows_lo(after(t))
                    w1_lo(after(t), 0)
                    w1_lo(after(t), 1)
                output(t, 0)
                if not is_last(t):
                    w1_lo(after(t), 2)
                    w1_lo(after(t), 3)
                output(t, 1)

            rows_lo(Tile(0, None))
            for q in range(WP):
                w1_lo(Tile(0, None), q)
            run(dve, tile, True)


def combine(nc, slots_y, out, m):
    T, D = out.shape
    TILES = T // P
    R = 4

    with ExitStack() as ctx:
        a = Steps(nc, ctx, "out")
        g = a.sb("g", [P, R, 2, D], F32)
        y = a.sb("y", [P, R, D], F32)
        o = a.sb("o", [P, R, D], F32)
        st = a.sb("st", [P, R, 6], F32)
        mv = a.sb("mv", [P, R, 2], F32)
        sd = a.sb("sd", [P, R, 2], F32)
        eps = a.sb("eps", [P, 1], F32)
        s_g = [a.sem(f"gathered{i}") for i in range(R)]
        s_eps = a.sem("eps_set")
        s_var = a.sem("variance")
        s_sd = a.sem("deviation")
        s_o = a.sem("normed")
        s_y = a.sem("summed")
        s_st = [a.sem(f"stored{i}") for i in range(R)]
        s_dve = a.sem("vector_chain")
        block = ctx.enter_context(nc.Block())

        @block.gpsimd
        def _(pool):
            for i in range(TILES):
                if i >= R:
                    pool.wait_ge(s_y, i - R + 1)
                for k in range(2):
                    pool.indirect_dma_start(g[:, i % R, k, :], None, slots_y,
                                            bass.IndirectOffsetOnAxis(ap=m.slot[:, k, i:i + 1], axis=0)).then_inc(s_g[i % R], 16)

        @block.vector
        def _(dve):
            done = [0]

            def link(ins):
                ins.then_inc(s_dve, 1)
                done[0] += 1
                dve.wait_ge(s_dve, done[0])

            dve.memset(eps[:, :], 1e-5).then_inc(s_eps, 1)
            for i in range(TILES + 1):
                if i < TILES:
                    r = i % R
                    dve.wait_ge(s_g[r], 32 * (i // R + 1))
                    link(dve.scalar_tensor_tensor(y[:, r, :], g[:, r, 0, :], m.gate[:, 0, i:i + 1], m.acc[:, i, :], ALU.mult, ALU.add))
                    dve.scalar_tensor_tensor(y[:, r, :], g[:, r, 1, :], m.gate[:, 1, i:i + 1], y[:, r, :], ALU.mult, ALU.add).then_inc(s_y, 1)
                    dve.wait_ge(s_y, i + 1)
                    link(dve.bn_stats(st[:, r, :], y[:, r, :]))
                    dve.bn_aggr(mv[:, r, :], st[:, r, :]).then_inc(s_var, 1)
                if i >= 1:
                    j = i - 1
                    r = j % R
                    dve.wait_ge(s_sd, j + 1)
                    link(dve.reciprocal(sd[:, r, 1:2], sd[:, r, 0:1]))
                    if j >= R:
                        dve.wait_ge(s_st[r], 16 * (j // R))
                    dve.tensor_scalar(o[:, r, :], y[:, r, :], mv[:, r, 0:1], sd[:, r, 1:2], ALU.subtract, ALU.mult).then_inc(s_o, 1)

        @block.scalar
        def _(act):
            act.wait_ge(s_eps, 1)
            for i in range(TILES):
                act.wait_ge(s_var, i + 1)
                act.activation(sd[:, i % R, 0:1], mv[:, i % R, 1:2], ACT.Sqrt, bias=eps[:, 0:1]).then_inc(s_sd, 1)

        @block.sync
        def _(sp):
            for i in range(TILES):
                sp.wait_ge(s_o, i + 1)
                sp.dma_start(out[i * P:(i + 1) * P, :], o[:, i % R, :]).then_inc(s_st[i % R], 16)
            for r in range(R):
                sp.wait_ge(s_st[r], 16 * (TILES // R))


class Carried:

    def __init__(self, nc, ctx, T, D, E, list_tile):
        a = Steps(nc, ctx, "all")
        n = T // P
        self.list_tile = list_tile
        lists = 2 * T // list_tile + E
        self.acc = a.sb("acc", [P, n, D], F32)
        self.rows = a.sb("rows", [P, n, D], F32)
        self.rowsT = a.sb("rowsT", [P, D // P, T], F32)
        self.logits = a.sb("logits", [P, n, E], F32)
        self.gate = a.sb("gate", [P, 2, n], F32)
        self.slot = a.sb("slot", [P, 2, n], U32)
        self.tile_expert = a.sb("tile_expert", [P, lists], I32)


def layer(nc, x, xT, Wqkv, rope_cos, rope_sin, Wo, norm_w, router_wT, sw1, sb1c, sw2, sb2,
          ew1, eb1c, ew2, eb2, tri, marks, out):
    T, D = x.shape
    E = ew1.shape[0]
    LT = 256
    slots = 2 * T + E * LT
    attn = nc.dram_tensor("attn_rows", (T, D), F32, kind="Internal").ap()
    slots_x = nc.dram_tensor("slots_x", (slots, D), F32, kind="Internal").ap()
    slots_y = nc.dram_tensor("slots_y", (slots, D), F32, kind="Internal").ap()
    attention(nc, xT, Wqkv, rope_cos, rope_sin, attn, slots_x)
    with ExitStack() as ctx:
        m = Carried(nc, ctx, T, D, E, LT)
        norm_and_route(nc, x, attn, Wo, norm_w, router_wT, m)
        shared_and_dispatch(nc, sw1, sb1c, sw2, sb2, tri, marks, slots_x, m)
        experts(nc, slots_x, ew1, eb1c, ew2, eb2, slots_y, m)
        combine(nc, slots_y, out, m)


def kernel(L0_attn_x, L0_attn_Wqkv, L0_attn_Wo, L0_ffn_norm_weight, L0_ffn_router_w, L0_ffn_sw1, L0_ffn_sb1,
           L0_ffn_sw2, L0_ffn_sb2, L0_ffn_ew1, L0_ffn_eb1, L0_ffn_ew2, L0_ffn_eb2):
    import concourse.bacc as bacc
    from concourse.bass_utils import run_bass_kernel_spmd

    x = np.asarray(L0_attn_x)
    B, L, D = x.shape
    T = B * L
    x2 = np.ascontiguousarray(x.reshape(T, D))
    E, _, HID = L0_ffn_ew1.shape
    DH, LT = 16, 256
    inv = (1.0 / np.float32(10000.0) ** (np.arange(0, DH, 2, dtype=np.float32) / np.float32(DH))).astype(np.float32)
    angles = np.outer(np.arange(L, dtype=np.float32), inv).astype(np.float32)
    angles = np.concatenate([angles, angles], -1)
    signs = np.where(np.arange(DH) < DH // 2, -1.0, 1.0).astype(np.float32)

    def by_tile(t):
        return np.ascontiguousarray(t.astype(np.float32).reshape(L // P, P, DH).transpose(1, 0, 2))

    tri = np.triu(np.ones((P, P), np.float32), 1)
    lists = 2 * T // LT + E
    marks = np.concatenate([
        np.arange(E, 0, -1), LT * np.arange(T // LT), np.arange(lists), np.arange(T // P) > 0,
    ]).astype(np.float32)
    marks = np.ascontiguousarray(np.broadcast_to(marks, (P, marks.size)))
    arrays = {
        "x": x2,
        "xT": np.ascontiguousarray(x2.T),
        "Wqkv": np.asarray(L0_attn_Wqkv),
        "rope_cos": by_tile(np.cos(angles)),
        "rope_sin": by_tile(np.sin(angles) * signs),
        "Wo": np.asarray(L0_attn_Wo),
        "norm_w": np.asarray(L0_ffn_norm_weight),
        "router_wT": np.ascontiguousarray(np.asarray(L0_ffn_router_w).T),
        "sw1": np.asarray(L0_ffn_sw1),
        "sb1c": np.ascontiguousarray(np.asarray(L0_ffn_sb1).reshape(HID // P, P).T),
        "sw2": np.asarray(L0_ffn_sw2),
        "sb2": np.asarray(L0_ffn_sb2),
        "ew1": np.asarray(L0_ffn_ew1),
        "eb1c": np.ascontiguousarray(np.asarray(L0_ffn_eb1).reshape(E, HID // P, P).transpose(0, 2, 1)),
        "ew2": np.asarray(L0_ffn_ew2),
        "eb2": np.asarray(L0_ffn_eb2),
        "tri": tri,
        "marks": marks,
    }
    nc = bacc.Bacc("TRN2", target_bir_lowering=False, num_devices=1)
    args = [nc.dram_tensor(n, v.shape, mybir.dt.from_np(v.dtype), kind="ExternalInput").ap() for n, v in arrays.items()]
    out = nc.dram_tensor("out", (T, D), F32, kind="ExternalOutput").ap()
    layer(nc, *args, out)
    r = run_bass_kernel_spmd(nc, [arrays], core_ids=[0])
    return r.results[0]["out"].reshape(B, L, D)
```

```python
from contextlib import ExitStack

import concourse.bass as bass
from concourse import mybir
import numpy as np

F32 = mybir.dt.float32
F32R = mybir.dt.float32r
BF16 = mybir.dt.bfloat16
U32 = mybir.dt.uint32
I32 = mybir.dt.int32
ALU = mybir.AluOpType
ACT = mybir.ActivationFunctionType
AX_X = mybir.AxisListType.X
P = 128


class Steps:

    def __init__(self, nc, ctx, tag):
        self.nc, self.ctx, self.tag = nc, ctx, tag

    def sb(self, name, shape, dt):
        return self.ctx.enter_context(self.nc.sbuf_tensor(f"{self.tag}_{name}", shape, dt))

    def ps(self, name, shape, dt):
        return self.ctx.enter_context(self.nc.psum_tensor(f"{self.tag}_{name}", shape, dt))

    def sem(self, name):
        return self.ctx.enter_context(self.nc.semaphore(f"{self.tag}_{name}"))


def attention(nc, xT, Wqkv, rope_cos, rope_sin, attn_out, slots_x, norm):
    D, T = xT.shape
    DH, L = rope_cos.shape[2], P * rope_cos.shape[1]
    H = D // DH
    B = T // L
    NT = L // P
    DC = D // P
    G = 4
    HG = H // G
    U = G * NT
    NG = B * HG
    TERMS = 6
    KR = TERMS * DH
    SCALE = float(DH) ** -0.5
    A_LEAD = U + 4
    BODY = 2 * HG
    FIRST = 1
    PASSES = (NG - FIRST - 1) // BODY
    HEAD, TAIL = FIRST, FIRST + PASSES * BODY
    QK_LEAD, V_LEAD = 6, 4
    T_LEAD = A_LEAD + 8
    PROJECT_QK, ROPE, COPY_OUT, TURN_OUT, NORM_OUT = (1, 2), (2, 3, 4), 4, 8, (8, 9)
    PROJECT_V, COPY_V, SPLIT_MAX, TURN_MAX, COPY_MAX = 12, 12, 12, (13, 15), (14, U)
    PIECE_1, PIECE_2, SPREAD, SPLIT_X = 7, 13, 0, 14
    ADD_PV = 2
    RING = 4
    PR = 8
    assert NT == HG and NG % BODY == 0 and U == 16

    Q_PIECES, K_PIECES = (1, 1, 1, 2, 2, 3), (1, 2, 3, 1, 2, 1)
    assert len(Q_PIECES) == len(K_PIECES) == TERMS

    with ExitStack() as ctx:
        a = Steps(nc, ctx, "att")
        w = a.sb("w", [P, DC, 3 * D], F32)
        cos = a.sb("cos", [P, NT, DH], F32)
        sin = a.sb("sin", [P, NT, DH], F32)
        xt = a.sb("xt", [P, 2, DC, L], F32)
        wh = a.sb("wh", [P, DC, 3 * D], F32R)
        wl = a.sb("wl", [P, DC, 3 * D], F32R)
        xh = a.sb("xh", [P, 2, DC, L], F32R)
        xl = a.sb("xl", [P, 2, DC, L], F32R)
        zero = norm.acc[:, 0:8, :].rearrange("p t d -> p (t d)")
        ident = a.sb("ident", [P, P], BF16)
        identf = a.sb("identf", [P, P], F32)
        stack = a.sb("stack", [P, 2, NT, 2, H, KR], BF16)
        qk = a.sb("qk", [P, RING, G, 2, L], BF16)
        V = a.sb("V", [P, 2, NT, H, 32], F32)
        prob = a.sb("prob", [P, PR, L], F32)
        mx = a.sb("mx", [P, 2, U], F32)
        mrest = a.sb("mrest", [P, U], F32)
        mstk = a.sb("mstk", [P, U, 32], BF16)
        rc = a.sb("rc", [P, 2 * D], F32)
        rs = a.sb("rs", [P, 2 * D], F32)
        rr = a.sb("rr", [P, 2 * D], F32)
        r1 = a.sb("r1", [P, 2 * D], F32)
        oT = a.sb("oT", [P, L], F32)
        rden = a.sb("rden", [P, U], F32)
        ob = a.sb("ob", [P, 2, NT, D], F32)

        psA = [a.ps(f"psA{i}", [P, L], F32) for i in range(3)]
        A_BANK = [0, 1, 2] * 5 + [1]
        psB = [a.ps(f"psB{i}", [P, L], F32) for i in range(2)]
        psV = a.ps("psV", [P, L], F32)
        psT = a.ps("psT", [P, 2, L], BF16)
        psX = a.ps("psX", [P, 512], F32)
        psXt = psX[:, :].bitcast(BF16)

        s_w = a.sem("w_loaded")
        s_tab = a.sem("tables_loaded")
        s_x = [a.sem(f"x_loaded{i}") for i in range(2)]
        s_wh, s_wl = a.sem("w_hi"), a.sem("w_lo")
        s_xh, s_xl = a.sem("x_hi"), a.sem("x_lo")
        s_const = a.sem("constants")
        s_init = a.sem("init")
        s_zero = a.sem("slots_zeroed")
        s_amm = a.sem("score_rows")
        s_max = a.sem("row_max")
        s_bmm = a.sem("score_cols")
        s_exp = a.sem("probs")
        s_pv = a.sem("pv")
        s_oev = a.sem("o_copied")
        s_otr = a.sem("o_turned")
        s_onrm = a.sem("o_normed")
        s_ost = [a.sem(f"o_stored{i}") for i in range(2)]
        s_tmm = a.sem("head_turned")
        s_tev = a.sem("head_ready")
        s_msp = a.sem("max_split")
        s_mtr = a.sem("max_turned")
        s_mev = a.sem("max_ready")
        s_qmm = a.sem("qk_projected")
        s_qrd = a.sem("qk_read")
        s_rr = a.sem("qk_turned")
        s_p1 = a.sem("piece_1")
        s_r1 = a.sem("rest_1")
        s_p2 = a.sem("piece_2")
        s_p3 = a.sem("piece_3_q")
        s_qsp = a.sem("qk_split")
        s_stk = a.sem("stacked")
        s_vmm = a.sem("v_projected")
        s_vev = a.sem("v_ready")
        s_dve = a.sem("vector_chain")

        def at(it, v, per_group):
            return v if it is None else v + it * (per_group * BODY)

        def wait(eng, it, s, v, per_group):
            if it is None and v <= 0:
                return
            assert v > 0, (v, s)
            eng.wait_ge(s, at(it, v, per_group))

        def groups(eng, period, after_loop=None):
            for p in range(-QK_LEAD, HEAD):
                period(p, None)
            with eng.Fori(0, PASSES) as it:
                for p in range(HEAD, HEAD + BODY):
                    period(p, it)
            if after_loop is not None:
                after_loop()
            for p in range(TAIL, NG + 1):
                period(p, None)

        def valid(i, n):
            return 0 <= i < n

        def heads_of(t):
            return t[:, :].rearrange("p (h d) -> p h d", d=DH)

        def terms(stack, b, t):
            return stack[:, b % 2, t].rearrange("p i h (m d) -> p (i h) m d", d=DH)

        block = ctx.enter_context(nc.Block())

        @block.sync
        def _(sp):
            x_seq = xT.rearrange("(c p) (b l) -> b p c l", p=P, l=L)
            out_seq = attn_out.rearrange("(b t p) d -> b p t d", t=NT, p=P)
            sp.dma_start(w[:, :, :], Wqkv.rearrange("(c p) n -> p c n", p=P)).then_inc(s_w, 16)
            sp.dma_start(xt[:, 0, :, :], x_seq[0]).then_inc(s_x[0], 16)
            sp.dma_start(cos[:, :, :], rope_cos).then_inc(s_tab, 16)
            sp.dma_start(sin[:, :, :], rope_sin).then_inc(s_tab, 16)
            sp.dma_start(xt[:, 1, :, :], x_seq[1]).then_inc(s_x[1], 16)
            sp.wait_ge(s_init, 5)
            slots = slots_x.rearrange("(p r) d -> p (r d)", p=P)
            zeroed = 0
            for c in range(0, slots.shape[1], zero.shape[1]):
                n = min(zero.shape[1], slots.shape[1] - c)
                sp.dma_start(slots[:, c:c + n], zero[:, 0:n]).then_inc(s_zero, 16)
                zeroed += 16
            with sp.Fori(0, B // 2 - 1) as i:
                for k in range(2):
                    sp.wait_ge(s_xl, k + 1 + i * 2)
                    sp.dma_start(xt[:, k, :, :], x_seq[bass.ds(2 + k + i * 2, 1)].rearrange("o p c l -> p (o c) l")).then_inc(s_x[k], 16)
                    sp.wait_ge(s_onrm, HG * (k + 1) + i * (2 * HG))
                    sp.dma_start(out_seq[bass.ds(k + i * 2, 1)].rearrange("o p t d -> p (o t) d"), ob[:, k, :, :]).then_inc(s_ost[k], 16)
            for k in range(2):
                sp.wait_ge(s_onrm, HG * (B - 1 + k))
                sp.dma_start(out_seq[B - 2 + k], ob[:, k, :, :]).then_inc(s_ost[k], 16)
                if k == 0:
                    sp.wait_ge(s_zero, zeroed)
                    sp.wait_ge(s_const, 2)
                    for b in range(B - 1):
                        if b >= B - 3:
                            sp.wait_ge(s_ost[b % 2], 16 * (b // 2 + 1))
                        norm.load_attention(sp, attn_out, b)
            for k in range(2):
                sp.wait_ge(s_ost[k], 16 * (B // 2))

        @block.gpsimd
        def _(pool):
            for k, step in enumerate((
                lambda: pool.memset(ident[:, :], 0.0),
                lambda: pool.affine_select(out=ident[:, :], in_=ident[:, :], compare_op=ALU.not_equal, fill=1.0,
                                           base=0, pattern=[[-1, P]], channel_multiplier=1),
                lambda: pool.memset(identf[:, :], 0.0),
                lambda: pool.affine_select(out=identf[:, :], in_=identf[:, :], compare_op=ALU.not_equal, fill=1.0,
                                           base=0, pattern=[[-1, P]], channel_multiplier=1),
                lambda: pool.memset(zero, 0.0),
                lambda: pool.memset(V[:, :, :, :, DH + 1:], 0.0),
                lambda: pool.memset(V[:, :, :, :, DH:DH + 1], 1.0),
                lambda: pool.memset(mstk[:, :, :], 0.0),
            )):
                step().then_inc(s_init, 1)
                pool.wait_ge(s_init, k + 1)
            def x_lo(b, it):
                v = b + 1
                pool.wait_ge(s_xh, v if it is None else v + it * 2)
                pool.tensor_tensor(xl[:, b % 2], xt[:, b % 2], xh[:, b % 2].bitcast(F32), ALU.subtract).then_inc(s_xl, 1)

            def period(p, it):
                tile = p + QK_LEAD
                if not valid(tile, NT * B):
                    return
                b, t = tile // NT, tile % NT
                st = terms(stack, b, t)
                wait(pool, it, s_qrd, tile + 1, 1)
                pool.tensor_tensor(rr[:, :], rc[:, :], rs[:, :], ALU.add).then_inc(s_rr, 1)
                wait(pool, it, s_p1, tile + 1, 1)
                pool.tensor_tensor(heads_of(r1), heads_of(rr), st[:, :, 0, :], ALU.subtract).then_inc(s_r1, 1)
                wait(pool, it, s_p2, tile + 1, 1)
                pool.tensor_tensor(st[:, 0:H, 5, :], heads_of(r1)[:, 0:H], st[:, 0:H, 4, :], ALU.subtract).then_inc(s_p3, 1)
                wait(pool, it, s_p3, tile + 1, 1)
                pool.tensor_tensor(st[:, H:, 2, :], heads_of(r1)[:, H:], st[:, H:, 4, :], ALU.subtract).then_inc(s_qsp, 1)
                if t == NT - 1 and valid(tile + 1, NT * B):
                    x_lo(b + 1, it)

            groups(pool, period)

        @block.tensor
        def _(pe):
            pe.wait_ge(s_wl, 1)

            def score_rows(n, it):
                g, h, qt = n // U, n // NT, n % NT
                if qt == 0:
                    wait(pe, it, s_tev, h + 1, G)
                back = next(d for d in range(1, U) if A_BANK[(n - d) % U] == A_BANK[n % U])
                wait(pe, it, s_max, n - back + 1, U)
                r = qk[0:KR, g % RING, h % G]
                pe.matmul(psA[A_BANK[n % U]][:, :], r[:, 0, qt * P:(qt + 1) * P], r[:, 1, :], start=True, stop=True).then_inc(s_amm, 1)

            def score_cols(n, it):
                g, u = n // U, n % U
                kt, j = u // G, u % G
                if u % 2 == 0 and u < G:
                    wait(pe, it, s_mev, 2 * g + 1 + u // 2, 2)
                wait(pe, it, s_exp, n - 1, U)
                r = qk[:, g % RING, j]
                pe.matmul(psB[n % 2][:, :], r[:, 1, kt * P:(kt + 1) * P], r[:, 0, :], start=True, stop=True).then_inc(s_bmm, 1)

            def turn_head(h, half, it):
                g, b = h // G, h // H
                if half == 0:
                    wait(pe, it, s_tev, h, G)
                    if h % H == 0:
                        wait(pe, it, s_stk, NT * (b + 1), 1)
                    if it is None and h == 0:
                        pe.wait_ge(s_init, 8)
                        pe.wait_ge(s_const, 2)
                for t in range(NT):
                    m = pe.transpose(psT[0:KR, half, t * P:(t + 1) * P], stack[:, b % 2, t, half, h % H, :], ident[:, :])
                if half == 1:
                    m.then_inc(s_tmm, 1)

            QK, OUT, VALUE, MAX0, MAX1 = range(5)

            def take_psX(p, use, it):
                if it is not None:
                    last = {QK: (s_mev, 2 * p + 2, 2), OUT: (s_qrd, p + QK_LEAD + 1, 1), VALUE: (s_onrm, p, 1),
                            MAX0: (s_vev, p + V_LEAD + 1, 1), MAX1: (s_mev, 2 * p + 3, 2)}[use]
                    wait(pe, it, *last)
                    return
                for s, n, most in ((s_qrd, p + QK_LEAD + (use > QK), NG), (s_onrm, p - 1 + (use > OUT), NG),
                                   (s_vev, p + V_LEAD + (use > VALUE), NG), (s_mev, 2 * p + 2 + (use > MAX0), 2 * NG)):
                    wait(pe, it, s, min(n, most), 1)

            def turn_max(g, half, it):
                take_psX(g - 1, (MAX0, MAX1)[half], it)
                if half == 0:
                    wait(pe, it, s_msp, g + 1, 1)
                for k in range(U // 2):
                    m = pe.transpose(psXt[96:128, k * P:(k + 1) * P], mstk[:, half * (U // 2) + k, :], ident[:, :])
                m.then_inc(s_mtr, 1)

            def add_pv(g, kt, it):
                b, hg = g // HG, g % HG
                if kt == 0:
                    wait(pe, it, s_oev, g, 1)
                    if hg == 0:
                        wait(pe, it, s_vev, NT * (b + 1), 1)
                n = g * U + kt * G
                wait(pe, it, s_exp, n + G, U)
                for j in range(G):
                    m = pe.matmul(psV[32 * j:32 * j + 32, :], V[:, b % 2, kt, hg * G + j, :], prob[:, (n + j) % PR, :],
                                  start=(kt == 0), stop=(kt == NT - 1))
                m.then_inc(s_pv, 1)

            def turn_out(g, it):
                take_psX(g + 1, OUT, it)
                wait(pe, it, s_oev, g + 1, 1)
                for qt in range(NT):
                    m = pe.transpose(psX[:, qt * P:(qt + 1) * P], oT[:, qt * P:(qt + 1) * P], identf[:, :])
                m.then_inc(s_otr, 1)

            def project(tile, c, it, value):
                b, t = tile // NT, tile % NT
                if c == 0:
                    take_psX(tile - (V_LEAD if value else QK_LEAD), VALUE if value else QK, it)
                    if t == 0 and not value:
                        pe.wait_ge(s_xl, b + 1 if it is None else b + 1 + it * 2)
                o, cols = (psX[:, 0:D], slice(2 * D, 3 * D)) if value else (psX[:, :], slice(0, 2 * D))
                rows = slice(t * P, (t + 1) * P)
                pe.matmul(o, xh[:, b % 2, c, rows], wh[:, c, cols], start=(c == 0), stop=False)
                pe.matmul(o, xh[:, b % 2, c, rows], wl[:, c, cols], start=False, stop=False)
                m = pe.matmul(o, xl[:, b % 2, c, rows], wh[:, c, cols], start=False, stop=(c == DC - 1))
                if c == DC - 1:
                    m.then_inc(s_vmm if value else s_qmm, 1)

            def period(p, it):
                for u in range(U):
                    n = p * U + u
                    if valid(n, NG * U):
                        score_cols(n, it)
                    if valid(n + A_LEAD, NG * U):
                        score_rows(n + A_LEAD, it)
                    k = n + T_LEAD
                    if valid(k // 4, NG * G) and k % 4 < 2:
                        turn_head(k // 4, k % 4, it)
                    if u % G == ADD_PV and valid(n - ADD_PV - G, NG * U):
                        add_pv((n - ADD_PV - G) // U, ((n - ADD_PV - G) % U) // G, it)
                    if u in TURN_MAX and valid(p + 1, NG):
                        turn_max(p + 1, TURN_MAX.index(u), it)
                    if u == TURN_OUT and valid(p - 1, NG):
                        turn_out(p - 1, it)
                    if u in PROJECT_QK and valid(p + QK_LEAD, NT * B):
                        project(p + QK_LEAD, PROJECT_QK.index(u), it, False)
                    if u == PROJECT_V and valid(p + V_LEAD, NT * B):
                        for c in range(DC):
                            project(p + V_LEAD, c, it, True)

            groups(pe, period)

        @block.scalar
        def _(act):
            def exps(n, it):
                wait(act, it, s_bmm, n + 1, U)
                if n % G == 0:
                    wait(act, it, s_pv, n // G + 1 - PR // G, NT)
                act.activation(prob[:, n % PR, :], psB[n % 2][:, :], ACT.Exp, scale=SCALE).then_inc(s_exp, 1)

            def copy_head(h, it):
                g = h // G
                wait(act, it, s_tmm, h + 1, G)
                act.activation(qk[0:KR, g % RING, h % G, :, :], psT[0:KR, :, :], ACT.Copy).then_inc(s_tev, 1)

            def copy_out(g, it):
                wait(act, it, s_pv, NT * (g + 1), NT)
                act.activation(oT[:, :], psV[:, :], ACT.Copy).then_inc(s_oev, 1)

            def copy_v(tile, it):
                b, t = tile // NT, tile % NT
                wait(act, it, s_vmm, tile + 1, 1)
                if t == 0:
                    wait(act, it, s_pv, NT * HG * (b - 1), NT)
                act.activation(V[:, b % 2, t, :, 0:DH], psX[:, 0:D].rearrange("p (h d) -> p h d", d=DH), ACT.Copy).then_inc(s_vev, 1)

            def spread(tile, it):
                b, t = tile // NT, tile % NT
                q, k = (stack[:, b % 2, t, i].rearrange("p h (m d) -> p h m d", d=DH) for i in range(2))
                wait(act, it, s_qsp, tile + 1, 1)
                act.activation(q[:, :, 1:3, :], q[:, :, 0:1, :].to_broadcast([P, H, 2, DH]), ACT.Copy)
                act.activation(k[:, :, 3:6:2, :], k[:, :, 0:1, :].to_broadcast([P, H, 2, DH]), ACT.Copy)
                act.activation(q[:, :, 3, :], q[:, :, 4, :], ACT.Copy)
                act.activation(k[:, :, 1, :], k[:, :, 4, :], ACT.Copy).then_inc(s_stk, 1)

            def x_hi(b, it):
                v = 16 * (b // 2 + 1)
                act.wait_ge(s_x[b % 2], v if it is None else v + it * 16)
                wait(act, it, s_vmm, NT * (b - 1), 1)
                act.activation(xh[:, b % 2], xt[:, b % 2], ACT.Copy).then_inc(s_xh, 1)

            act.wait_ge(s_w, 16)
            act.activation(wh[:, :, :], w[:, :, :], ACT.Copy).then_inc(s_wh, 1)
            x_hi(0, None)
            act.wait_ge(s_init, 5)
            act.wait_ge(s_const, 1)
            act.activation(qk[96:99, :, :, 1, :], zero[96:99, 0:L].unsqueeze(1).unsqueeze(1).to_broadcast([3, RING, G, L]),
                           ACT.Copy, bias=1.0).then_inc(s_const, 1)

            def period(p, it):
                for u in range(U):
                    n = p * U + u
                    if u == SPLIT_X and (p + QK_LEAD + 1) % NT == 0 and valid(p + QK_LEAD + 1, NT * B):
                        x_hi((p + QK_LEAD + 1) // NT, it)
                    if valid(n, NG * U):
                        exps(n, it)
                    k = n + T_LEAD
                    if valid(k // 4, NG * G) and k % 4 == 2:
                        copy_head(k // 4, it)
                    if u == COPY_OUT and valid(p - 1, NG):
                        copy_out(p - 1, it)
                    if u == COPY_V and valid(p + V_LEAD, NT * B):
                        copy_v(p + V_LEAD, it)
                    if u == SPREAD and valid(p + QK_LEAD - 1, NT * B):
                        spread(p + QK_LEAD - 1, it)

            groups(act, period)

        @block.vector
        def _(dve):
            LINKS = 4
            done = [0]

            def link(ins):
                ins.then_inc(s_dve, 1)
                done[0] += 1

            def linked(it, back=0):
                wait(dve, it, s_dve, done[0] - back, LINKS)

            def row_max(n, it):
                wait(dve, it, s_amm, n + 1, U)
                g, h, qt = n // U, n // NT, n % NT
                dve.reduce_max(mx[:, g % 2, n % U:n % U + 1], psA[A_BANK[n % U]][:, :], AX_X).then_inc(s_max, 1)

            def split_max(g, k, it):
                m = mx[:, g % 2, :]
                if k == 0:
                    wait(dve, it, s_max, U * (g + 1), U)
                    wait(dve, it, s_mtr, 2 * g, 2)
                    link(dve.tensor_scalar(mstk[:, :, 0], m, -1.0, None, ALU.mult))
                elif k == 1:
                    linked(it)
                    link(dve.scalar_tensor_tensor(mrest[:, :], m, -1.0, mstk[:, :, 0], ALU.mult, ALU.subtract))
                elif k == 2:
                    linked(it)
                    link(dve.tensor_copy(mstk[:, :, 1], mrest[:, :]))
                else:
                    linked(it)
                    dve.tensor_tensor(mstk[:, :, 2], mrest[:, :], mstk[:, :, 1], ALU.subtract).then_inc(s_msp, 1)

            def copy_max(g, half, it):
                wait(dve, it, s_mtr, 2 * g + half + 1, 2)
                dve.tensor_copy(qk[96:128, g % RING, 2 * half:2 * half + 2, 0, :],
                                psXt[96:128, :].rearrange("p (j l) -> p j l", l=L)).then_inc(s_mev, 1)

            def norm_out(g, k, it):
                b, hg = g // HG, g % HG
                o = psX[:, :].rearrange("p (n c) -> p n c", c=32)
                if k == 0:
                    wait(dve, it, s_otr, g + 1, 1)
                    link(dve.reciprocal(rden[:, :], o[:, :, DH]))
                else:
                    linked(it)
                    if hg == 0:
                        v = 16 * (b // 2)
                        if it is not None:
                            dve.wait_ge(s_ost[b % 2], v + it * 16)
                        elif v > 0:
                            dve.wait_ge(s_ost[b % 2], v)
                    dve.tensor_tensor(ob[:, b % 2, :, hg * G * DH:(hg + 1) * G * DH].rearrange("p t (j d) -> p t j d", d=DH),
                                      o[:, :, 0:DH].rearrange("p (t j) d -> p t j d", j=G),
                                      rden[:, :].rearrange("p (t j) -> p t j", j=G).unsqueeze(3).to_broadcast([P, NT, G, DH]),
                                      ALU.mult).then_inc(s_onrm, 1)

            def rope(tile, k, it):
                b, t = tile // NT, tile % NT
                x, half = heads_of(psX), DH // 2

                def table(tb, c0, c1):
                    return tb[:, t, c0:c1].unsqueeze(1).to_broadcast([P, 2 * H, c1 - c0])

                if k == 0:
                    wait(dve, it, s_qmm, tile + 1, 1)
                    wait(dve, it, s_rr, tile, 1)
                    dve.tensor_tensor(heads_of(rc), x, table(cos, 0, DH), ALU.mult)
                elif k == 1:
                    dve.tensor_tensor(heads_of(rs)[:, :, 0:half], x[:, :, half:], table(sin, 0, half), ALU.mult)
                else:
                    dve.tensor_tensor(heads_of(rs)[:, :, half:], x[:, :, 0:half], table(sin, half, DH), ALU.mult).then_inc(s_qrd, 1)

            def piece_1(tile, it):
                b, t = tile // NT, tile % NT
                wait(dve, it, s_rr, tile + 1, 1)
                if t == 0:
                    wait(dve, it, s_tmm, H * (b - 1), G)
                dve.tensor_copy(terms(stack, b, t)[:, :, 0, :], heads_of(rr)).then_inc(s_p1, 1)

            def piece_2(tile, it):
                b, t = tile // NT, tile % NT
                wait(dve, it, s_r1, tile + 1, 1)
                dve.tensor_copy(terms(stack, b, t)[:, :, 4, :], heads_of(r1)).then_inc(s_p2, 1)

            dve.memset(qk[96:128, :, :, 1, :], 0.0).then_inc(s_const, 1)
            dve.wait_ge(s_wh, 1)
            dve.tensor_tensor(wl[:, :, :], w[:, :, :], wh[:, :, :].bitcast(F32), ALU.subtract).then_inc(s_wl, 1)
            dve.wait_ge(s_xh, 1)
            dve.tensor_tensor(xl[:, 0], xt[:, 0], xh[:, 0].bitcast(F32), ALU.subtract).then_inc(s_xl, 1)
            dve.wait_ge(s_init, 8)
            dve.wait_ge(s_tab, 32)

            def period(p, it):
                for u in range(U):
                    n = p * U + u
                    if u == COPY_MAX[1] % U and valid(p, NG):
                        copy_max(p, 1, it)
                    if u == COPY_MAX[0] and valid(p + 1, NG):
                        copy_max(p + 1, 0, it)
                    if valid(n + A_LEAD, NG * U):
                        row_max(n + A_LEAD, it)
                    if u in ROPE and valid(p + QK_LEAD, NT * B):
                        rope(p + QK_LEAD, ROPE.index(u), it)
                    if u == PIECE_1 and valid(p + QK_LEAD, NT * B):
                        piece_1(p + QK_LEAD, it)
                    if u == PIECE_2 and valid(p + QK_LEAD, NT * B):
                        piece_2(p + QK_LEAD, it)
                    if u in NORM_OUT and valid(p - 1, NG):
                        norm_out(p - 1, NORM_OUT.index(u), it)
                    if u == SPLIT_MAX and valid(p + 1, NG):
                        for k in range(4):
                            split_max(p + 1, k, it)

            def after_loop():
                done[0] += LINKS * BODY * (PASSES - 1)

            groups(dve, period, after_loop)


EARLY_BLOCKS = 10


class NormInputs:

    def __init__(self, nc, ctx, T, L, D):
        a = Steps(nc, ctx, "pre")
        self.acc = a.sb("acc", [P, T // P, D], F32)
        self.s_at = [a.sem(f"attention_loaded{b}") for b in range(T // L)]
        self.NT = L // P

    def load_attention(self, sp, attn, b):
        src = attn.rearrange("(b t p) d -> b p t d", t=self.NT, p=P)
        sp.dma_start(self.acc[:, b * self.NT:(b + 1) * self.NT, :], src[b]).then_inc(self.s_at[b], 16)


def norm_and_route(nc, x, attn, Wo, norm_w, router_wT, sw1, sb1c, sw2, sb2, rows, given, m):
    T, D = attn.shape
    DC, NT = D // P, given.NT
    E = router_wT.shape[1]
    NB = T // (NT * P)
    TILES = NB * NT
    SWP = DC * sw1.shape[1] // 512
    SPLIT_FROM = 6

    with ExitStack() as ctx:
        a = Steps(nc, ctx, "nrm")
        ident = a.sb("ident", [P, P], F32)
        eps = a.sb("eps", [P, 2], F32)
        wo = a.sb("wo", [P, DC, D], F32)
        rw = a.sb("rw", [P, DC, E], F32)
        nw = a.sb("nw", [P, D], F32)
        xr = a.sb("xr", [P, 2, NT, D], F32)
        aT = a.sb("aT", [P, 2, D], F32)
        y = a.sb("y", [P, 4, D], F32)
        st = a.sb("st", [P, 4, 6], F32)
        mv = a.sb("mv", [P, 4, 2], F32)
        sd = a.sb("sd", [P, 4, 4], F32)
        ms = a.sb("ms", [P, 4, 1], F32)

        sw = [a.sb(f"sw{i}", [P, SWP, 512], F32) for i in range(2)]

        psT = [a.ps(f"psT{i}", [P, 512], F32) for i in range(2)]
        psP = [a.ps(f"psP{i}", [P, 512], F32) for i in range(2)]
        psN = [a.ps(f"psN{i}", [P, 512], F32) for i in range(2)]
        psL = [a.ps(f"psL{i}", [P, 512], F32) for i in range(2)]

        s_wo, s_w = a.sem("projection_weights"), a.sem("weights")
        s_sw = a.sem("shared_weights")
        s_swh, s_swl = a.sem("shared_hi"), a.sem("shared_lo")
        s_xr = [a.sem(f"residual_loaded{i}") for i in range(2)]
        s_id = a.sem("identity")
        s_ttr = a.sem("attn_turned")
        s_tcp = a.sem("attn_copied")
        s_prj = a.sem("projected")
        s_y = a.sem("residual_added")
        s_var = a.sem("variance")
        s_sd = a.sem("deviation")
        s_x1 = a.sem("x1")
        s_ms = a.sem("mean_square")
        s_rms = a.sem("root_mean_square")
        s_irms = a.sem("inverse_root")
        s_xw = a.sem("x1_weighted")
        s_row = a.sem("normed")
        s_ntr = a.sem("normed_turned")
        s_ncp = a.sem("normed_copied")
        s_log = a.sem("logits")
        s_lcp = a.sem("logits_copied")
        s_dve = a.sem("vector_chain")

        block = ctx.enter_context(nc.Block())

        @block.sync
        def _(sp):
            x_blk = x.rearrange("(b t p) d -> b p t d", t=NT, p=P)
            sp.dma_start(wo[:, :, :], Wo.rearrange("(c p) n -> p c n", p=P)).then_inc(s_wo, 16)
            sp.dma_start(xr[:, 0], x_blk[0]).then_inc(s_xr[0], 16)
            sp.dma_start(rw[:, :, :], router_wT.rearrange("(c p) e -> p c e", p=P)).then_inc(s_w, 16)
            sp.dma_start(nw[:, :], norm_w.partition_broadcast(P)).then_inc(s_w, 16)
            given.load_attention(sp, attn, NB - 1)
            for b in range(NB):
                if b >= 2:
                    sp.wait_ge(s_y, NT * (b - 1))
                if b >= 1:
                    sp.dma_start(xr[:, b % 2], x_blk[b]).then_inc(s_xr[b % 2], 16)
                if b == 1:
                    for w, src in ((sw[0], sw1), (sw[1], sw2)):
                        n = src.shape[1]
                        sp.dma_start(w[:, :, :].rearrange("p a b -> p (a b)").rearrange("p (c n) -> p c n", n=n),
                                     src.rearrange("(c p) n -> p c n", p=P)).then_inc(s_sw, 16)
                    sp.dma_start(m.sb1[:, :], sb1c).then_inc(s_sw, 16)
                    sp.dma_start(m.sb2[:, :], sb2.partition_broadcast(P)).then_inc(s_sw, 16)

        @block.gpsimd
        def _(pool):
            for k, step in enumerate((
                lambda: pool.memset(ident[:, :], 0.0),
                lambda: pool.affine_select(out=ident[:, :], in_=ident[:, :], compare_op=ALU.not_equal, fill=1.0,
                                           base=0, pattern=[[-1, P]], channel_multiplier=1),
                lambda: pool.memset(eps[:, 0:1], 1e-5),
                lambda: pool.memset(eps[:, 1:2], 1e-8),
            )):
                step().then_inc(s_id, 1)
                pool.wait_ge(s_id, k + 1)
            pool.wait_ge(s_w, 32)
            pool.wait_ge(s_sw, 64)
            for i in range(TILES):
                pool.wait_ge(s_x1, i + 1)
                pool.tensor_tensor(rows[:, i, :], m.acc[:, i, :], nw[:, :], ALU.mult).then_inc(s_xw, 1)
                if SPLIT_FROM - 5 <= i < SPLIT_FROM - 5 + 4 * SWP and (i - SPLIT_FROM + 5) % 2 == 0:
                    q = (i - SPLIT_FROM + 5) // 2
                    pool.wait_ge(s_swh, q + 1)
                    pool.tensor_tensor(m.sw_lo[q // SWP][:, q % SWP, :], sw[q // SWP][:, q % SWP, :],
                                       m.sw_hi[q // SWP][:, q % SWP, :].bitcast(F32), ALU.subtract).then_inc(s_swl, 1)
            pool.wait_ge(s_xw, TILES)
            pool.wait_ge(s_swl, 2 * SWP)

        SLOTS = TILES + 8

        def stages(slot, lags):
            return [slot - lag if 0 <= slot - lag < TILES else None for lag in lags]

        @block.tensor
        def _(pe):
            pe.wait_ge(s_id, 2)
            for slot in range(SLOTS):
                turn, proj, norm, route = stages(slot, (0, 1, 6, 7))
                if turn is not None:
                    i = turn
                    b, t = i // NT, i % NT
                    if t == 0:
                        pe.wait_ge(given.s_at[b], 16)
                    if i >= 2:
                        pe.wait_ge(s_tcp, i - 1)
                    for c in range(DC):
                        ins = pe.transpose(psT[i % 2][:, c * P:(c + 1) * P], m.acc[:, i, c * P:(c + 1) * P], ident[:, :])
                    ins.then_inc(s_ttr, 1)
                if proj is not None:
                    i = proj
                    if i == 0:
                        pe.wait_ge(s_wo, 16)
                    pe.wait_ge(s_tcp, i + 1)
                    if i >= 2:
                        pe.wait_ge(s_y, i - 1)
                    for c in range(DC):
                        ins = pe.matmul(psP[i % 2][:, 0:D], aT[:, i % 2, c * P:(c + 1) * P], wo[:, c, :],
                                        start=(c == 0), stop=(c == DC - 1))
                    ins.then_inc(s_prj, 1)
                if norm is not None:
                    i = norm
                    pe.wait_ge(s_row, i + 1)
                    if i >= 2:
                        pe.wait_ge(s_ncp, i - 1)
                    for c in range(DC):
                        ins = pe.transpose(psN[i % 2][:, c * P:(c + 1) * P], rows[:, i, c * P:(c + 1) * P], ident[:, :])
                    ins.then_inc(s_ntr, 1)
                if route is not None:
                    i = route
                    if i == 0:
                        pe.wait_ge(s_w, 32)
                    pe.wait_ge(s_ncp, i + 1)
                    if i >= 2:
                        pe.wait_ge(s_lcp, i - 1)
                    for c in range(DC):
                        ins = pe.matmul(psL[i % 2][:, 0:E], m.rowsT[:, c, i * P:(i + 1) * P], rw[:, c, :],
                                        start=(c == 0), stop=(c == DC - 1))
                    ins.then_inc(s_log, 1)

        @block.scalar
        def _(act):
            act.wait_ge(s_id, 4)
            for slot in range(SLOTS):
                turn, dev, rms, scale, norm, route = stages(slot, (0, 2, 3, 5, 6, 7))
                if turn is not None:
                    i = turn
                    act.wait_ge(s_ttr, i + 1)
                    if i >= 2:
                        act.wait_ge(s_prj, i - 1)
                    act.activation(aT[:, i % 2, :], psT[i % 2][:, 0:D], ACT.Copy).then_inc(s_tcp, 1)
                if SPLIT_FROM <= slot < SPLIT_FROM + 4 * SWP and (slot - SPLIT_FROM) % 2 == 0:
                    q = (slot - SPLIT_FROM) // 2
                    act.wait_ge(s_sw, 64)
                    act.activation(m.sw_hi[q // SWP][:, q % SWP, :], sw[q // SWP][:, q % SWP, :], ACT.Copy).then_inc(s_swh, 1)
                if dev is not None:
                    i = dev
                    act.wait_ge(s_var, i + 1)
                    act.activation(sd[:, i % 4, 0:1], mv[:, i % 4, 1:2], ACT.Sqrt, bias=eps[:, 0:1]).then_inc(s_sd, 1)
                if rms is not None:
                    i = rms
                    act.wait_ge(s_ms, i + 1)
                    act.activation(sd[:, i % 4, 2:3], ms[:, i % 4, :], ACT.Sqrt, bias=eps[:, 1:2]).then_inc(s_rms, 1)
                if scale is not None:
                    i = scale
                    act.wait_ge(s_irms, i + 1)
                    act.wait_ge(s_xw, i + 1)
                    act.activation(rows[:, i, :], rows[:, i, :], ACT.Identity, scale=sd[:, i % 4, 3:4]).then_inc(s_row, 1)
                if norm is not None:
                    i = norm
                    act.wait_ge(s_ntr, i + 1)
                    act.activation(m.rowsT[:, :, i * P:(i + 1) * P], psN[i % 2][:, 0:D].rearrange("p (c q) -> p c q", c=DC),
                                   ACT.Copy).then_inc(s_ncp, 1)
                if route is not None:
                    i = route
                    act.wait_ge(s_log, i + 1)
                    act.activation(m.logits[:, i, :], psL[i % 2][:, 0:E], ACT.Copy).then_inc(s_lcp, 1)

        @block.vector
        def _(dve):
            done = [0]

            def link(ins):
                ins.then_inc(s_dve, 1)
                done[0] += 1
                dve.wait_ge(s_dve, done[0])

            for slot in range(SLOTS):
                proj, dev, rms = stages(slot, (1, 3, 4))
                if dev is not None:
                    i = dev
                    dve.wait_ge(s_sd, i + 1)
                    link(dve.reciprocal(sd[:, i % 4, 1:2], sd[:, i % 4, 0:1]))
                    dve.tensor_scalar(m.acc[:, i, :], y[:, i % 4, :], mv[:, i % 4, 0:1], sd[:, i % 4, 1:2],
                                      ALU.subtract, ALU.mult).then_inc(s_x1, 1)
                    dve.scalar_tensor_tensor(ms[:, i % 4, :], mv[:, i % 4, 1:2], sd[:, i % 4, 1:2], sd[:, i % 4, 1:2],
                                             ALU.mult, ALU.mult).then_inc(s_ms, 1)
                if rms is not None:
                    i = rms
                    dve.wait_ge(s_rms, i + 1)
                    dve.reciprocal(sd[:, i % 4, 3:4], sd[:, i % 4, 2:3]).then_inc(s_irms, 1)
                if proj is not None:
                    i = proj
                    b, t = i // NT, i % NT
                    if t == 0:
                        dve.wait_ge(s_xr[b % 2], 16 * (b // 2 + 1))
                    dve.wait_ge(s_prj, i + 1)
                    dve.tensor_tensor(y[:, i % 4, :], psP[i % 2][:, 0:D], xr[:, b % 2, t, :], ALU.add).then_inc(s_y, 1)
                    dve.wait_ge(s_y, i + 1)
                    link(dve.bn_stats(st[:, i % 4, :], y[:, i % 4, :]))
                    dve.bn_aggr(mv[:, i % 4, :], st[:, i % 4, :]).then_inc(s_var, 1)


class Nth:

    def __init__(self, k, it=None, base=0):
        self.k, self.it, self.base = k, it, base
        self.parity = k % 2
        self.n = k if it is None else k + it * 2

    def is_number(self, n):
        return self.it is None and self.k == n

    def next(self):
        return Nth(self.k + 1, self.it)

    def before(self):
        return Nth(self.k - 1, self.it)

    def wait(self, eng, s, per, off):
        v = per * self.k + off
        if self.it is None:
            if v > 0:
                eng.wait_ge(s, v)
        else:
            assert v + 2 * per > 0
            eng.wait_ge(s, v + self.it * (2 * per))


class Shared:

    def __init__(self, a, m, first, buffers=1):
        self.m, self.first, self.buffers = m, first, buffers
        self.DC, self.D = m.rowsT.shape[1], m.acc.shape[2]
        self.HC = m.sb1.shape[1]
        self.BL = 2 * P
        self.xh = a.sb("xh", [P, 2, self.DC, self.BL], F32R)
        self.xl = a.sb("xl", [P, 2, self.DC, self.BL], F32R)
        self.h32 = a.sb("h32", [P, 4, self.BL], F32)
        self.hh = [a.sb(f"hh{i}", [P, self.HC, self.BL], F32R) for i in range(buffers)]
        self.hl = [a.sb(f"hl{i}", [P, self.HC, self.BL], F32R) for i in range(buffers)]
        self.psU = [a.ps(f"psU{i}", [P, 512], F32) for i in range(4)]
        self.psD = [a.ps(f"psD{i}", [P, 2, self.D], F32) for i in range(2)]
        self.rows_hi_ready, self.rows_lo_ready = a.sem("rows_hi"), a.sem("rows_lo")
        self.up_done = a.sem("up")
        self.relu_done = a.sem("relu")
        self.hi_ready, self.lo_ready = a.sem("hidden_hi"), a.sem("hidden_lo")
        self.down_done = a.sem("down")
        self.added = a.sem("added")

    def hidden_of(self, n):
        i = n.parity if self.buffers == 2 else 0
        return self.hh[i], self.hl[i]

    def rows_of(self, n):
        return self.m.rowsT[:, :, bass.ds(n.n * self.BL + self.first * P, self.BL)]

    def rows_hi(self, act, n):
        n.wait(act, self.up_done, self.HC, -self.HC)
        act.activation(self.xh[:, n.parity], self.rows_of(n), ACT.Copy).then_inc(self.rows_hi_ready, 1)

    def rows_lo(self, dve, n):
        n.wait(dve, self.rows_hi_ready, 1, 1)
        dve.tensor_tensor(self.xl[:, n.parity], self.rows_of(n), self.xh[:, n.parity].bitcast(F32),
                          ALU.subtract).then_inc(self.rows_lo_ready, 1)

    def up(self, pe, n, first=0, last=None):
        hi, lo, x = self.m.sw1_hi, self.m.sw1_lo, n.parity
        n.wait(pe, self.rows_lo_ready, 1, 1)
        for h in range(first, last or self.HC):
            n.wait(pe, self.relu_done, self.HC, h - 3)
            ps, cols = self.psU[h % 4][:, 0:self.BL], slice(h * P, (h + 1) * P)
            for c in range(self.DC):
                pe.matmul(ps, hi[:, c, cols], self.xh[:, x, c, :], start=(c == 0), stop=False)
                pe.matmul(ps, hi[:, c, cols], self.xl[:, x, c, :], start=False, stop=False)
                ins = pe.matmul(ps, lo[:, c, cols], self.xh[:, x, c, :], start=False, stop=(c == self.DC - 1))
            ins.then_inc(self.up_done, 1)

    def relu(self, act, n, h, rounded=True):
        n.wait(act, self.up_done, self.HC, h + 1)
        n.wait(act, self.lo_ready, self.HC, h - 3)
        src = self.psU[h % 4][:, 0:self.BL]
        ins = act.activation(self.h32[:, h % 4, :], src, ACT.Relu, bias=self.m.sb1[:, h:h + 1])
        if rounded:
            ins = act.activation(self.hidden_of(n)[0][:, h, :], src, ACT.Relu, bias=self.m.sb1[:, h:h + 1])
        ins.then_inc(self.relu_done, 1)

    def hidden_hi(self, dve, n, h, before):
        n.wait(dve, self.relu_done, self.HC, h + 1)
        dve.tensor_copy(self.hidden_of(n)[0][:, h, :], self.h32[:, h % 4, :]).then_inc(self.hi_ready, 1)
        n.wait(dve, self.hi_ready, self.HC // 2, h // 2 + 1 - before * self.HC // 2)

    def hidden_lo(self, eng, n, h):
        n.wait(eng, self.relu_done, self.HC, h + 1)
        hh, hl = self.hidden_of(n)
        eng.tensor_tensor(hl[:, h, :], self.h32[:, h % 4, :], hh[:, h, :].bitcast(F32),
                          ALU.subtract).then_inc(self.lo_ready, 1)

    def down(self, pe, n, part=0, parts=1):
        hi, lo = self.m.sw2_hi, self.m.sw2_lo
        hh, hl = self.hidden_of(n)
        steps = 2 * self.HC // parts
        if part == 0:
            n.wait(pe, self.added, 1, -1)
        for step in range(part * steps, (part + 1) * steps):
            r, h = divmod(step, self.HC)
            if r == 0:
                n.wait(pe, self.lo_ready, self.HC, h + 1)
            ps, rows = self.psD[n.parity][:, r, :], slice(r * P, (r + 1) * P)
            pe.matmul(ps, hh[:, h, rows], hi[:, h, :], start=(h == 0), stop=False)
            pe.matmul(ps, hh[:, h, rows], lo[:, h, :], start=False, stop=False)
            ins = pe.matmul(ps, hl[:, h, rows], hi[:, h, :], start=False, stop=(h == self.HC - 1))
        if part == parts - 1:
            ins.then_inc(self.down_done, 1)

    def add(self, dve, n):
        n.wait(dve, self.down_done, 1, 1)
        acc = self.m.acc[:, bass.ds(n.n * 2 + self.first, 2), :]
        dve.tensor_tensor(acc, self.psD[n.parity][:, :, :], acc, ALU.add).then_inc(self.added, 1)


def shared_and_dispatch(nc, tri, marks, slots_x, rows, weights, m):
    TILES, E = m.logits.shape[1], m.logits.shape[2]
    NB = m.early_blocks
    RANK_AFTER = 1
    POOLED = 2
    LT = m.list_tile
    NL = m.tile_expert.shape[1]
    MOST = TILES * P // LT

    with ExitStack() as ctx:
        a = Steps(nc, ctx, "shr")
        trs = a.sb("trs", [P, P], F32)
        ones = a.sb("ones", [P, P], F32)
        mk = a.sb("mk", [P, marks.shape[1]], F32)
        prb = a.sb("prb", [P, TILES, E], F32)
        key = a.sb("key", [P, TILES, E], F32)
        oh = a.sb("oh", [P, 2, TILES, E], F32)
        both = a.sb("both", [P, TILES, E], F32)
        top = a.sb("top", [P, 2, TILES], F32)
        kt = a.sb("kt", [P, TILES], F32)
        den = a.sb("den", [P, TILES], F32)
        tot = a.sb("tot", [P, E, TILES], F32)
        cum = a.sb("cum", [P, E, TILES], F32)
        over = a.sb("over", [P, E, MOST], F32)
        nb = a.sb("nb", [P, E], F32)
        cb = a.sb("cb", [P, E], F32)
        base = a.sb("base", [P, E], F32)
        pos = a.sb("pos", [P, TILES, E], F32)
        spot = a.sb("spot", [P, 2, TILES], F32)
        past = a.sb("past", [P, NL, E], F32)
        tef = a.sb("tef", [P, NL], F32)

        shared = Shared(a, m, 0)
        psR = a.ps("psR", [P, 512], F32)
        psC = a.ps("psC", [P, 512], F32)

        s_k = a.sem("constants")
        s_sig = a.sem("probabilities")
        s_both = a.sem("experts_marked")
        s_rank = a.sem("ranks")
        s_bias = a.sem("bias_added")
        s_slot = a.sem("slots")
        s_tile = a.sem("tile_experts")
        s_sc = a.sem("rows_scattered")
        s_dve = a.sem("vector_chain")

        rev = mk[:, 0:E]
        thr = mk[:, E:E + MOST]
        idx = mk[:, E + MOST:E + MOST + NL]
        first = mk[:, E + MOST + NL:E + MOST + NL + TILES]
        assert marks.shape[1] == E + MOST + NL + TILES

        block = ctx.enter_context(nc.Block())

        @block.sync
        def _(sp):
            sp.dma_start(mk[:, :], marks).then_inc(s_k, 16)
            sp.dma_start(trs[:, :], tri).then_inc(s_k, 16)
            sp.wait_ge(s_tile, 1)
            weights.load_first(sp, m)

        def run(eng, blocks):
            for n in range(POOLED):
                blocks(Nth(n))
            with eng.Fori(1, NB // 2 - 1) as it:
                for k in range(2):
                    blocks(Nth(k, it))
            for n in range(NB - 2, NB):
                blocks(Nth(n))

        @block.tensor
        def _(pe):
            def do(n):
                shared.up(pe, n)
                if n.is_number(RANK_AFTER):
                    pe.wait_ge(s_both, 1)
                    pe.wait_ge(s_k, 32)
                    flat = both[:, :, :].rearrange("p t e -> p (t e)")
                    pe.matmul(psR[:, 0:TILES * E], trs[:, :], flat, start=True, stop=True)
                    pe.matmul(psC[:, 0:TILES * E], ones[:, :], flat, start=True, stop=True).then_inc(s_rank, 1)
                shared.down(pe, n)

            run(pe, do)

        @block.scalar
        def _(act):
            def do(n):
                for h in range(shared.HC):
                    shared.relu(act, n, h, rounded=h % 2 == 0 or n.is_number(0) or n.is_number(1))
                if not n.is_number(NB - 1):
                    shared.rows_hi(act, n.next())

            shared.rows_hi(act, Nth(0))
            act.activation(prb[:, :, :], m.logits[:, :, :], ACT.Sigmoid).then_inc(s_sig, 1)
            run(act, do)

        @block.vector
        def _(dve):
            done = [0]

            def link(ins):
                ins.then_inc(s_dve, 1)
                done[0] += 1
                dve.wait_ge(s_dve, done[0])

            def over_experts(v):
                return v.unsqueeze(2).to_broadcast([P, TILES, E])

            def over_tiles(v):
                return v.unsqueeze(1).to_broadcast([P, TILES, E])

            def pick(k):
                link(dve.reduce_max(top[:, k, :], prb[:, :, :], AX_X))
                link(dve.tensor_tensor(key[:, :, :], prb[:, :, :], over_experts(top[:, k, :]), ALU.is_equal))
                link(dve.tensor_tensor(key[:, :, :], key[:, :, :], over_tiles(rev), ALU.mult))
                link(dve.reduce_max(kt[:, :], key[:, :, :], AX_X))
                link(dve.tensor_tensor(oh[:, k, :, :], key[:, :, :], over_experts(kt[:, :]), ALU.is_equal))

            def choose():
                dve.wait_ge(s_k, 32)
                dve.wait_ge(s_sig, 1)
                link(dve.memset(ones[:, :], 1.0))
                pick(0)
                link(dve.scalar_tensor_tensor(prb[:, :, :].rearrange("p t e -> p (t e)"), oh[:, 0, :, :].rearrange("p t e -> p (t e)"),
                                              -2.0, prb[:, :, :].rearrange("p t e -> p (t e)"), ALU.mult, ALU.add))
                pick(1)
                dve.tensor_tensor(both[:, :, :], oh[:, 0, :, :], oh[:, 1, :, :], ALU.add).then_inc(s_both, 1)
                link(dve.tensor_tensor(den[:, :], top[:, 0, :], top[:, 1, :], ALU.add))
                link(dve.tensor_scalar(den[:, :], den[:, :], 1e-6, None, ALU.add))
                link(dve.reciprocal(den[:, :], den[:, :]))
                link(dve.tensor_tensor(m.gate[:, :, :], top[:, :, :], den[:, :].unsqueeze(1).to_broadcast([P, 2, TILES]), ALU.mult))

            def place():
                dve.wait_ge(s_rank, 1)
                link(dve.tensor_copy(tot[:, :, :], psC[:, 0:TILES * E].rearrange("p (t e) -> p e t", e=E)))
                for e in range(E):
                    link(dve.tensor_tensor_scan(cum[:, e, :], first, tot[:, e, :], 0.0, ALU.mult, ALU.add))
                link(dve.tensor_tensor(over[:, :, :], cum[:, :, TILES - 1:TILES].to_broadcast([P, E, MOST]),
                                       thr.unsqueeze(1).to_broadcast([P, E, MOST]), ALU.is_gt))
                link(dve.reduce_sum(nb[:, :], over[:, :, :], AX_X))
                link(dve.tensor_tensor_scan(cb[:, :], first[:, 0:E], nb[:, :], 0.0, ALU.mult, ALU.add))
                link(dve.tensor_tensor(base[:, :], cb[:, :], nb[:, :], ALU.subtract))
                link(dve.tensor_scalar(base[:, :], base[:, :], float(LT), None, ALU.mult))
                link(dve.tensor_tensor(cum[:, :, :], cum[:, :, :], tot[:, :, :], ALU.subtract))
                link(dve.tensor_tensor(pos[:, :, :], psR[:, 0:TILES * E].rearrange("p (t e) -> p t e", e=E),
                                       cum[:, :, :].rearrange("p e t -> p t e"), ALU.add))
                link(dve.tensor_tensor(pos[:, :, :], pos[:, :, :], over_tiles(base[:, :]), ALU.add))
                for k in range(2):
                    link(dve.tensor_tensor(key[:, :, :], pos[:, :, :], oh[:, k, :, :], ALU.mult))
                    link(dve.reduce_sum(spot[:, k, :], key[:, :, :], AX_X))
                dve.tensor_copy(m.slot[:, :, :], spot[:, :, :]).then_inc(s_slot, 1)
                link(dve.tensor_tensor(past[:, :, :], idx.unsqueeze(2).to_broadcast([P, NL, E]),
                                       cb[:, :].unsqueeze(1).to_broadcast([P, NL, E]), ALU.is_ge))
                link(dve.reduce_sum(tef[:, :], past[:, :, :], AX_X))
                link(dve.tensor_scalar(tef[:, :], tef[:, :], float(E - 1), None, ALU.min))
                dve.tensor_copy(m.tile_expert[:, :], tef[:, :]).then_inc(s_tile, 1)

            def add_bias(n, j):
                n.wait(dve, shared.added, 1, -1 if j == 0 else 0)
                some = m.acc[:, bass.ds(n.n * 4 + (2 * j - 8), 2), :]
                dve.tensor_tensor(some, some, m.sb2[:, :].unsqueeze(1).to_broadcast([P, 2, m.sb2.shape[1]]), ALU.add).then_inc(s_bias, 1)

            def do(n):
                for h in range(shared.HC):
                    if h % 2 == 1:
                        shared.hidden_hi(dve, n, h, POOLED)
                    shared.hidden_lo(dve, n, h)
                if not n.is_number(NB - 1):
                    shared.rows_lo(dve, n.next())
                add_bias(n, 0)
                n.wait(dve, s_bias, 2, -3)
                shared.add(dve, n.before())
                add_bias(n, 1)

            assert 2 * (NB - 2) == TILES // 2
            shared.rows_lo(dve, Nth(0))
            choose()
            shared.rows_lo(dve, Nth(1))
            shared.rows_lo(dve, Nth(2))
            shared.add(dve, Nth(0))
            place()
            with dve.Fori(1, NB // 2 - 1) as it:
                for k in range(2):
                    do(Nth(k, it))
            for n in range(NB - 2, NB):
                do(Nth(n))
            dve.wait_ge(s_bias, 2 * (NB - 2))
            shared.add(dve, Nth(NB - 1))

        @block.gpsimd
        def _(pool):
            for n in range(POOLED):
                for h in range(shared.HC):
                    shared.hidden_lo(pool, Nth(n), h)
            pool.wait_ge(s_slot, 1)
            for i in range(TILES):
                for k in range(2):
                    pool.indirect_dma_start(slots_x, bass.IndirectOffsetOnAxis(ap=m.slot[:, k, i:i + 1], axis=0),
                                            rows[:, i, :], None).then_inc(s_sc, 16)
            pool.wait_ge(s_sc, 16 * 2 * TILES)


class ExpertWeights:

    def __init__(self, nc, ctx, ew1, eb1c, ew2, eb2):
        a = Steps(nc, ctx, "ew")
        E, D, HID = ew1.shape
        self.last = E - 1
        self.w1 = [a.sb("w1_0", [P, D // P, HID], F32)]
        self.w2 = [a.sb("w2_0", [P, HID // P, D], F32)]
        self.b1 = a.sb("b1", [P, 2, HID // P], F32)
        self.b2 = a.sb("b2", [P, 2, D], F32)
        self.s_w1 = [a.sem(f"w1_loaded{i}") for i in range(2)]
        self.s_w2 = [a.sem(f"w2_loaded{i}") for i in range(2)]
        self.sources = ew1, eb1c, ew2, eb2

    def add_second(self, a):
        for w in (self.w1, self.w2):
            w.append(a.sb(f"w{len(w)}_{w[0].shape[1]}", [P, w[0].shape[1], w[0].shape[2]], F32))

    def load_w1(self, sp, k, e):
        src = self.sources[0]
        sp.dma_start(self.w1[k][:, :, :], src[bass.ds(e, 1)].rearrange("o (c p) h -> p (o c) h", p=P)).then_inc(self.s_w1[k], 16)

    def load_b1(self, sp, k, e):
        sp.dma_start(self.b1[:, k, :], self.sources[1][bass.ds(e, 1)].rearrange("o p h -> p (o h)")).then_inc(self.s_w1[k], 16)

    def load_w2(self, sp, k, e):
        src = self.sources[2]
        sp.dma_start(self.w2[k][:, :, :], src[bass.ds(e, 1)].rearrange("o (c p) d -> p (o c) d", p=P)).then_inc(self.s_w2[k], 16)

    def load_b2(self, sp, k, e):
        sp.dma_start(self.b2[:, k, :], self.sources[3][bass.ds(e, 1), :].to_broadcast([P, self.b2.shape[2]])).then_inc(self.s_w2[k], 16)

    def load_first(self, sp, m):
        e = sp.value_load(m.tile_expert[0:1, 0:1], min_val=0, max_val=self.last)
        for load in (self.load_w1, self.load_b1, self.load_w2, self.load_b2):
            load(sp, 0, e)


def experts(nc, slots_x, weights, slots_y, m):
    w1, w2, b1, b2, s_w1, s_w2 = weights.w1, weights.w2, weights.b1, weights.b2, weights.s_w1, weights.s_w2
    D, HID = slots_x.shape[1], w1[0].shape[2]
    DC, HC = D // P, HID // P
    LT = m.list_tile
    NL = m.tile_expert.shape[1]
    RT = LT // P
    WP = 4
    HP = HC // WP
    assert NL % 2 == 1 and RT * D == 512 and RT == 2

    with ExitStack() as ctx:
        a = Steps(nc, ctx, "exp")
        weights.add_second(a)
        ident = a.sb("ident", [P, P], F32)
        w1h = a.sb("w1h", [P, DC, HID], F32R)
        w1l = a.sb("w1l", [P, DC, HID], F32R)
        w2h = a.sb("w2h", [P, HC, D], F32R)
        w2l = a.sb("w2l", [P, HC, D], F32R)
        xs = a.sb("xs", [P, 2, RT, D], F32)
        xh = a.sb("xh", [P, 2, DC, LT], F32R)
        xl = a.sb("xl", [P, 2, DC, LT], F32R)
        h32 = a.sb("h32", [P, 4, LT], F32)
        hh = a.sb("hh", [P, HC, LT], F32R)
        hl = a.sb("hl", [P, HC, LT], F32R)
        ys = a.sb("ys", [P, 2, RT, D], F32)

        psT = a.ps("psT", [P, 512], F32)
        psU = [a.ps(f"psU{i}", [P, 512], F32) for i in range(4)]
        psD = [a.ps(f"psD{i}", [P, 512], F32) for i in range(RT)]

        s_id = a.sem("identity")
        s_x = [a.sem(f"rows_loaded{i}") for i in range(2)]
        s_tr = a.sem("rows_turned")
        s_xh, s_xl = a.sem("rows_hi"), a.sem("rows_lo")
        s_w1h, s_w1l = a.sem("w1_hi"), a.sem("w1_lo")
        s_w2h, s_w2l = a.sem("w2_hi"), a.sem("w2_lo")
        s_up = a.sem("up")
        s_rel = a.sem("relu")
        s_hh, s_hl = a.sem("hidden_hi"), a.sem("hidden_lo")
        s_dn = a.sem("down")
        s_y = a.sem("outputs")
        s_st = [a.sem(f"stored{i}") for i in range(2)]

        x_tile = slots_x.rearrange("(n r p) d -> n p r d", r=RT, p=P)
        y_tile = slots_y.rearrange("(n r p) d -> n p r d", r=RT, p=P)

        def w1_piece(t, q):
            return t[:, :, q * HP * P:(q + 1) * HP * P]

        def w2_piece(t, q):
            return t[:, q * HP:(q + 1) * HP, :]

        class Tile:

            def __init__(self, k, it, base=0):
                self.k, self.it, self.base = k, it, base
                self.j = k + 2 * base if it is None else k + 2 * base + it * 2
                self.first = it is None and base == 0

            def wait(self, eng, s, per_tile, off):
                v = per_tile * (self.k + 2 * self.base) + off
                if self.it is None:
                    if v > 0:
                        eng.wait_ge(s, v)
                else:
                    assert v + 2 * per_tile > 0
                    eng.wait_ge(s, v + self.it * (2 * per_tile))

            def wait_pair(self, eng, s, per_use, off):
                v = per_use * self.base + off
                if self.it is None:
                    if v > 0:
                        eng.wait_ge(s[self.k], v)
                else:
                    eng.wait_ge(s[self.k], v + self.it * per_use)

        def run(eng, tile):
            for k in range(2):
                tile(Tile(k, None))
            with eng.Fori(1, NL // 2) as it:
                for k in range(2):
                    tile(Tile(k, it))
            tile(Tile(0, None, NL // 2))

        def is_last(t):
            return t.it is None and t.base == NL // 2

        def after(t):
            if t.k == 0:
                return Tile(1, t.it, t.base)
            return Tile(0, t.it, t.base + 1)

        block = ctx.enter_context(nc.Block())

        @block.sync
        def _(sp):
            def tile(t):
                k, j = t.k, t.j
                t.wait(sp, s_tr, 1, -1)
                sp.dma_start(xs[:, k], x_tile[bass.ds(j, 1)].rearrange("o p r d -> p (o r) d")).then_inc(s_x[k], 16)
                if t.first and k == 0:
                    return
                e = sp.value_load(m.tile_expert[0:1, bass.ds(j, 1)], min_val=0, max_val=weights.last)
                t.wait(sp, s_w1l, WP, -WP)
                weights.load_w1(sp, k, e)
                t.wait(sp, s_rel, HC, -HC)
                weights.load_b1(sp, k, e)
                t.wait(sp, s_w2l, WP, -WP)
                weights.load_w2(sp, k, e)
                t.wait(sp, s_y, RT, -RT)
                weights.load_b2(sp, k, e)

            run(sp, tile)

        @block.gpsimd
        def _(pool):
            pool.memset(ident[:, :], 0.0).then_inc(s_id, 1)
            pool.wait_ge(s_id, 1)
            pool.affine_select(out=ident[:, :], in_=ident[:, :], compare_op=ALU.not_equal, fill=1.0,
                               base=0, pattern=[[-1, P]], channel_multiplier=1).then_inc(s_id, 1)

            def store(k, j):
                pool.dma_start(y_tile[bass.ds(j, 1)].rearrange("o p r d -> p (o r) d"), ys[:, k]).then_inc(s_st[k], 16)

            def tile(t):
                for q in range(WP):
                    t.wait(pool, s_w2h, WP, q + 1)
                    pool.tensor_tensor(w2_piece(w2l, q), w2_piece(w2[t.k], q), w2_piece(w2h, q).bitcast(F32),
                                       ALU.subtract).then_inc(s_w2l, 1)
                t.wait(pool, s_y, RT, RT)
                store(t.k, t.j)

            run(pool, tile)
            for k in range(2):
                pool.wait_ge(s_st[k], 16 * ((NL + 1 - k) // 2))

        @block.tensor
        def _(pe):
            pe.wait_ge(s_id, 2)

            def turn(t):
                t.wait_pair(pe, s_x, 16, 16)
                t.wait(pe, s_xl, 1, 0)
                for r in range(RT):
                    for c in range(DC):
                        ins = pe.transpose(psT[:, c * LT + r * P:c * LT + (r + 1) * P], xs[:, t.k, r, c * P:(c + 1) * P], ident[:, :])
                ins.then_inc(s_tr, 1)

            def tile(t):
                k = t.k
                t.wait(pe, s_xl, 1, 1)
                for h in range(HC):
                    if h % HP == 0:
                        t.wait(pe, s_w1l, WP, h // HP + 1)
                    t.wait(pe, s_rel, HC, h - 3)
                    ps, cols = psU[h % 4][:, 0:LT], slice(h * P, (h + 1) * P)
                    for c in range(DC):
                        pe.matmul(ps, w1h[:, c, cols], xh[:, k, c, :], start=(c == 0), stop=False)
                        pe.matmul(ps, w1h[:, c, cols], xl[:, k, c, :], start=False, stop=False)
                        ins = pe.matmul(ps, w1l[:, c, cols], xh[:, k, c, :], start=False, stop=(c == DC - 1))
                    ins.then_inc(s_up, 1)
                if not is_last(t):
                    turn(after(t))
                for r in range(RT):
                    t.wait(pe, s_y, RT, r - 1)
                    for h in range(HC):
                        if r == 0:
                            t.wait(pe, s_hl, HC, h + 1)
                            if h % HP == 0:
                                t.wait(pe, s_w2l, WP, h // HP + 1)
                        ps, rows = psD[r][:, 0:D], slice(r * P, (r + 1) * P)
                        pe.matmul(ps, hh[:, h, rows], w2h[:, h, :], start=(h == 0), stop=False)
                        pe.matmul(ps, hh[:, h, rows], w2l[:, h, :], start=False, stop=False)
                        ins = pe.matmul(ps, hl[:, h, rows], w2h[:, h, :], start=False, stop=(h == HC - 1))
                    ins.then_inc(s_dn, 1)

            turn(Tile(0, None))
            run(pe, tile)

        @block.scalar
        def _(act):
            def rows_hi(t):
                t.wait(act, s_tr, 1, 1)
                t.wait(act, s_up, HC, -HC)
                act.activation(xh[:, t.k], psT[:, :].rearrange("p (c r) -> p c r", c=DC), ACT.Copy).then_inc(s_xh, 1)

            def w1_hi(t, q):
                if q == 0:
                    t.wait_pair(act, s_w1, 32, 32)
                t.wait(act, s_up, HC, (q + 1) * HP - HC)
                act.activation(w1_piece(w1h, q), w1_piece(w1[t.k], q), ACT.Copy).then_inc(s_w1h, 1)

            def w2_hi(t, q):
                if q == 0:
                    t.wait_pair(act, s_w2, 32, 32)
                    t.wait(act, s_dn, RT, 0)
                act.activation(w2_piece(w2h, q), w2_piece(w2[t.k], q), ACT.Copy).then_inc(s_w2h, 1)

            def relu(t, h):
                t.wait(act, s_up, HC, h + 1)
                t.wait(act, s_hl, HC, h - 3)
                act.activation(h32[:, h % 4, :], psU[h % 4][:, 0:LT], ACT.Relu, bias=b1[:, t.k, h:h + 1]).then_inc(s_rel, 1)

            def tile(t):
                for h in range(HC):
                    relu(t, h)
                    if h % 2 == 0:
                        w2_hi(t, h // 2)
                if not is_last(t):
                    rows_hi(after(t))
                    for q in range(WP):
                        w1_hi(after(t), q)

            rows_hi(Tile(0, None))
            for q in range(WP):
                w1_hi(Tile(0, None), q)
            run(act, tile)

        @block.vector
        def _(dve):
            def rows_lo(t):
                t.wait(dve, s_xh, 1, 1)
                dve.tensor_tensor(xl[:, t.k], psT[:, :].rearrange("p (c r) -> p c r", c=DC), xh[:, t.k].bitcast(F32),
                                  ALU.subtract).then_inc(s_xl, 1)

            def w1_lo(t, q):
                t.wait(dve, s_w1h, WP, q + 1)
                dve.tensor_tensor(w1_piece(w1l, q), w1_piece(w1[t.k], q), w1_piece(w1h, q).bitcast(F32),
                                  ALU.subtract).then_inc(s_w1l, 1)

            def split_hidden(t, h):
                t.wait(dve, s_rel, HC, h + 1)
                dve.tensor_copy(hh[:, h, :], h32[:, h % 4, :]).then_inc(s_hh, 1)

            def split_hidden_lo(t, h):
                t.wait(dve, s_hh, HC, h + 1)
                dve.tensor_tensor(hl[:, h, :], h32[:, h % 4, :], hh[:, h, :].bitcast(F32), ALU.subtract).then_inc(s_hl, 1)

            def output(t, r):
                if r == 0:
                    t.wait_pair(dve, s_w2, 32, 32)
                    t.wait_pair(dve, s_st, 16, 0)
                t.wait(dve, s_dn, RT, r + 1)
                dve.tensor_tensor(ys[:, t.k, r, :], psD[r][:, 0:D], b2[:, t.k, :], ALU.add).then_inc(s_y, 1)

            def tile(t):
                for h in range(HC):
                    split_hidden(t, h)
                    split_hidden_lo(t, h)
                if not is_last(t):
                    rows_lo(after(t))
                    w1_lo(after(t), 0)
                    w1_lo(after(t), 1)
                output(t, 0)
                if not is_last(t):
                    w1_lo(after(t), 2)
                    w1_lo(after(t), 3)
                output(t, 1)

            rows_lo(Tile(0, None))
            for q in range(WP):
                w1_lo(Tile(0, None), q)
            run(dve, tile)


def combine(nc, slots_y, out, m):
    T, D = out.shape
    TILES = T // P
    R, RG = 8, 8
    NB = TILES // 2 - m.early_blocks

    with ExitStack() as ctx:
        a = Steps(nc, ctx, "out")
        g = a.sb("g", [P, RG, 2, D], F32)
        y = a.sb("y", [P, R, D], F32)
        o = a.sb("o", [P, R, D], F32)
        st = a.sb("st", [P, R, 6], F32)
        mv = a.sb("mv", [P, R, 2], F32)
        sd = a.sb("sd", [P, R, 3], F32)
        shared = Shared(a, m, 2 * m.early_blocks, buffers=2)
        eps = a.sb("eps", [P, 1], F32)
        s_g = [a.sem(f"gathered{i}") for i in range(RG)]
        s_eps = a.sem("eps_set")
        s_var = a.sem("variance")
        s_sd = a.sem("deviation")
        s_nm = a.sem("mean_scaled")
        s_o = a.sem("normed")
        s_y = a.sem("summed")
        s_st = [a.sem(f"stored{i}") for i in range(R)]
        s_dve = a.sem("vector_chain")
        block = ctx.enter_context(nc.Block())

        @block.gpsimd
        def _(pool):
            for i in range(TILES):
                if i >= RG:
                    pool.wait_ge(s_y, i - RG + 1)
                for k in range(2):
                    pool.indirect_dma_start(g[:, i % RG, k, :], None, slots_y,
                                            bass.IndirectOffsetOnAxis(ap=m.slot[:, k, i:i + 1], axis=0)).then_inc(s_g[i % RG], 16)

        @block.vector
        def _(dve):
            done = [0]

            def link(ins):
                ins.then_inc(s_dve, 1)
                done[0] += 1
                dve.wait_ge(s_dve, done[0])

            dve.memset(eps[:, :], 1e-5).then_inc(s_eps, 1)
            shared.rows_lo(dve, Nth(0))
            for slot in range(TILES + 2):
                if slot < TILES:
                    i, r = slot, slot % R
                    dve.wait_ge(s_g[i % RG], 32 * (i // RG + 1))
                    if i >= R:
                        dve.wait_ge(s_o, i - R + 1)
                    if i >= shared.first:
                        Nth((i - shared.first) // 2).wait(dve, shared.added, 1, 1)
                    link(dve.scalar_tensor_tensor(y[:, r, :], g[:, i % RG, 0, :], m.gate[:, 0, i:i + 1], m.acc[:, i, :], ALU.mult, ALU.add))
                    dve.scalar_tensor_tensor(y[:, r, :], g[:, i % RG, 1, :], m.gate[:, 1, i:i + 1], y[:, r, :], ALU.mult, ALU.add).then_inc(s_y, 1)
                    dve.wait_ge(s_y, i + 1)
                    link(dve.bn_stats(st[:, r, :], y[:, r, :]))
                    dve.bn_aggr(mv[:, r, :], st[:, r, :]).then_inc(s_var, 1)
                if slot >= 2:
                    j = slot - 2
                    r = j % R
                    dve.wait_ge(s_sd, j + 1)
                    link(dve.reciprocal(sd[:, r, 1:2], sd[:, r, 0:1]))
                    dve.scalar_tensor_tensor(sd[:, r, 2:3], mv[:, r, 0:1], -1.0, sd[:, r, 1:2], ALU.mult, ALU.mult).then_inc(s_nm, 1)
                n, h = divmod(2 * (slot - 1), shared.HC)
                if 0 <= n < NB:
                    shared.hidden_lo(dve, Nth(n), h)
                    shared.hidden_lo(dve, Nth(n), h + 1)
                if h == 2 and 0 <= n and n + 1 < NB:
                    shared.rows_lo(dve, Nth(n + 1))
                if h == 0 and 2 <= n <= NB + 1:
                    shared.add(dve, Nth(n - 2))

        @block.tensor
        def _(pe):
            for n in range(NB + 1):
                for part in range(4):
                    if n < NB:
                        shared.up(pe, Nth(n), 2 * part, 2 * part + 2)
                    if n >= 1:
                        shared.down(pe, Nth(n - 1), part, 4)

        @block.scalar
        def _(act):
            shared.rows_hi(act, Nth(0))
            act.wait_ge(s_eps, 1)
            for slot in range(TILES + 3):
                n, h = divmod(2 * slot, shared.HC)
                if n < NB:
                    shared.relu(act, Nth(n), h)
                    shared.relu(act, Nth(n), h + 1)
                if h == 2 and n + 1 < NB:
                    shared.rows_hi(act, Nth(n + 1))
                if 1 <= slot <= TILES:
                    i = slot - 1
                    act.wait_ge(s_var, i + 1)
                    act.activation(sd[:, i % R, 0:1], mv[:, i % R, 1:2], ACT.Sqrt, bias=eps[:, 0:1]).then_inc(s_sd, 1)
                if slot >= 3:
                    j = slot - 3
                    r = j % R
                    act.wait_ge(s_nm, j + 1)
                    if j >= R:
                        act.wait_ge(s_st[r], 16 * (j // R))
                    act.activation(o[:, r, :], y[:, r, :], ACT.Identity, bias=sd[:, r, 2:3], scale=sd[:, r, 1:2]).then_inc(s_o, 1)

        @block.sync
        def _(sp):
            for i in range(TILES):
                sp.wait_ge(s_o, i + 1)
                sp.dma_start(out[i * P:(i + 1) * P, :], o[:, i % R, :]).then_inc(s_st[i % R], 16)
            for r in range(R):
                sp.wait_ge(s_st[r], 16 * (TILES // R))


class Carried:

    def __init__(self, nc, ctx, acc, T, D, E, HID, list_tile):
        a = Steps(nc, ctx, "all")
        n = T // P
        self.list_tile = list_tile
        lists = (2 * T + E * (list_tile - 1)) // list_tile
        self.early_blocks = EARLY_BLOCKS
        self.acc = acc
        self.rowsT = a.sb("rowsT", [P, D // P, T], F32)
        self.sw_hi = [a.sb(f"sw{i + 1}_hi", [P, D // P * HID // 512, 512], F32R) for i in range(2)]
        self.sw_lo = [a.sb(f"sw{i + 1}_lo", [P, D // P * HID // 512, 512], F32R) for i in range(2)]
        for i, cols in enumerate((HID, D)):
            for part, t in (("hi", self.sw_hi[i]), ("lo", self.sw_lo[i])):
                v = t[:, :, :].rearrange("p a b -> p (a b)").rearrange("p (c n) -> p c n", n=cols)
                if i == 0 and part == "hi":
                    self.sw1_hi = v
                elif i == 0:
                    self.sw1_lo = v
                elif part == "hi":
                    self.sw2_hi = v
                else:
                    self.sw2_lo = v
        self.sb1 = a.sb("sb1", [P, HID // P], F32)
        self.sb2 = a.sb("sb2", [P, D], F32)
        self.logits = a.sb("logits", [P, n, E], F32)
        self.gate = a.sb("gate", [P, 2, n], F32)
        self.slot = a.sb("slot", [P, 2, n], U32)
        self.tile_expert = a.sb("tile_expert", [P, lists], I32)


def layer(nc, x, xT, Wqkv, rope_cos, rope_sin, Wo, norm_w, router_wT, sw1, sb1c, sw2, sb2,
          ew1, eb1c, ew2, eb2, tri, marks, out):
    T, D = x.shape
    E = ew1.shape[0]
    LT = 256
    slots = (2 * T + E * (LT - 1)) // LT * LT
    attn = nc.dram_tensor("attn_rows", (T, D), F32, kind="Internal").ap()
    slots_x = nc.dram_tensor("slots_x", (slots, D), F32, kind="Internal").ap()
    slots_y = nc.dram_tensor("slots_y", (slots, D), F32, kind="Internal").ap()
    with ExitStack() as ctx:
        given = NormInputs(nc, ctx, T, P * rope_cos.shape[1], D)
        attention(nc, xT, Wqkv, rope_cos, rope_sin, attn, slots_x, given)
        m = Carried(nc, ctx, given.acc, T, D, E, sw1.shape[1], LT)
        weights = ExpertWeights(nc, ctx, ew1, eb1c, ew2, eb2)
        with nc.sbuf_tensor("all_rows", [P, T // P, D], F32) as rows:
            norm_and_route(nc, x, attn, Wo, norm_w, router_wT, sw1, sb1c, sw2, sb2, rows, given, m)
            shared_and_dispatch(nc, tri, marks, slots_x, rows, weights, m)
        experts(nc, slots_x, weights, slots_y, m)
        combine(nc, slots_y, out, m)


def kernel(L0_attn_x, L0_attn_Wqkv, L0_attn_Wo, L0_ffn_norm_weight, L0_ffn_router_w, L0_ffn_sw1, L0_ffn_sb1,
           L0_ffn_sw2, L0_ffn_sb2, L0_ffn_ew1, L0_ffn_eb1, L0_ffn_ew2, L0_ffn_eb2):
    import concourse.bacc as bacc
    from concourse.bass_utils import run_bass_kernel_spmd

    x = np.asarray(L0_attn_x)
    B, L, D = x.shape
    T = B * L
    x2 = np.ascontiguousarray(x.reshape(T, D))
    E, _, HID = L0_ffn_ew1.shape
    DH, LT = 16, 256
    inv = (1.0 / np.float32(10000.0) ** (np.arange(0, DH, 2, dtype=np.float32) / np.float32(DH))).astype(np.float32)
    angles = np.outer(np.arange(L, dtype=np.float32), inv).astype(np.float32)
    angles = np.concatenate([angles, angles], -1)
    signs = np.where(np.arange(DH) < DH // 2, -1.0, 1.0).astype(np.float32)

    def by_tile(t):
        return np.ascontiguousarray(t.astype(np.float32).reshape(L // P, P, DH).transpose(1, 0, 2))

    tri = np.triu(np.ones((P, P), np.float32), 1)
    lists = (2 * T + E * (LT - 1)) // LT
    marks = np.concatenate([
        np.arange(E, 0, -1), LT * np.arange(T // LT), np.arange(lists), np.arange(T // P) > 0,
    ]).astype(np.float32)
    marks = np.ascontiguousarray(np.broadcast_to(marks, (P, marks.size)))
    arrays = {
        "x": x2,
        "xT": np.ascontiguousarray(x2.T),
        "Wqkv": np.asarray(L0_attn_Wqkv),
        "rope_cos": by_tile(np.cos(angles)),
        "rope_sin": by_tile(np.sin(angles) * signs),
        "Wo": np.asarray(L0_attn_Wo),
        "norm_w": np.asarray(L0_ffn_norm_weight),
        "router_wT": np.ascontiguousarray(np.asarray(L0_ffn_router_w).T),
        "sw1": np.asarray(L0_ffn_sw1),
        "sb1c": np.ascontiguousarray(np.asarray(L0_ffn_sb1).reshape(HID // P, P).T),
        "sw2": np.asarray(L0_ffn_sw2),
        "sb2": np.asarray(L0_ffn_sb2),
        "ew1": np.asarray(L0_ffn_ew1),
        "eb1c": np.ascontiguousarray(np.asarray(L0_ffn_eb1).reshape(E, HID // P, P).transpose(0, 2, 1)),
        "ew2": np.asarray(L0_ffn_ew2),
        "eb2": np.asarray(L0_ffn_eb2),
        "tri": tri,
        "marks": marks,
    }
    nc = bacc.Bacc("TRN2", target_bir_lowering=False, num_devices=1)
    args = [nc.dram_tensor(n, v.shape, mybir.dt.from_np(v.dtype), kind="ExternalInput").ap() for n, v in arrays.items()]
    out = nc.dram_tensor("out", (T, D), F32, kind="ExternalOutput").ap()
    layer(nc, *args, out)
    r = run_bass_kernel_spmd(nc, [arrays], core_ids=[0])
    return r.results[0]["out"].reshape(B, L, D)
```
